# Optimizing a Trainium2 kernel written in Bass

```python
import numpy as np
import jax
import jax.numpy as jnp

def _softmax(x, axis=-1):
    return jax.nn.softmax(x, axis=axis)

def _gelu(x):
    return jax.nn.gelu(x, approximate=True)

def _silu(x):
    return jax.nn.silu(x)

def _sigmoid(x):
    return jax.nn.sigmoid(x)

def _layernorm(x, axis=-1, eps=1e-05):
    m = jnp.mean(x, axis=axis, keepdims=True)
    v = jnp.var(x, axis=axis, keepdims=True)
    return (x - m) / jnp.sqrt(v + eps)

def _scatter_add(tgt, idx, src, axis=0):
    return tgt.at[idx].add(src)

def _segment_sum(src, seg, n):
    return jax.ops.segment_sum(src, seg, n)
kernel_name = 'mk_gps_d1_gnn_r8_12df7e'

def setup_inputs(seed: int=0):
    np.random.seed(seed)
    _w = jnp.asarray

    def _rec_inputs():
        import jax
        import jax.numpy as jnp
        _gk = jax.random.key(seed)
        x = -0.0003713 + 1 * jax.random.normal(jax.random.fold_in(_gk, 1), (12500, 256), jnp.float32)
        src = jax.random.randint(jax.random.fold_in(_gk, 2), (200000,), 0, 12500, jnp.int32)
        dst = jax.random.randint(jax.random.fold_in(_gk, 3), (200000,), 0, 12500, jnp.int32)
        _o = jnp.argsort(dst, stable=True)
        src = src[_o]
        dst = dst[_o]
        return (x, src, dst)
    x, src, dst = _rec_inputs()

    def _L0_gnn_setup():
        import jax, jax.numpy as jnp
        import numpy as np
        N = 6250
        E = 100000
        H = 256
        HEADS = 4
        OUT = H // HEADS
        NEG_SLOPE = 0.2
        EPS = 1e-05
        key = jax.random.key(seed)
        ks = jax.random.split(key, 6)
        s = 1.0 / np.sqrt(H)
        x = jax.random.normal(ks[0], (N, H), dtype=jnp.float32)
        edge_index = jax.random.randint(ks[1], (2, E), 0, N, dtype=jnp.int32)
        W = jax.random.normal(ks[2], (H, HEADS * OUT), dtype=jnp.float32) * s
        att_src = jax.random.normal(ks[3], (HEADS, OUT), dtype=jnp.float32) * s
        att_dst = jax.random.normal(ks[4], (HEADS, OUT), dtype=jnp.float32) * s
        bias = jnp.zeros((H,), dtype=jnp.float32)
        gamma = jnp.ones((H,), dtype=jnp.float32)
        beta = jnp.zeros((H,), dtype=jnp.float32)
        return {'x': x, 'edge_index': edge_index, 'W': W, 'att_src': att_src, 'att_dst': att_dst, 'bias': bias, 'gamma': gamma, 'beta': beta}
    _L0_gnn_all = _L0_gnn_setup()
    _L0_gnn_in = {k: v for k, v in _L0_gnn_all.items() if k in ('W', 'att_src', 'att_dst', 'bias', 'gamma', 'beta')}
    del _L0_gnn_all

    def _L0_mix_setup():
        import jax, jax.numpy as jnp
        import numpy as np
        B, N, C, H = (8, 2048, 256, 8)
        D = C // H
        GH = C // 4
        key = jax.random.key(seed)
        ks = jax.random.split(key, 6)
        s = 0.02
        return {'x': jax.random.normal(ks[0], (B, N, C), dtype=jnp.float32), 'Wqkv': jax.random.normal(ks[1], (C, 3 * C), dtype=jnp.float32) * s, 'Wproj': jax.random.normal(ks[2], (C, C), dtype=jnp.float32) * s, 'bproj': jnp.zeros((C,), dtype=jnp.float32), 'ln_g': jnp.ones((C,), dtype=jnp.float32), 'ln_b': jnp.zeros((C,), dtype=jnp.float32), 'Wg1': jax.random.normal(ks[3], (C, GH), dtype=jnp.float32) * s, 'bg1': jnp.zeros((GH,), dtype=jnp.float32), 'Wg2': jax.random.normal(ks[4], (GH, C), dtype=jnp.float32) * s, 'bg2': jnp.zeros((C,), dtype=jnp.float32)}
    _L0_mix_all = _L0_mix_setup()
    _L0_mix_in = {k: v for k, v in _L0_mix_all.items() if k in ('Wqkv', 'Wproj', 'bproj', 'ln_g', 'ln_b', 'Wg1', 'bg1', 'Wg2', 'bg2')}
    del _L0_mix_all

    def _L0_ffn_setup():
        import math
        import jax, jax.numpy as jnp
        import numpy as np
        CAPACITY_FACTOR = 1.25
        key = jax.random.key(seed)
        ks = jax.random.split(key, 5)
        B, L, D, F, E = (8, 1024, 256, 1024, 8)
        h = jax.random.normal(ks[0], (B, L, D), dtype=jnp.float32)
        gate_w = jax.random.normal(ks[1], (D, E), dtype=jnp.float32) * 0.02
        gate_b = jnp.zeros((E,), dtype=jnp.float32)
        w1 = jax.random.normal(ks[2], (E, D, F), dtype=jnp.float32) * (1.0 / math.sqrt(D))
        b1 = jnp.zeros((E, F), dtype=jnp.float32)
        w2 = jax.random.normal(ks[3], (E, F, D), dtype=jnp.float32) * (1.0 / math.sqrt(F))
        b2 = jnp.zeros((E, D), dtype=jnp.float32)
        return {'h': h, 'gate_w': gate_w, 'gate_b': gate_b, 'w1': w1, 'b1': b1, 'w2': w2, 'b2': b2}
    _L0_ffn_all = _L0_ffn_setup()
    _L0_ffn_in = {k: v for k, v in _L0_ffn_all.items() if k in ('gate_w', 'gate_b', 'w1', 'b1', 'w2', 'b2')}
    del _L0_ffn_all
    return {'x': x, 'src': src, 'dst': dst, 'L0_gnn_W': _L0_gnn_in['W'], 'L0_gnn_att_src': _L0_gnn_in['att_src'], 'L0_gnn_att_dst': _L0_gnn_in['att_dst'], 'L0_gnn_bias': _L0_gnn_in['bias'], 'L0_gnn_gamma': _L0_gnn_in['gamma'], 'L0_gnn_beta': _L0_gnn_in['beta'], 'L0_mix_Wqkv': _L0_mix_in['Wqkv'], 'L0_mix_Wproj': _L0_mix_in['Wproj'], 'L0_mix_bproj': _L0_mix_in['bproj'], 'L0_mix_ln_g': _L0_mix_in['ln_g'], 'L0_mix_ln_b': _L0_mix_in['ln_b'], 'L0_mix_Wg1': _L0_mix_in['Wg1'], 'L0_mix_bg1': _L0_mix_in['bg1'], 'L0_mix_Wg2': _L0_mix_in['Wg2'], 'L0_mix_bg2': _L0_mix_in['bg2'], 'L0_ffn_gate_w': _L0_ffn_in['gate_w'], 'L0_ffn_gate_b': _L0_ffn_in['gate_b'], 'L0_ffn_w1': _L0_ffn_in['w1'], 'L0_ffn_b1': _L0_ffn_in['b1'], 'L0_ffn_w2': _L0_ffn_in['w2'], 'L0_ffn_b2': _L0_ffn_in['b2']}

def reference(x, src, dst, L0_gnn_W, L0_gnn_att_src, L0_gnn_att_dst, L0_gnn_bias, L0_gnn_gamma, L0_gnn_beta, L0_mix_Wqkv, L0_mix_Wproj, L0_mix_bproj, L0_mix_ln_g, L0_mix_ln_b, L0_mix_Wg1, L0_mix_bg1, L0_mix_Wg2, L0_mix_bg2, L0_ffn_gate_w, L0_ffn_gate_b, L0_ffn_w1, L0_ffn_b1, L0_ffn_w2, L0_ffn_b2):
    import jax
    import jax.numpy as jnp

    def _L0_gnn_ref(x, edge_index, W, att_src, att_dst, bias, gamma, beta):
        import jax, jax.numpy as jnp
        import numpy as np
        N = 6250
        E = 100000
        H = 256
        HEADS = 4
        OUT = H // HEADS
        NEG_SLOPE = 0.2
        EPS = 1e-05
        n = x.shape[0]
        loop = jnp.arange(n, dtype=edge_index.dtype)
        src = jnp.concatenate([edge_index[0], loop])
        dst = jnp.concatenate([edge_index[1], loop])
        h = (x @ W).reshape(n, HEADS, OUT)
        a_s = jnp.einsum('nhd,hd->nh', h, att_src)
        a_d = jnp.einsum('nhd,hd->nh', h, att_dst)
        alpha = jax.nn.leaky_relu(a_s[src] + a_d[dst], NEG_SLOPE)
        amax = jax.ops.segment_max(alpha, dst, num_segments=n)
        ex = jnp.exp(alpha - amax[dst])
        denom = jax.ops.segment_sum(ex, dst, num_segments=n)
        coef = ex / denom[dst]
        msg = coef[:, :, None] * h[src]
        agg = jax.ops.segment_sum(msg, dst, num_segments=n)
        out = agg.reshape(n, H) + bias
        out = jax.nn.relu(out)
        y = out + x
        mu = jnp.mean(y, axis=-1, keepdims=True)
        var = jnp.var(y, axis=-1, keepdims=True)
        return (y - mu) * jax.lax.rsqrt(var + EPS) * gamma + beta

    def _L0_mix_ref(x, Wqkv, Wproj, bproj, ln_g, ln_b, Wg1, bg1, Wg2, bg2):
        import jax, jax.numpy as jnp
        import numpy as np
        B, N, C, H = (8, 2048, 256, 8)
        D = C // H
        GH = C // 4
        b, n, c = x.shape
        h, d = (H, D)
        qkv = (x @ Wqkv).reshape(b, n, 3, h, d)
        q, k, v = (qkv[:, :, 0], qkv[:, :, 1], qkv[:, :, 2])
        k = jax.nn.softmax(k, axis=1)
        context = jnp.einsum('bnhd,bnhv->bhdv', k, v)
        out = jnp.einsum('bnhd,bhdv->bnhv', q, context).reshape(b, n, c)
        mu = jnp.mean(x, axis=-1, keepdims=True)
        var = jnp.var(x, axis=-1, keepdims=True)
        xn = (x - mu) * jax.lax.rsqrt(var + 1e-05) * ln_g + ln_b
        hgate = jax.nn.gelu(xn @ Wg1 + bg1, approximate=False)
        gate = jax.nn.sigmoid(hgate @ Wg2 + bg2)
        return out * gate @ Wproj + bproj

    def _L0_ffn_ref(h, gate_w, gate_b, w1, b1, w2, b2):
        import math
        import jax, jax.numpy as jnp
        import numpy as np
        CAPACITY_FACTOR = 1.25
        B, L, D = h.shape
        E = gate_w.shape[1]
        T = B * L
        C = max(1, math.ceil(CAPACITY_FACTOR * T / E))
        x = h.reshape(T, D)
        logits = x @ gate_w + gate_b
        probs = jax.nn.softmax(logits, axis=-1)
        idx = jnp.argmax(probs, axis=-1)
        prb = jnp.take_along_axis(probs, idx[:, None], axis=1)[:, 0]
        one_hot = jax.nn.one_hot(idx, E, dtype=jnp.float32)
        pos = (jnp.cumsum(one_hot, axis=0) * one_hot).sum(-1).astype(jnp.int32) - 1
        kept = pos < C
        pos_safe = jnp.where(kept, pos, C)
        buf = jnp.zeros((E, C, D), dtype=h.dtype).at[idx, pos_safe].set(x, mode='drop')
        hmid = jax.nn.relu(jnp.einsum('ecd,edf->ecf', buf, w1) + b1[:, None, :])
        ybuf = jnp.einsum('ecf,efd->ecd', hmid, w2) + b2[:, None, :]
        pos_g = jnp.minimum(pos, C - 1)
        y_tok = ybuf[idx, pos_g] * (prb * kept)[:, None]
        y = y_tok.reshape(B, L, D)
        y = jnp.nan_to_num(y, nan=0.0, posinf=10000.0, neginf=-10000.0)
        return y
    edge_index = jnp.stack([src, dst])
    xn = _layernorm(x, axis=-1)
    x = x + _L0_gnn_ref(xn, edge_index, L0_gnn_W, L0_gnn_att_src, L0_gnn_att_dst, L0_gnn_bias, L0_gnn_gamma, L0_gnn_beta) + _L0_mix_ref(xn[None], L0_mix_Wqkv, L0_mix_Wproj, L0_mix_bproj, L0_mix_ln_g, L0_mix_ln_b, L0_mix_Wg1, L0_mix_bg1, L0_mix_Wg2, L0_mix_bg2)[0]
    x = x + _L0_ffn_ref(_layernorm(x, axis=-1)[None], L0_ffn_gate_w, L0_ffn_gate_b, L0_ffn_w1, L0_ffn_b1, L0_ffn_w2, L0_ffn_b2)[0]
    return x

_drawn_inputs = setup_inputs


def setup_inputs(seed=0):
    import zlib

    import numpy as np

    out = dict(_drawn_inputs(seed))
    spreads = {'L0_gnn_bias': (0.0, 0.8),
     'L0_gnn_gamma': (1.0, 0.6),
     'L0_gnn_beta': (0.0, 0.8),
     'L0_mix_bproj': (0.0, 0.8),
     'L0_mix_ln_g': (1.0, 0.6),
     'L0_mix_ln_b': (0.0, 0.8),
     'L0_mix_bg1': (0.0, 0.8),
     'L0_mix_bg2': (0.0, 0.8),
     'L0_ffn_gate_b': (0.0, 0.604),
     'L0_ffn_b1': (0.0, 2.0),
     'L0_ffn_b2': (0.0, 2.0)}
    factors = {'L0_gnn_att_dst': 36.72,
     'L0_mix_Wqkv': 8.0,
     'L0_mix_Wproj': 8.0,
     'L0_mix_Wg1': 8.0,
     'L0_mix_Wg2': 8.0,
     'L0_gnn_W': 4.474,
     'L0_gnn_att_src': 8.0,
     'L0_ffn_gate_w': 3.366,
     'L0_ffn_w1': 6.146,
     'L0_ffn_w2': 4.201}
    for name, (base, spread) in spreads.items():
        noise = np.random.default_rng([zlib.crc32(name.encode()), seed]).standard_normal(out[name].shape)
        drawn = base * np.exp(spread * noise) if base else spread * noise
        out[name] = jnp.asarray(drawn.astype(out[name].dtype))
    for name, factor in factors.items():
        out[name] = (out[name] * factor).astype(out[name].dtype)
    return out
```

```python
from contextlib import ExitStack

import numpy as np

import concourse.bass as bass
from concourse import mybir

F32 = mybir.dt.float32
BF16 = mybir.dt.bfloat16
I32 = mybir.dt.int32
ALU = mybir.AluOpType
ACT = mybir.ActivationFunctionType
X = mybir.AxisListType.X

N, H, E = 12500, 256, 200000
HEADS, OUT = 4, 64
NEG_SLOPE, EPS = 0.2, 1e-5

P = 125
TILES = N // P
GT = 4
GROUPS = TILES // GT
GN = GT * P
UNROLL = 5
TURNS = GROUPS // UNROLL
HC = H // 128
HW = H + 2 * HEADS
ROW = H + HEADS


def rows_split(eng, out, in_, sem):
    eng.dma_start(out[0:112], in_[0:112]).then_inc(sem, 16)
    eng.dma_start(out[112:P], in_[112:P]).then_inc(sem, 16)


EG = 512
EDGE_GROUPS = -(-E // EG)
EP = EDGE_GROUPS * EG
EC = EP // 128
NO_NODE = 16383
FAN = 64
DST_ROWS = -(-EP // (FAN * FAN)) * FAN
PIVOTS = DST_ROWS // FAN
CHUNK = TILES // TURNS
STEPS = EDGE_GROUPS + TILES - 1
NEVER = -1e30

EXPERTS, F = 8, 1024
C_MAX = -(-5 * N // (4 * EXPERTS))
CAP = -(-C_MAX // 512) * 512
SLOTS = EXPERTS * CAP
CHUNKS = CAP // 512
TOKW = H + 1
FLT_MAX = float(np.finfo(np.float32).max)


def pool_gate(nc, K):
    nc.gpsimd.sem_inc(K.gate, 1)


class Chain:

    def __init__(self, eng, sem, per=0, turn=0):
        self.eng, self.sem, self.per, self.turn, self.n = eng, sem, per, turn, 0

    def did(self, ins):
        ins.then_inc(self.sem, 1)
        self.n += 1
        return self.n

    def value(self, n):
        return self.turn * self.per + n if self.per else n

    def settle(self, n=None):
        self.eng.wait_ge(self.sem, self.value(self.n if n is None else n))

    def close(self):
        assert self.n == self.per, (self.n, self.per)


class Scope:

    def __init__(self, nc, stage):
        self.nc, self.stage, self.ctx, self.held = nc, stage, ExitStack(), []

    def __enter__(self):
        return self

    def __exit__(self, *a):
        self.ctx.__exit__(*a)
        if self.held and a[0] is None:
            self.nc.clear_and_free_semaphores(self.held)
            self.nc.all_engine_barrier()

    def sb(self, name, shape, dt=F32):
        return self.ctx.enter_context(self.nc.sbuf_tensor(name, shape, dt))

    def ps(self, name, shape, dt=F32):
        return self.ctx.enter_context(self.nc.psum_tensor(name, shape, dt))

    def sem(self, name):
        self.held.append(self.nc.alloc_semaphore(f"{self.stage}_{name}"))
        return self.held[-1]

    def sems(self, name, n):
        return [self.sem(f"{name}{i}") for i in range(n)]

    def block(self):
        return self.ctx.enter_context(self.nc.Block())


def constants(nc, K):
    with Scope(nc, "constants") as s:
        made = s.sem("made")
        block = s.block()

        @block.gpsimd
        def _(pool):
            c = Chain(pool, made)
            c.did(nc.gpsimd.memset(K.ident[:], 0.0))
            c.settle()
            c.did(nc.gpsimd.affine_select(out=K.ident[:], in_=K.ident[:], compare_op=ALU.not_equal, fill=1.0,
                                          base=0, pattern=[[-1, 128]], channel_multiplier=1))
            c.did(nc.gpsimd.iota(K.iota_col[:], pattern=[[1, 512]], base=0, channel_multiplier=0,
                                 allow_small_or_imprecise_dtypes=True))
            c.did(nc.gpsimd.iota(K.node_id[:], pattern=[[P, TILES]], base=0, channel_multiplier=1,
                                 allow_small_or_imprecise_dtypes=True))
            c.settle()



def norm_stats(nc, c, x, stats, mv, var):
    for t in range(GT):
        c.did(nc.vector.bn_stats(stats[:, t, :], x[:, t, :]))
    c.settle()
    nc.vector.tensor_copy(mv[:, 0, 2:3], stats[:, 0, 1:2])
    for t in range(GT):
        c.did(nc.vector.bn_aggr(mv[:, t, 0:2], stats[:, t, :]))
    c.settle()
    return nc.vector.tensor_scalar(var[:, :], mv[:, :, 1], EPS, None, ALU.add)


def norm_rows(nc, c, x, out, mv, std, rstd):
    c.did(nc.vector.reciprocal(rstd[:, :], std[:, :]))
    c.settle()
    return [nc.vector.tensor_scalar(out[:, t, :], x[:, t, :], mv[:, t, 0:1], rstd[:, t:t + 1],
                                    ALU.subtract, ALU.mult) for t in range(GT)]


def turns(eng, n, body):
    body(0, True)
    if n > 1:
        with eng.Fori(1, n) as it:
            body(it, False)


def one(ap, i):
    if isinstance(i, int):
        return ap[i]
    v = ap[bass.ds(i, 1)]
    names = " ".join(f"d{k}" for k in range(len(v.shape)))
    rest = names.split(" ")[1:]
    return v.rearrange(f"{names} -> ({'d0 ' + rest[0]}) {' '.join(rest[1:])}")


class EdgeSearch:

    def __init__(self, nc, K, s):
        self.nc, self.K = nc, K
        self.piv = s.sb("piv", [P, PIVOTS], I32)
        self.pivf = s.sb("pivf", [P, PIVOTS])
        self.fill = s.sb("fill", [1, DST_ROWS * FAN - E], I32)
        self.zero = s.sb("zero", [1, EP - E], I32)
        self.nid1 = s.sb("nid1", [P, TILES])
        self.less = s.sb("less", [P, CHUNK, FAN])
        self.cnt = s.sb("cnt", [P, CHUNK])
        self.low = s.sb("low", [P, CHUNK])
        self.row = s.sb("row", [P, CHUNK])
        self.idx = s.sb("idx", [P, 2, CHUNK], I32)
        self.got = s.sb("got", [P, 2, CHUNK, FAN], I32)
        self.pad_ready = s.sem("pad_ready")
        self.dst_padded = s.sem("dst_padded")
        self.piv_in = s.sem("piv_in")
        self.table_in = s.sem("table_in")
        self.idx_ready = s.sem("idx_ready")
        self.rows_in = s.sems("rows_in", 2)
        self.counted = s.sem("counted")

    def load(self, sp, A):
        K = self.K
        sp.wait_ge(self.pad_ready, 2)
        sp.dma_start(K.dst_d[0:E], A.dst).then_inc(self.dst_padded, 16)
        sp.dma_start(K.src_d[0:E], A.src).then_inc(self.dst_padded, 16)
        sp.dma_start(K.dst_d[E:DST_ROWS * FAN], self.fill[0, :]).then_inc(self.dst_padded, 16)
        sp.dma_start(K.src_d[E:EP], self.zero[0, :]).then_inc(self.dst_padded, 16)
        sp.wait_ge(self.dst_padded, 64)
        firsts = K.dst_d.rearrange("(a b c) -> a b c", b=FAN, c=FAN)
        with self.nc.allow_non_contiguous_dma(reason="first entries of rows, once"):
            sp.dma_start(self.piv[:, :], firsts[:, 0, 0].rearrange("(a r) -> a r", a=1).to_broadcast([P, PIVOTS])).then_inc(self.piv_in, 16)
            sp.dma_start(K.top_d, firsts[:, :, 0]).then_inc(self.table_in, 16)

    def prepare(self, dve):
        nc = self.nc
        nc.vector.memset(self.fill[:], NO_NODE).then_inc(self.pad_ready, 1)
        nc.vector.memset(self.zero[:], 0).then_inc(self.pad_ready, 1)
        nc.vector.tensor_scalar(self.nid1[:], self.K.node_id[:], 1.0, None, ALU.add).then_inc(self.counted, 1)

    def pivots(self, dve):
        nc = self.nc
        dve.wait_ge(self.piv_in, 16)
        nc.vector.tensor_copy(self.pivf[:], self.piv[:]).then_inc(self.counted, 1)
        dve.wait_ge(self.counted, 2)

    def count(self, dve, level, it):
        nc, base = self.nc, 2 + it * 10 + (0, 3, 7)[level]
        nodes = self.nid1[:, bass.ds(it * CHUNK, CHUNK)]
        if level == 0:
            n, entries = PIVOTS, self.pivf[:, :].rearrange("p (a f) -> p a f", a=1).to_broadcast([P, CHUNK, PIVOTS])
        else:
            n, entries = FAN, self.got[:, level - 1]
            dve.wait_ge(self.rows_in[level - 1], it * 16 * CHUNK + 16 * CHUNK)
        less = self.less[:, :, 0:n]
        nc.vector.tensor_tensor(less, entries, nodes.rearrange("p (t f) -> p t f", f=1).to_broadcast([P, CHUNK, n]),
                                ALU.is_lt).then_inc(self.counted, 1)
        dve.wait_ge(self.counted, base + 1)
        nc.vector.tensor_reduce(self.cnt[:, :], less, X, ALU.add).then_inc(self.counted, 1)
        dve.wait_ge(self.counted, base + 2)
        if level == 2:
            nc.vector.scalar_tensor_tensor(self.K.rend[:, bass.ds(it * CHUNK, CHUNK)], self.row[:, :], float(FAN),
                                           self.cnt[:, :], ALU.mult, ALU.add).then_inc(self.counted, 1)
            return
        nc.vector.tensor_scalar(self.low[:, :] if level else self.row[:, :], self.cnt[:, :], 1.0, 0.0,
                                ALU.subtract, ALU.max).then_inc(self.counted, 1)
        dve.wait_ge(self.counted, base + 3)
        if level:
            nc.vector.scalar_tensor_tensor(self.row[:, :], self.row[:, :], float(FAN), self.low[:, :],
                                           ALU.mult, ALU.add).then_inc(self.counted, 1)
            dve.wait_ge(self.counted, base + 4)
        nc.vector.tensor_copy(self.idx[:, level, :], self.row[:, :]).then_inc(self.idx_ready, 1)

    def gathers(self, pool):
        nc = self.nc
        pool.wait_ge(self.table_in, 16)
        with pool.Fori(0, TURNS) as it:
            for level in range(2):
                pool.wait_ge(self.idx_ready, it * 2 + (level + 1))
                pool_gate(nc, self.K)
                table = self.K.top_d if level == 0 else self.K.dst_d.rearrange("(r f) -> r f", f=FAN)
                for t in range(CHUNK):
                    nc.gpsimd.indirect_dma_start(
                        out=self.got[:, level, t, :], out_offset=None, in_=table,
                        in_offset=bass.IndirectOffsetOnAxis(ap=self.idx[:, level, t:t + 1], axis=0),
                    ).then_inc(self.rows_in[level], 16)


def stage_steps(nc, K):
    with Scope(nc, "steps") as s:
        rendT = s.sb("rendT", [TILES, P])
        rstartT = s.sb("rstartT", [TILES, P])
        zero = s.sb("zero1", [1, 1])
        part = s.sb("part", [TILES, 1])
        thr = s.sb("thr", [TILES, 1])
        ends = s.sb("ends", [TILES, STEPS])
        reach = s.sb("reach", [TILES, STEPS])
        ones = s.sb("ones_t", [TILES, 128])
        stepf = s.sb("stepf", [128, STEPS])
        group = s.sb("groupf", [1, STEPS])
        ps = s.ps("ps_steps", [128, 3, 512])
        made = s.sem("made")
        turned = s.sem("turned")
        rend_ready = s.sem("rend_ready")
        stored = s.sem("stored")
        loaded = s.sem("loaded")
        dve_done = s.sem("dve_done")
        counted = s.sem("counted")
        block = s.block()

        @block.gpsimd
        def _(pool):
            nc.gpsimd.iota(ends[:], pattern=[[EG, STEPS]], base=EG, channel_multiplier=0,
                           allow_small_or_imprecise_dtypes=True).then_inc(made, 1)
            nc.gpsimd.iota(part[:], pattern=[[0, 1]], base=0, channel_multiplier=EG,
                           allow_small_or_imprecise_dtypes=True).then_inc(made, 1)
            nc.gpsimd.iota(stepf[:], pattern=[[1, STEPS]], base=0, channel_multiplier=0,
                           allow_small_or_imprecise_dtypes=True).then_inc(made, 1)

        @block.tensor
        def _(pe):
            nc.tensor.transpose(ps[0:TILES, 0, 0:P], K.rend[:], K.ident[0:P, 0:P]).then_inc(turned, 1)
            pe.wait_ge(loaded, 16)
            nc.tensor.transpose(ps[0:P, 1, 0:TILES], rstartT[:], K.ident[0:TILES, 0:TILES]).then_inc(turned, 1)
            pe.wait_ge(counted, 1)
            nc.tensor.matmul(ps[:, 2, 0:STEPS], ones[:], reach[:], start=True, stop=True).then_inc(turned, 1)

        @block.sync
        def _(sp):
            sp.wait_ge(rend_ready, 2)
            sp.dma_start(K.rp_d[1:N + 1], rendT[:, :]).then_inc(stored, 16)
            sp.dma_start(K.rp_d[0:1], zero[0, :]).then_inc(stored, 16)
            sp.wait_ge(stored, 32)
            sp.dma_start(rstartT[:, :], K.rp_d[0:N].rearrange("(t p) -> t p", p=P)).then_inc(loaded, 16)

        @block.vector
        def _(dve):
            c = Chain(dve, dve_done)
            c.did(nc.vector.memset(ones[:], 1.0))
            nc.vector.memset(zero[:], 0.0).then_inc(rend_ready, 1)
            dve.wait_ge(turned, 1)
            nc.vector.tensor_copy(rendT[:, :], ps[0:TILES, 0, 0:P]).then_inc(rend_ready, 1)
            dve.wait_ge(made, 3)
            dve.wait_ge(loaded, 16)
            c.did(nc.vector.tensor_tensor(thr[:], rstartT[:, 0:1], part[:], ALU.add))
            c.settle()
            nc.vector.tensor_scalar(reach[:], ends[:], thr[:, 0:1], None, ALU.is_gt).then_inc(counted, 1)
            dve.wait_ge(turned, 2)
            c.did(nc.vector.tensor_copy(K.rstart[:, :], ps[0:P, 1, 0:TILES]))
            dve.wait_ge(turned, 3)
            c.did(nc.vector.tensor_scalar(K.step_node[:, :], ps[:, 2, 0:STEPS], float(P), float(P), ALU.mult, ALU.subtract))
            c.did(nc.vector.tensor_scalar(K.step_tile[:, :], ps[0:1, 2, 0:STEPS], 1.0, None, ALU.subtract))
            c.did(nc.vector.tensor_tensor(group[:, :], stepf[0:1, :], ps[0:1, 2, 0:STEPS], ALU.subtract))
            c.settle()
            c.did(nc.vector.tensor_scalar(K.step_group[:, :], group[:, :], 1.0, None, ALU.add))
            c.settle()


def stage_embed(nc, K, A):
    U = UNROLL
    with Scope(nc, "embed") as s:
        wx = s.sb("wx", [128, HC, HW])
        att = s.sb("att", [128, 2, H])
        wtmp = s.sb("wtmp", [128, HC, 2, H])
        x = s.sb("x_in", [P, U, GT, H])
        xn = s.sb("xn", [P, U, GT, H])
        xt = s.sb("xt", [128, U, HC, GN])
        hs = s.sb("hs", [P, U, GT, HW])
        stats = s.sb("stats", [P, GT, 6])
        mv = s.sb("mv", [P, GT, 3])
        var = s.sb("var", [P, GT])
        std = s.sb("std", [P, GT])
        rstd = s.sb("rstd", [P, GT])
        tp = s.ps("tp", [128, 2, HC, 512])
        hp = s.ps("hp", [128, GT, 512])
        w_in = s.sem("w_in")
        wx_ready = s.sem("wx_ready")
        x_in = s.sems("x_in", U)
        var_ready = s.sem("var_ready")
        std_ready = s.sem("std_ready")
        xn_ready = s.sem("xn_ready")
        xn_out = s.sems("xn_out", U)
        tp_ready = s.sem("tp_ready")
        xt_ready = s.sem("xt_ready")
        xt_out = s.sems("xt_out", U)
        h_ready = s.sem("h_ready")
        hs_ready = s.sem("hs_ready")
        h_out = s.sems("h_out", U)
        asd_ready = s.sem("asd_ready")
        a_out = s.sem("a_out")
        dve_done = s.sem("dve_done")
        block = s.block()
        xg = A.x.rearrange("(g t p) f -> g p t f", p=P, t=GT)
        xng = K.xn_d.rearrange("(g t p) f -> g p t f", p=P, t=GT)
        hg = K.h_d.rearrange("(g t p) f -> g p t f", p=P, t=GT)
        find = EdgeSearch(nc, K, s)

        @block.gpsimd
        def _(pool):
            find.gathers(pool)

        @block.sync
        def _(sp):
            sp.dma_start(wx[:, :, 0:H], A.W.rearrange("(c p) n -> p c n", p=128)).then_inc(w_in, 16)
            for k, a in enumerate((A.att_src, A.att_dst)):
                sp.dma_start(att[:, k, :], a.rearrange("(a h) o -> a (h o)", a=1).to_broadcast([128, H])).then_inc(w_in, 16)
            for u in range(U):
                rows_split(sp, x[:, u], xg[u], x_in[u])

            find.load(sp, A)

            def body(it, more):
                for u in range(U):
                    g = it * U + u
                    sp.wait_ge(xn_ready, g * GT + GT)
                    if more:
                        rows_split(sp, x[:, u], one(xg, g + U), x_in[u])
                    rows_split(sp, one(xng, g), xn[:, u], xn_out[u])
                    sp.wait_ge(xt_ready, g + 1)
                    sp.dma_start(one(K.xt_d, g), xt[:, u].rearrange("p c n -> p (c n)")).then_inc(xt_out[u], 16)
                    sp.wait_ge(hs_ready, g + 1)
                    rows_split(sp, one(hg, g), hs[:, u, :, 0:H], h_out[u])

            with sp.Fori(0, TURNS - 1) as it:
                body(it, True)
            body(TURNS - 1, False)
            sp.wait_ge(asd_ready, GROUPS)
            rows_split(sp, K.a_d.rearrange("(t p) h -> p t h", p=P), K.asd[:, :, 0:HEADS], a_out)
            sp.wait_ge(a_out, 32)
            for u in range(U):
                sp.wait_ge(xn_out[u], 32 * TURNS)
                sp.wait_ge(xt_out[u], 16 * TURNS)
                sp.wait_ge(h_out[u], 32 * TURNS)

        @block.vector
        def _(dve):
            find.prepare(dve)
            dve.wait_ge(w_in, 48)
            for k in range(2):
                for c in range(HC):
                    nc.vector.tensor_tensor(wtmp[:, c, k, :], wx[:, c, 0:H], att[:, k, :], ALU.mult).then_inc(wx_ready, 1)
            dve.wait_ge(wx_ready, 4)
            for k in range(2):
                for c in range(HC):
                    nc.vector.tensor_reduce(wx[:, c, H + k * HEADS:H + (k + 1) * HEADS],
                                            wtmp[:, c, k, :].rearrange("p (h o) -> p h o", h=HEADS), X, ALU.add).then_inc(wx_ready, 1)

            def h_copy(g, v, stored, fresh):
                dve.wait_ge(h_ready, g + 1)
                if not fresh:
                    dve.wait_ge(h_out[v], stored)
                nc.vector.tensor_copy(K.asd[:, bass.ds(g * GT, GT), :], hp[0:P, :, H:HW]).then_inc(asd_ready, 1)
                nc.vector.tensor_copy(hs[:, v], hp[0:P, :, 0:HW]).then_inc(hs_ready, 1)

            find.pivots(dve)
            per = U * (2 * GT + 1)

            def body(it, first):
                c = Chain(dve, dve_done, per, it)
                for u in range(U):
                    g = it * U + u
                    dve.wait_ge(x_in[u], it * 32 + 32)
                    norm_stats(nc, c, x[:, u], stats, mv, var).then_inc(var_ready, 1)
                    if not (first and u < 2):
                        h_copy(g - 2, (u - 2) % U, it * 32 if u >= 2 else (it - 1) * 32, first or (u < 2 and first))
                    if u % 2 == 0:
                        find.count(dve, u // 2, it)
                    dve.wait_ge(std_ready, g + 1)
                    if not first:
                        dve.wait_ge(xn_out[u], it * 32)
                        dve.wait_ge(tp_ready, g - U + 1)
                    for ins in norm_rows(nc, c, x[:, u], xn[:, u], mv, std, rstd):
                        ins.then_inc(xn_ready, 1)
                c.close()

            turns(dve, TURNS, body)
            for g in (GROUPS - 2, GROUPS - 1):
                h_copy(g, g % U, 32 * (TURNS - 1), False)

        @block.scalar
        def _(act):
            def body(it, first):
                for u in range(U):
                    g = it * U + u
                    act.wait_ge(var_ready, g + 1)
                    nc.scalar.activation(std[:, :], var[:, :], ACT.Sqrt).then_inc(std_ready, 1)
                    act.wait_ge(tp_ready, g + 1)
                    if not first:
                        act.wait_ge(xt_out[u], it * 16)
                        act.wait_ge(h_ready, g - U + 1)
                    nc.scalar.activation(xt[:, u], tp[:, u % 2, :, 0:GN], ACT.Copy).then_inc(xt_ready, 1)

            turns(act, TURNS, body)

        @block.tensor
        def _(pe):
            pe.wait_ge(wx_ready, 8)

            def project(g, u, first):
                pe.wait_ge(xt_ready, g + 1)
                if not first:
                    pe.wait_ge(hs_ready, g)
                for t in range(GT):
                    for k in range(HC):
                        mm = nc.tensor.matmul(hp[0:P, t, 0:HW], xt[:, u, k, t * P:(t + 1) * P], wx[:, k, :],
                                              start=(k == 0), stop=(k == HC - 1))
                mm.then_inc(h_ready, 1)

            def body(it, first):
                for u in range(U):
                    g = it * U + u
                    pe.wait_ge(xn_ready, g * GT + GT)
                    if not (first and u < 2):
                        pe.wait_ge(xt_ready, g if u == 0 else g - 1)
                    for t in range(GT):
                        for k in range(HC):
                            mm = nc.tensor.transpose(tp[:, u % 2, k, t * P:(t + 1) * P],
                                                     xn[:, u, t, k * 128:(k + 1) * 128], K.ident[0:P, 0:P])
                    mm.then_inc(tp_ready, 1)
                    if not (first and u == 0):
                        project(g - 1, (u - 1) % U, first and u == 1)

            turns(pe, TURNS, body)
            project(GROUPS - 1, U - 1, False)


class SourceGather:

    GCOLS = 34

    def __init__(self, nc, K, s):
        self.nc, self.K = nc, K
        self.src = s.sb("src_all", [128, EC], I32)
        self.idx = s.sb("src_idx", [128, 2, self.GCOLS], I32)
        self.got = s.sb("as_got", [128, 2, self.GCOLS, HEADS])
        self.src_in = s.sem("src_in")
        self.idx_ready = s.sem("src_idx_ready")
        self.rows_in = s.sems("as_rows_in", 2)
        self.rows_out = s.sems("as_rows_out", 2)

    def run(self, pool):
        nc, n = self.nc, self.GCOLS
        pool.dma_start(self.src[:, :], self.K.src_d.rearrange("(p j) -> p j", p=128)).then_inc(self.src_in, 16)
        pool.wait_ge(self.src_in, 16)
        table = self.K.a_d
        kept = self.K.as_d.rearrange("(p j) h -> p j h", p=128)

        def store(turn, slot):
            pool.wait_ge(self.rows_in[slot], turn * (16 * n) + 16 * n)
            pool_gate(nc, self.K)
            pool.dma_start(kept[:, bass.ds((turn * 2 + slot) * n, n), :], self.got[:, slot]).then_inc(self.rows_out[slot], 16)

        def body(it, first):
            for slot in range(2):
                if not first:
                    pool.wait_ge(self.rows_out[slot], it * 16)
                nc.gpsimd.tensor_copy(self.idx[:, slot, :], self.src[:, bass.ds((it * 2 + slot) * n, n)]).then_inc(self.idx_ready, 1)
                pool.wait_ge(self.idx_ready, it * 2 + slot + 1)
                pool_gate(nc, self.K)
                for j in range(n):
                    nc.gpsimd.indirect_dma_start(
                        out=self.got[:, slot, j, :], out_offset=None, in_=table,
                        in_offset=bass.IndirectOffsetOnAxis(ap=self.idx[:, slot, j:j + 1], axis=0),
                    ).then_inc(self.rows_in[slot], 16)
                if slot:
                    store(it, 0)
                elif not first:
                    store(it - 1, 1)

        count = EC // (2 * n)
        turns(pool, count, body)
        store(count - 1, 1)
        for slot in range(2):
            pool.wait_ge(self.rows_out[slot], 16 * count)


def stage_mix(nc, K, A):
    U = UNROLL
    C = H
    GH = C // 4
    D = 32
    with Scope(nc, "mix") as s:
        gather = SourceGather(nc, K, s)
        wqkv = s.sb("wqkv", [128, HC, 3 * C])
        wg1 = s.sb("wg1", [128, HC, GH])
        wg1g = s.sb("wg1g", [128, HC, GH])
        lng = s.sb("lng", [128, HC])
        lnb = s.sb("lnb", [128, HC])
        bg1 = s.sb("bg1", [GH, 1])
        bias1 = s.sb("bias1", [GH, 1])
        wg2 = s.sb("wg2", [GH, C])
        bg2 = s.sb("bg2", [128, HC])
        wproj = s.sb("wproj", [128, HC, C])
        bproj = s.sb("bproj", [P, C])
        kmax_g = s.sb("kmax_g", [128, HC, GROUPS])
        kmax = s.sb("kmax", [128, HC])
        nkmax = s.sb("nkmax", [1, C])
        ones = s.sb("ones1", [1, P])
        wqT = s.sb("wqT", [128, HC, C])
        ctx_acc = s.sb("ctx_acc", [128, HC, 129])
        ctx_inv = s.sb("ctx_inv", [128, HC])
        ctx_bd = s.sb("ctx_bd", [128, HC, 128])
        wqc = s.sb("wqc", [128, HC, C])
        xt = s.sb("xt2", [128, U, HC * GN])
        io = s.sb("io2", [128, U, GT * H])
        z = s.sb("z", [P, GT, H])
        zt = s.sb("zt", [128, HC, GN])
        hgt = s.sb("hgt", [GH, GN])
        gt = s.sb("gt", [128, 2, HC * GN])
        pk = s.sb("pk", [P, 2, C])
        vx = s.sb("vx", [P, 2, HC, 129])
        og = s.sb("og", [128, HC * GN])
        mo = s.sb("mo", [P, 2, GT, C])
        stats = s.sb("stats2", [P, GT, 6])
        mv = s.sb("mv2", [P, GT, 3])
        var = s.sb("var2", [P, GT])
        std = s.sb("std2", [P, GT])
        rstd = s.sb("rstd2", [P, GT])
        ps = s.ps("ps_mix", [128, 8, 512])
        w_in = s.sem("w_in2")
        set_up = s.sem("set_up")
        in_a = s.sems("in_a", U)
        in_b = s.sems("in_b", U)
        in_c = s.sems("in_c", U)
        var_ready, std_ready, z_ready, zt_psum, zt_ready = (s.sem(n) for n in (
            "var_ready2", "std_ready2", "z_ready", "zt_psum", "zt_ready"))
        kt_ready, kt_used, hg_psum, hg_ready, gate_psum, gate_ready = (s.sem(n) for n in (
            "kt_ready", "kt_used", "hg_psum", "hg_ready", "gate_psum", "gate_ready"))
        gate_out = s.sems("gate_out", 2)
        kmax_ready, kmax_row, nkmax_ready = s.sem("kmax_ready"), s.sem("kmax_row"), s.sem("nkmax_ready")
        kv_psum, p_ready, v_ready, ctx_psum, ctx_added = (s.sem(n) for n in (
            "kv_psum", "p_ready", "v_ready", "ctx_psum", "ctx_added"))
        bd_ready, wqc_psum, wqc_ready = s.sem("bd_ready"), s.sem("wqc_psum"), s.sem("wqc_ready")
        out_psum, og_ready, mix_psum, mix_ready = (s.sem(n) for n in ("out_psum", "og_ready", "mix_psum", "mix_ready"))
        mix_out = s.sems("mix_out", 2)
        dve_done = s.sem("dve_done2")
        dve_end = s.sem("dve_end2")
        block = s.block()
        xng = K.xn_d.rearrange("(g t p) f -> g p t f", p=P, t=GT)
        mixg = K.mix_d.rearrange("(g t p) f -> g p t f", p=P, t=GT)
        rows = lambda u: io[0:P, u, :].rearrange("p (t f) -> p t f", t=GT)
        fm = lambda t, k: t.rearrange("p (k n) -> p k n", k=HC)[:, k, :]

        @block.gpsimd
        def _(pool):
            gather.run(pool)

        @block.sync
        def _(sp):
            with nc.allow_non_contiguous_dma(reason="biases to columns, once"):
                for t, a in ((wqkv, A.mix_Wqkv), (wg1, A.mix_Wg1), (wproj, A.mix_Wproj)):
                    sp.dma_start(t[:], a.rearrange("(c p) n -> p c n", p=128)).then_inc(w_in, 16)
                for t, a in ((lng, A.mix_ln_g), (lnb, A.mix_ln_b), (bg2, A.mix_bg2)):
                    sp.dma_start(t[:], a.rearrange("(c p) -> p c", p=128)).then_inc(w_in, 16)
                sp.dma_start(bg1[:, :], A.mix_bg1.rearrange("(p a) -> p a", a=1)).then_inc(w_in, 16)
            sp.dma_start(wg2[:, :], A.mix_Wg2).then_inc(w_in, 16)
            sp.dma_start(bproj[:, :], A.mix_bproj.rearrange("(a n) -> a n", a=1).to_broadcast([P, C])).then_inc(w_in, 16)

            def load_a(g, u):
                sp.dma_start(xt[:, u, :], one(K.xt_d, g)).then_inc(in_a[u], 16)
                rows_split(sp, rows(u), one(xng, g), in_a[u])

            def load_b(g, u):
                sp.dma_start(xt[:, u, :], one(K.xt_d, g)).then_inc(in_b[u], 16)

            def load_c(g, u):
                sp.dma_start(xt[:, u, :], one(K.xt_d, g)).then_inc(in_c[u], 16)
                sp.dma_start(io[:, u, 0:HC * GN], one(K.gt_d, g)).then_inc(in_c[u], 16)

            for u in range(U):
                load_a(u, u)

            def gates(it, more):
                for u in range(U):
                    g = it * U + u
                    sp.wait_ge(kt_ready, g + 1)
                    sp.wait_ge(z_ready, g * GT + GT)
                    (load_a if more else load_b)(g + U if more else u, u)
                    sp.wait_ge(gate_ready, g + 1)
                    if isinstance(g, int):
                        sp.dma_start(K.gt_d[g], gt[:, u % 2, :]).then_inc(gate_out[u % 2], 16)
                    else:
                        sp.dma_start(one(K.gt_d, g), gt[:, u % 2, :]).then_inc(gate_out[u % 2], 16)

            with sp.Fori(0, TURNS - 1) as it:
                gates(it, True)
            gates(TURNS - 1, False)

            def context(it, more):
                for u in range(U):
                    g = it * U + u
                    sp.wait_ge(kv_psum, g * GT + GT)
                    if more:
                        load_b(g + U, u)
                    else:
                        if u == 0:
                            for b in range(2):
                                sp.wait_ge(gate_out[b], 16 * (3 - b) * TURNS)
                        load_c(u, u)

            with sp.Fori(0, TURNS - 1) as it:
                context(it, True)
            context(TURNS - 1, False)

            def output(it, more):
                for u in range(U):
                    g = it * U + u
                    sp.wait_ge(og_ready, g + 1)
                    if more:
                        load_c(g + U, u)
                    sp.wait_ge(mix_ready, g + 1)
                    rows_split(sp, one(mixg, g), mo[:, u % 2], mix_out[u % 2])

            with sp.Fori(0, TURNS - 1) as it:
                output(it, True)
            output(TURNS - 1, False)
            for b in range(2):
                sp.wait_ge(mix_out[b], 32 * (3 - b) * TURNS)

        def stored(it, u, per):
            return (it * (3 if u % 2 == 0 else 2) + u // 2) * per

        @block.vector
        def _(dve):
            c = Chain(dve, dve_end)
            dve.wait_ge(w_in, 144)
            for k in range(HC):
                nc.vector.tensor_scalar(wg1g[:, k, :], wg1[:, k, :], lng[:, k:k + 1], None, ALU.mult).then_inc(set_up, 1)
            nc.vector.memset(ones[:], 1.0).then_inc(set_up, 1)
            nc.vector.memset(ctx_acc[:], 0.0).then_inc(set_up, 1)
            nc.vector.memset(ctx_bd[:], 0.0).then_inc(set_up, 1)
            for b in range(2):
                nc.vector.memset(vx[:, b, :, 128:129], 1.0).then_inc(set_up, 1)
            dve.wait_ge(wqc_psum, 1)
            nc.vector.tensor_tensor(bias1[:], ps[0:GH, 7, 0:1], bg1[:], ALU.add).then_inc(set_up, 1)
            for k in range(HC):
                nc.vector.tensor_copy(wqT[:, k, :], ps[:, k, 0:C]).then_inc(set_up, 1)

            per = U * (2 * GT + 1)

            def gates(it, first):
                c = Chain(dve, dve_done, per, it)
                for u in range(U):
                    g = it * U + u
                    dve.wait_ge(in_a[u], it * 48 + 48)
                    norm_stats(nc, c, rows(u), stats, mv, var).then_inc(var_ready, 1)
                    dve.wait_ge(kt_ready, g + 1)
                    nc.vector.tensor_reduce(kmax_g[:, :, bass.ds(g, 1)], ps[:, 0:2, 0:GN], X, ALU.max).then_inc(kt_used, 1)
                    dve.wait_ge(std_ready, g + 1)
                    if not (first and u == 0):
                        dve.wait_ge(zt_psum, g)
                    for ins in norm_rows(nc, c, rows(u), z, mv, std, rstd):
                        ins.then_inc(z_ready, 1)
                c.close()

            turns(dve, TURNS, gates)
            dve.wait_ge(kt_used, GROUPS)
            nc.vector.tensor_reduce(kmax[:], kmax_g[:], X, ALU.max).then_inc(kmax_ready, 1)
            dve.wait_ge(kmax_row, 1)
            nc.vector.tensor_scalar(nkmax[:], ps[0:1, 7, 0:C], -1.0, None, ALU.mult).then_inc(nkmax_ready, 1)

            def context(it, first):
                for u in range(U):
                    g = it * U + u
                    for t in range(GT):
                        i = g * GT + t
                        dve.wait_ge(kv_psum, i + 1)
                        if not (first and u == 0 and t < 2):
                            dve.wait_ge(ctx_psum, i - 1)
                        nc.vector.tensor_copy(vx[:, t % 2, :, 0:128],
                                              ps[0:P, 2 + t % 2, 0:C].rearrange("p (c v) -> p c v", c=HC)).then_inc(v_ready, 1)
                    dve.wait_ge(ctx_psum, g * GT + GT)
                    if not (first and u == 0):
                        dve.wait_ge(ctx_added, g)
                    nc.vector.tensor_tensor(ctx_acc[:], ctx_acc[:], ps[:, 4:6, 0:129], ALU.add).then_inc(ctx_added, 1)

            dve.wait_ge(set_up, 7)
            turns(dve, TURNS, context)
            dve.wait_ge(ctx_added, GROUPS)
            c.did(nc.vector.reciprocal(ctx_inv[:], ctx_acc[:, :, 128]))
            c.settle()
            for k in range(HC):
                for h in range(128 // D):
                    q = slice(h * D, h * D + D)
                    nc.vector.tensor_scalar(ctx_bd[q, k, q], ctx_acc[q, k, q], ctx_inv[q, k:k + 1], None,
                                            ALU.mult).then_inc(bd_ready, 1)
            dve.wait_ge(wqc_psum, 2)
            nc.vector.tensor_copy(wqc[:], ps[:, 6:8, 0:C]).then_inc(wqc_ready, 1)

            def output(it, first):
                for u in range(U):
                    g = it * U + u
                    dve.wait_ge(in_c[u], it * 32 + 32)
                    dve.wait_ge(out_psum, g + 1)
                    if not (first and u == 0):
                        dve.wait_ge(mix_psum, g)
                    nc.vector.tensor_tensor(og[:].rearrange("p (k n) -> p k n", k=HC), ps[:, 0:2, 0:GN],
                                            io[:, u, 0:HC * GN].rearrange("p (k n) -> p k n", k=HC), ALU.mult).then_inc(og_ready, 1)
                    dve.wait_ge(mix_psum, g + 1)
                    if not (first and u < 2):
                        dve.wait_ge(mix_out[u % 2], stored(it, u, 32))
                    nc.vector.tensor_tensor(mo[:, u % 2].rearrange("p (a b) f -> p a b f", a=2),
                                            ps[0:P, 2:4, :].rearrange("p a (b f) -> p a b f", b=2),
                                            bproj[:].rearrange("p (a b f) -> p a b f", a=1, b=1).to_broadcast([P, 2, 2, C]),
                                            ALU.add).then_inc(mix_ready, 1)

            turns(dve, TURNS, output)

        @block.scalar
        def _(act):
            act.wait_ge(set_up, 8)

            def gates(it, first):
                for u in range(U):
                    g = it * U + u
                    act.wait_ge(var_ready, g + 1)
                    nc.scalar.activation(std[:, :], var[:, :], ACT.Sqrt).then_inc(std_ready, 1)
                    act.wait_ge(zt_psum, g + 1)
                    if not (first and u == 0):
                        act.wait_ge(hg_psum, g)
                    nc.scalar.activation(zt[:], ps[:, 2:4, 0:GN], ACT.Copy).then_inc(zt_ready, 1)
                    act.wait_ge(hg_psum, g + 1)
                    nc.scalar.activation(hgt[:], ps[0:GH, 4, 0:GN], ACT.Gelu, bias=bias1[:, 0:1]).then_inc(hg_ready, 1)
                    act.wait_ge(gate_psum, g + 1)
                    if not (first and u < 2):
                        act.wait_ge(gate_out[u % 2], stored(it, u, 16))
                    nc.scalar.activation(fm(gt[:, u % 2, :], 0), ps[:, 5, 0:GN], ACT.Sigmoid, bias=bg2[:, 0:1])
                    nc.scalar.activation(fm(gt[:, u % 2, :], 1), ps[:, 6, 0:GN], ACT.Sigmoid, bias=bg2[:, 1:2]).then_inc(gate_ready, 1)

            turns(act, TURNS, gates)

            def context(it, first):
                for u in range(U):
                    for t in range(GT):
                        i = (it * U + u) * GT + t
                        act.wait_ge(kv_psum, i + 1)
                        if not (first and u == 0 and t < 2):
                            act.wait_ge(ctx_psum, i - 1)
                        nc.scalar.activation(pk[:, t % 2, :], ps[0:P, t % 2, 0:C], ACT.Exp).then_inc(p_ready, 1)

            turns(act, TURNS, context)

        @block.tensor
        def _(pe):
            pe.wait_ge(w_in, 144)
            for i in range(HC):
                for k in range(HC):
                    nc.tensor.transpose(ps[:, k, i * 128:(i + 1) * 128], wqkv[:, i, k * 128:(k + 1) * 128], K.ident[:])
            for k in range(HC):
                mm = nc.tensor.matmul(ps[0:GH, 7, 0:1], wg1[:, k, :], lnb[:, k:k + 1], start=(k == 0), stop=(k == HC - 1))
            mm.then_inc(wqc_psum, 1)
            pe.wait_ge(set_up, 10)

            def gates(it, first):
                for u in range(U):
                    g = it * U + u
                    pe.wait_ge(in_a[u], it * 48 + 48)
                    if not (first and u == 0):
                        pe.wait_ge(kt_used, g)
                    for m in range(HC):
                        for k in range(HC):
                            mm = nc.tensor.matmul(ps[:, m, 0:GN], wqkv[:, k, C + m * 128:C + (m + 1) * 128],
                                                  fm(xt[:, u, :], k), start=(k == 0), stop=(k == HC - 1))
                    mm.then_inc(kt_ready, 1)
                    pe.wait_ge(z_ready, g * GT + GT)
                    if not (first and u == 0):
                        pe.wait_ge(zt_ready, g)
                    for t in range(GT):
                        for k in range(HC):
                            mm = nc.tensor.transpose(ps[:, 2 + k, t * P:(t + 1) * P], z[:, t, k * 128:(k + 1) * 128],
                                                     K.ident[0:P, 0:P])
                    mm.then_inc(zt_psum, 1)
                    pe.wait_ge(zt_ready, g + 1)
                    if not (first and u == 0):
                        pe.wait_ge(hg_ready, g)
                    for k in range(HC):
                        mm = nc.tensor.matmul(ps[0:GH, 4, 0:GN], wg1g[:, k, :], zt[:, k, :], start=(k == 0), stop=(k == HC - 1))
                    mm.then_inc(hg_psum, 1)
                    pe.wait_ge(hg_ready, g + 1)
                    if not (first and u == 0):
                        pe.wait_ge(gate_ready, g)
                    for m in range(HC):
                        mm = nc.tensor.matmul(ps[:, 5 + m, 0:GN], wg2[:, m * 128:(m + 1) * 128], hgt[:], start=True, stop=True)
                    mm.then_inc(gate_psum, 1)

            turns(pe, TURNS, gates)
            pe.wait_ge(kmax_ready, 1)
            for k in range(HC):
                mm = nc.tensor.transpose(ps[0:1, 7, k * 128:(k + 1) * 128], kmax[:, k:k + 1], K.ident[:])
            mm.then_inc(kmax_row, 1)
            pe.wait_ge(nkmax_ready, 1)
            pe.wait_ge(gate_ready, GROUPS)

            def context(it, first):
                for u in range(U):
                    for t in range(GT):
                        i = (it * U + u) * GT + t
                        if t == 0:
                            pe.wait_ge(in_b[u], it * 16 + 16)
                        if not (first and u == 0 and t < 2):
                            pe.wait_ge(p_ready, i - 1)
                            pe.wait_ge(v_ready, i - 1)
                        for k in range(HC):
                            nc.tensor.matmul(ps[0:P, t % 2, 0:C], fm(xt[:, u, :], k)[:, t * P:(t + 1) * P],
                                             wqkv[:, k, C:2 * C], start=(k == 0), stop=False)
                        nc.tensor.matmul(ps[0:P, t % 2, 0:C], ones[:], nkmax[:], start=False, stop=True)
                        for k in range(HC):
                            mm = nc.tensor.matmul(ps[0:P, 2 + t % 2, 0:C], fm(xt[:, u, :], k)[:, t * P:(t + 1) * P],
                                                  wqkv[:, k, 2 * C:3 * C], start=(k == 0), stop=(k == HC - 1))
                        mm.then_inc(kv_psum, 1)
                        pe.wait_ge(p_ready, i + 1)
                        pe.wait_ge(v_ready, i + 1)
                        if t == 0 and not (first and u == 0):
                            pe.wait_ge(ctx_added, it * U + u)
                        for k in range(HC):
                            mm = nc.tensor.matmul(ps[:, 4 + k, 0:129], pk[:, t % 2, k * 128:(k + 1) * 128],
                                                  vx[:, t % 2, k, :], start=(t == 0), stop=(t == GT - 1))
                        mm.then_inc(ctx_psum, 1)

            turns(pe, TURNS, context)
            pe.wait_ge(bd_ready, HC * 128 // D)
            for m in range(HC):
                for k in range(HC):
                    mm = nc.tensor.matmul(ps[:, 6 + m, k * 128:(k + 1) * 128], wqT[:, k, m * 128:(m + 1) * 128],
                                          ctx_bd[:, k, :], start=True, stop=True)
            mm.then_inc(wqc_psum, 1)
            pe.wait_ge(wqc_ready, 1)

            def output(it, first):
                for u in range(U):
                    g = it * U + u
                    pe.wait_ge(in_c[u], it * 32 + 32)
                    if not (first and u == 0):
                        pe.wait_ge(og_ready, g)
                    for m in range(HC):
                        for k in range(HC):
                            mm = nc.tensor.matmul(ps[:, m, 0:GN], wqc[:, k, m * 128:(m + 1) * 128],
                                                  fm(xt[:, u, :], k), start=(k == 0), stop=(k == HC - 1))
                    mm.then_inc(out_psum, 1)
                    pe.wait_ge(og_ready, g + 1)
                    if not (first and u == 0):
                        pe.wait_ge(mix_ready, g)
                    for t in range(GT):
                        for k in range(HC):
                            mm = nc.tensor.matmul(ps[0:P, 2 + t // 2, (t % 2) * C:(t % 2 + 1) * C],
                                                  fm(og[:], k)[:, t * P:(t + 1) * P], wproj[:, k, :],
                                                  start=(k == 0), stop=(k == HC - 1))
                    mm.then_inc(mix_psum, 1)

            turns(pe, TURNS, output)


def zero_fill(nc, K):
    with Scope(nc, "zero_fill") as s:
        zeros = s.sb("zeros", [128, 4 * EC])
        ready = s.sem("zeros_ready")
        out = s.sem("zeros_out")
        block = s.block()
        at = K.rec_d.rearrange("(p j) r -> p (j r)", p=128)

        @block.vector
        def _(dve):
            nc.vector.memset(zeros[:], 0.0).then_inc(ready, 1)

        @block.sync
        def _(sp):
            sp.wait_ge(ready, 1)
            for k in range(2):
                sp.dma_start(at[:, k * 4 * EC:(k + 1) * 4 * EC], zeros[:, :]).then_inc(out, 16)
            n = SLOTS // 128 * TOKW // 8
            rest = K.buf_d.rearrange("(p j) r -> p (j r)", p=128)
            for k in range(8):
                sp.dma_start(rest[:, k * n:(k + 1) * n], zeros[:, 0:n]).then_inc(out, 16)
            sp.dma_start(K.y_d[SLOTS:SLOTS + 1, :], zeros[0:1, 0:H]).then_inc(out, 16)
            sp.wait_ge(out, 16 * 11)


def stage_alpha(nc, K):
    with Scope(nc, "alpha") as s:
        a4 = s.sb("a4", [128, EC, HEADS])
        m4 = s.sb("m4", [128, EC, HEADS])
        r8 = s.sb("r8", [128, EC, 2 * HEADS])
        meta = s.sb("meta", [128, EC, 6])
        dst = s.sb("dst_b", [128, EC], I32)
        prev = s.sb("prev_b", [128, EC], I32)
        src = s.sb("src_b", [128, EC], I32)
        same = s.sb("same", [128, EC])
        pen = s.sb("pen", [128, EC])
        head = s.sb("head", [128, EC])
        headpen = s.sb("headpen", [128, EC])
        tail = s.sb("tail", [128, 2, 2 * HEADS])
        rows = s.sb("rows", [2 * HEADS, 2, 128])
        run = s.sb("run", [2 * HEADS, 128])
        carry = s.sb("carry", [128, 2 * HEADS])
        has = s.sb("has", [P, TILES])
        miss = s.sb("miss", [P, TILES])
        last = s.sb("last", [P, TILES])
        lasti = s.sb("lasti", [P, TILES], I32)
        first = s.sb("first", [P, TILES])
        firsti = s.sb("firsti", [P, TILES], I32)
        seg = s.sb("seg", [P, TILES, HEADS])
        rec = s.sb("rec", [P, TILES, 2 * HEADS])
        tmp = s.sb("tmp_n", [P, TILES, HEADS])
        idx = s.sb("idx_c", [P, 2, CHUNK], I32)
        got = s.sb("got_c", [P, CHUNK, 2 * HEADS])
        ps = s.ps("ps_alpha", [128, 2, 512])
        edges_in = s.sem("edges_in")
        as_in = s.sem("as_in")
        rec_in = s.sem("rec_in")
        turned = s.sem("turned2")
        rows_ready = s.sem("rows_ready")
        m4_ready, m4_out = s.sem("m4_ready"), s.sem("m4_out")
        idx_ready, rec_ready = s.sem("node_idx_ready"), s.sem("rec_ready")
        copied, seg_in, seg_ready, rec_out, rec_free = (s.sem(n) for n in ("copied", "seg_in", "seg_ready", "rec_out", "rec_free"))
        arg_ready, ex_ready = s.sem("arg_ready"), s.sem("ex_ready")
        meta_ready, meta_out = s.sem("meta_ready"), s.sem("meta_out")
        done = s.sem("dve_done3")
        block = s.block()
        per_edge = lambda a: a.rearrange("(p j) h -> p j h", p=128)

        @block.sync
        def _(sp):
            flat = K.dst_d
            sp.dma_start(dst[:, :], flat[0:EP].rearrange("(p j) -> p j", p=128)).then_inc(edges_in, 16)
            sp.dma_start(prev[1:128, :], flat[EC - 1:EP - 1].rearrange("(p j) -> p j", p=127)).then_inc(edges_in, 16)
            sp.dma_start(prev[0:1, 1:EC], flat[0:EC - 1].rearrange("(p j) -> p j", p=1)).then_inc(edges_in, 16)
            sp.dma_start(src[:, :], K.src_d.rearrange("(p j) -> p j", p=128)).then_inc(edges_in, 16)
            sp.dma_start(a4[:], per_edge(K.as_d)).then_inc(as_in, 16)
            sp.wait_ge(m4_ready, HEADS)
            sp.dma_start(per_edge(K.mx_d), m4[:]).then_inc(m4_out, 16)
            sp.wait_ge(rec_out, 16 * TILES)
            sp.dma_start(r8[:], per_edge(K.rec_d)).then_inc(rec_in, 16)
            sp.wait_ge(meta_ready, 3)
            sp.dma_start(per_edge(K.meta_d), meta[:]).then_inc(meta_out, 16)
            sp.wait_ge(meta_out, 16)

        @block.gpsimd
        def _(pool):
            pool.wait_ge(m4_out, 16)
            pool.wait_ge(idx_ready, 2)
            with pool.Fori(0, TURNS) as it:
                nc.gpsimd.tensor_copy(idx[:, 0, :], lasti[:, bass.ds(it * CHUNK, CHUNK)]).then_inc(copied, 1)
                pool.wait_ge(copied, it * 2 + 1)
                pool_gate(nc, K)
                for t in range(CHUNK):
                    nc.gpsimd.indirect_dma_start(
                        out=got[:, t, 0:HEADS], out_offset=None, in_=K.mx_d,
                        in_offset=bass.IndirectOffsetOnAxis(ap=idx[:, 0, t:t + 1], axis=0)).then_inc(seg_in, 16)
                pool.wait_ge(seg_in, it * (16 * CHUNK) + 16 * CHUNK)
                pool_gate(nc, K)
                nc.gpsimd.tensor_copy(seg[:, bass.ds(it * CHUNK, CHUNK), :], got[:, :, 0:HEADS]).then_inc(copied, 1)
                pool.wait_ge(copied, it * 2 + 2)
                pool_gate(nc, K)
            nc.gpsimd.tensor_copy(idx[:, 0, :], idx[:, 0, :]).then_inc(seg_ready, 1)
            pool.wait_ge(rec_ready, 1)
            with pool.Fori(0, TURNS) as it:
                nc.gpsimd.tensor_copy(idx[:, 1, :], firsti[:, bass.ds(it * CHUNK, CHUNK)]).then_inc(copied, 1)
                nc.gpsimd.tensor_copy(got[:], rec[:, bass.ds(it * CHUNK, CHUNK), :]).then_inc(copied, 1)
                pool.wait_ge(copied, it * 2 + (2 * TURNS + 2))
                pool_gate(nc, K)
                for t in range(CHUNK):
                    nc.gpsimd.indirect_dma_start(
                        out=K.rec_d, out_offset=bass.IndirectOffsetOnAxis(ap=idx[:, 1, t:t + 1], axis=0),
                        in_=got[:, t, :], in_offset=None, bounds_check=EP - 1, oob_is_err=False).then_inc(rec_out, 16)
                pool.wait_ge(rec_out, it * (16 * CHUNK) + 16 * CHUNK)
                pool_gate(nc, K)

        @block.tensor
        def _(pe):
            w = HEADS
            for k in range(2):
                w = HEADS * (k + 1)
                pe.wait_ge(rows_ready, 4 * k + 2)
                for q in range(2):
                    mm = nc.tensor.transpose(ps[0:w, 0, q * 128:(q + 1) * 128], tail[:, q, 0:w], K.ident[:])
                mm.then_inc(turned, 1)
                pe.wait_ge(rows_ready, 4 * k + 4)
                nc.tensor.transpose(ps[:, 1, 0:w], run[0:w, :], K.ident[0:w, 0:w]).then_inc(turned, 1)

        @block.scalar
        def _(act):
            act.wait_ge(arg_ready, 1)
            nc.scalar.activation(K.exs[:], K.exs[:], ACT.Exp).then_inc(ex_ready, 1)
            act.wait_ge(arg_ready, 2)
            nc.scalar.activation(meta[:, :, 0:HEADS], a4[:], ACT.Exp).then_inc(meta_ready, 1)

        @block.vector
        def _(dve):
            c = Chain(dve, done)

            def carries(k, fields, scan_row):
                w = HEADS * (k + 1)
                dve.wait_ge(turned, 2 * k + 1)
                c.did(nc.vector.tensor_copy(rows[0:w, :, :], ps[0:w, 0, 0:256].rearrange("p (a b) -> p a b", a=2)))
                c.settle()
                nc.vector.memset(run[0:w, 0:1], NEVER if k == 0 else 0.0).then_inc(rows_ready, 1)
                scan_row(w)
                dve.wait_ge(turned, 2 * k + 2)
                c.did(nc.vector.tensor_copy(carry[:, 0:w], ps[:, 1, 0:w]))
                c.settle()

            dve.wait_ge(edges_in, 64)
            c.did(nc.vector.memset(prev[0:1, 0:1], -1))
            c.settle()
            c.did(nc.vector.tensor_tensor(same[:], dst[:], prev[:], ALU.is_equal))
            c.settle()
            c.did(nc.vector.tensor_scalar(pen[:], same[:], 1.0, -NEVER, ALU.subtract, ALU.mult))
            c.did(nc.vector.tensor_tensor_scan(head[:], same[:], same[:], 1.0, ALU.mult, ALU.mult))
            c.settle()
            c.did(nc.vector.tensor_scalar(headpen[:], head[:], 1.0, -NEVER, ALU.subtract, ALU.mult))
            c.did(nc.vector.tensor_tensor(has[:], K.rend[:], K.rstart[:], ALU.is_gt))
            c.settle()
            c.did(nc.vector.tensor_scalar(miss[:], has[:], 1.0, -NEVER, ALU.subtract, ALU.mult))
            c.did(nc.vector.scalar_tensor_tensor(last[:], K.rend[:], 1.0, has[:], ALU.subtract, ALU.mult))
            c.did(nc.vector.tensor_scalar(first[:], has[:], -4194304.0, 4194304.0, ALU.mult, ALU.add))
            c.settle()
            nc.vector.tensor_copy(lasti[:], last[:]).then_inc(idx_ready, 1)
            c.did(nc.vector.tensor_tensor(first[:], first[:], K.rstart[:], ALU.add))
            c.settle()
            nc.vector.tensor_copy(firsti[:], first[:]).then_inc(idx_ready, 1)
            dve.wait_ge(as_in, 16)
            for h in range(HEADS):
                c.did(nc.vector.tensor_tensor_scan(m4[:, :, h], pen[:], a4[:, :, h], NEVER, ALU.add, ALU.max))
            c.settle()
            nc.vector.tensor_copy(tail[:, 0, 0:HEADS], m4[:, EC - 1, :]).then_inc(rows_ready, 1)
            nc.vector.tensor_copy(tail[:, 1, 0:HEADS], headpen[:, EC - 1:EC].to_broadcast([128, HEADS])).then_inc(rows_ready, 1)

            def scan_max(w):
                nc.vector.tensor_tensor_scan(run[0:w, 1:128], rows[0:w, 1, 0:127], rows[0:w, 0, 0:127], NEVER,
                                             ALU.add, ALU.max).then_inc(rows_ready, 1)

            carries(0, HEADS, scan_max)
            for h in range(HEADS):
                nc.vector.scalar_tensor_tensor(m4[:, :, h], headpen[:], carry[:, h:h + 1], m4[:, :, h],
                                               ALU.add, ALU.max).then_inc(m4_ready, 1)
            dve.wait_ge(seg_ready, 1)
            c.did(nc.vector.tensor_tensor(seg[:], seg[:], miss[:].rearrange("p (t a) -> p t a", a=1).to_broadcast([P, TILES, HEADS]), ALU.add))
            c.settle()
            c.did(nc.vector.tensor_tensor(seg[:], seg[:], K.asd[:, :, 0:HEADS], ALU.max))
            c.settle()
            c.did(nc.vector.tensor_tensor(seg[:], seg[:], K.asd[:, :, HEADS:], ALU.add))
            c.did(nc.vector.tensor_tensor(tmp[:], K.asd[:, :, 0:HEADS], K.asd[:, :, HEADS:], ALU.add))
            c.did(nc.vector.tensor_copy(rec[:, :, 0:HEADS], K.asd[:, :, HEADS:]))
            c.settle()
            c.did(nc.vector.scalar_tensor_tensor(rec[:, :, HEADS:], seg[:], NEG_SLOPE, seg[:], ALU.mult, ALU.max))
            c.did(nc.vector.scalar_tensor_tensor(K.exs[:], tmp[:], NEG_SLOPE, tmp[:], ALU.mult, ALU.max))
            c.settle()
            nc.vector.tensor_copy(got[:, 0, 0:1], rec[:, 0, 0:1]).then_inc(rec_ready, 1)
            nc.vector.tensor_tensor(K.exs[:], K.exs[:], rec[:, :, HEADS:], ALU.subtract).then_inc(arg_ready, 1)
            nc.vector.tensor_copy(meta[:, :, 4], dst[:]).then_inc(meta_ready, 1)
            nc.vector.tensor_copy(meta[:, :, 5].bitcast(I32), src[:]).then_inc(meta_ready, 1)
            dve.wait_ge(rec_in, 16)
            for f in range(2 * HEADS):
                c.did(nc.vector.tensor_tensor_scan(r8[:, :, f], same[:], r8[:, :, f], 0.0, ALU.mult, ALU.add))
            c.settle()
            nc.vector.tensor_copy(tail[:, 0, :], r8[:, EC - 1, :]).then_inc(rows_ready, 1)
            nc.vector.tensor_copy(tail[:, 1, :], head[:, EC - 1:EC].to_broadcast([128, 2 * HEADS])).then_inc(rows_ready, 1)

            def scan_fill(w):
                nc.vector.tensor_tensor_scan(run[0:w, 1:128], rows[0:w, 1, 0:127], rows[0:w, 0, 0:127], 0.0,
                                             ALU.mult, ALU.add).then_inc(rows_ready, 1)

            carries(1, 2 * HEADS, scan_fill)
            for f in range(2 * HEADS):
                c.did(nc.vector.scalar_tensor_tensor(r8[:, :, f], head[:], carry[:, f:f + 1], r8[:, :, f],
                                                     ALU.mult, ALU.add))
            c.settle()
            c.did(nc.vector.tensor_tensor(a4[:], a4[:], r8[:, :, 0:HEADS], ALU.add))
            c.settle()
            c.did(nc.vector.scalar_tensor_tensor(a4[:], a4[:], NEG_SLOPE, a4[:], ALU.mult, ALU.max))
            c.settle()
            c.did(nc.vector.tensor_tensor(a4[:], a4[:], r8[:, :, HEADS:], ALU.subtract))
            c.settle()
            nc.vector.tensor_scalar(a4[:], a4[:], 0.0, None, ALU.min).then_inc(arg_ready, 1)


def stage_aggregate(nc, K):
    U = 5
    n_turns = STEPS // U
    assert STEPS % U == 0
    with Scope(nc, "aggregate") as s:
        meta = s.sb("meta_s", [128, U, 4, 6])
        g = s.sb("g", [128, U, 4, ROW])
        local = s.sb("local", [128, U, 4])
        pick = s.sb("pick", [128, U, 4, P])
        ps = s.ps("ps_agg", [128, U, 512])
        self_in = s.sem("self_in")
        self_done = s.sem("self_done")
        meta_in = s.sems("meta_in", U)
        g_in = s.sems("g_in", U)
        local_ready = s.sem("local_ready")
        pick_ready = s.sem("pick_ready")
        msg_ready = s.sem("msg_ready")
        agg_ready = s.sem("agg_ready")
        added = s.sem("added")
        block = s.block()
        groups = K.meta_d.rearrange("(g p i) r -> g p (i r)", p=128, i=4)

        @block.sync
        def _(sp):
            hk = K.h_d.rearrange("(t p) f -> p t f", p=P)
            rows_split(sp, K.acc[:, :, 0:H], hk, self_in)

            def body(it, first):
                for u in range(U):
                    i = it * U + u
                    t = sp.value_load(K.step_group[0:1, bass.ds(i, 1)], min_val=0, max_val=EDGE_GROUPS - 1)
                    if not first:
                        sp.wait_ge(agg_ready, i - U + 1)
                    sp.dma_start(meta[:, u].rearrange("p i r -> p (i r)"), one(groups, t)).then_inc(meta_in[u], 16)

            turns(sp, n_turns, body)

        @block.gpsimd
        def _(pool):
            def body(it, first):
                for u in range(U):
                    pool.wait_ge(meta_in[u], it * 16 + 16)
                    pool_gate(nc, K)
                    if not first:
                        pool.wait_ge(agg_ready, it * U + u - U + 1)
                        pool_gate(nc, K)
                    for i in range(4):
                        nc.gpsimd.indirect_dma_start(
                            out=g[:, u, i, 0:H], out_offset=None, in_=K.h_d,
                            in_offset=bass.IndirectOffsetOnAxis(ap=meta[:, u, i, 5:6].bitcast(I32), axis=0),
                        ).then_inc(g_in[u], 16)

            turns(pool, n_turns, body)

        @block.vector
        def _(dve):
            dve.wait_ge(self_in, 32)
            for t in range(0, TILES, 20):
                a = K.acc[:, t:t + 20, :]
                for h in range(HEADS):
                    nc.vector.tensor_tensor(a[:, :, h * OUT:(h + 1) * OUT], a[:, :, h * OUT:(h + 1) * OUT],
                                            K.exs[:, t:t + 20, h:h + 1].to_broadcast([P, 20, OUT]), ALU.mult).then_inc(self_done, 1)
                nc.vector.tensor_copy(a[:, :, H:ROW], K.exs[:, t:t + 20, :]).then_inc(self_done, 1)
            dve.wait_ge(self_done, 5 * (HEADS + 1))

            def add(i, u):
                b = dve.value_load(K.step_tile[0:1, bass.ds(i, 1)], min_val=0, max_val=TILES - 1)
                dve.wait_ge(agg_ready, i + 1)
                if not isinstance(i, int) or i:
                    dve.wait_ge(added, i)
                a = K.acc[:, bass.ds(b, 1), :].rearrange("p a f -> p (a f)")
                nc.vector.tensor_tensor(a, a, ps[0:P, u, 0:ROW], ALU.add).then_inc(added, 1)

            def body(it, first):
                for u in range(U):
                    i = it * U + u
                    dve.wait_ge(meta_in[u], it * 16 + 16)
                    if not first:
                        dve.wait_ge(agg_ready, i - U + 1)
                    nc.vector.tensor_scalar(local[:, u, :], meta[:, u, :, 4], K.step_node[:, bass.ds(i, 1)], None,
                                            ALU.subtract).then_inc(local_ready, 1)
                    dve.wait_ge(local_ready, i + 1)
                    for k in range(4):
                        nc.vector.tensor_scalar(pick[:, u, k, :], K.iota_col[:, 0:P], local[:, u, k:k + 1], None,
                                                ALU.is_equal).then_inc(pick_ready, 1)
                    dve.wait_ge(g_in[u], it * 64 + 64)
                    for k in range(4):
                        v = g[:, u, k, 0:H].rearrange("p (h o) -> p h o", h=HEADS)
                        nc.vector.tensor_tensor(v, v, meta[:, u, k, 0:HEADS].rearrange("p (h o) -> p h o", o=1)
                                                .to_broadcast([128, HEADS, OUT]), ALU.mult).then_inc(msg_ready, 1)
                    nc.vector.tensor_copy(g[:, u, :, H:ROW], meta[:, u, :, 0:HEADS]).then_inc(msg_ready, 1)
                    if not (first and u == 0):
                        add(i - 1, (u - 1) % U)

            turns(dve, n_turns, body)
            add(STEPS - 1, U - 1)

        @block.tensor
        def _(pe):
            def body(it, first):
                for u in range(U):
                    i = it * U + u
                    pe.wait_ge(pick_ready, i * 4 + 4)
                    pe.wait_ge(msg_ready, i * 5 + 5)
                    if not first:
                        pe.wait_ge(added, i - U + 1)
                    for k in range(4):
                        mm = nc.tensor.matmul(ps[0:P, u, 0:ROW], pick[:, u, k, :], g[:, u, k, :], start=(k == 0), stop=(k == 3))
                    mm.then_inc(agg_ready, 1)

            turns(pe, n_turns, body)


def stage_tokens(nc, K, A):
    U = UNROLL
    with Scope(nc, "tokens") as s:
        bias = s.sb("bias_b", [P, 3, H])
        xin = s.sb("xin", [P, 3, 3, GT, H])
        y = s.sb("y_t", [P, GT, H])
        base = s.sb("base", [P, 2, GT, H])
        x1 = s.sb("x1", [P, 2, GT, H])
        rden = s.sb("rden", [P, GT, HEADS])
        gw = s.sb("gw", [128, HC, EXPERTS])
        gb = s.sb("gb", [P, EXPERTS])
        tokt = s.sb("tokt", [128, HC, GN])
        stats = s.sb("stats3", [P, GT, 6])
        mv = s.sb("mv3", [P, GT, 3])
        var = s.sb("var3", [P, GT])
        std = s.sb("std3", [P, GT])
        rstd = s.sb("rstd3", [P, GT])
        ps = s.ps("ps_tok", [128, 3, 512])
        w_in = s.sem("w_in3")
        x_in = s.sems("x_in3", 3)
        var_ready, std_ready = s.sem("var_ready3"), s.sem("std_ready3")
        base_half, base_ready, x1_ready, tok_ready = (s.sem(n) for n in ("base_half", "base_ready", "x1_ready", "tok_ready"))
        x1_out = s.sems("x1_out", 2)
        tok_psum, tokt_ready, log_psum, log_ready = (s.sem(n) for n in ("tok_psum", "tokt_ready", "log_psum", "log_ready"))
        dve_done = s.sem("dve_done4")
        block = s.block()
        grp = lambda a: a.rearrange("(g t p) f -> g p t f", p=P, t=GT)
        row = lambda a, n: a.rearrange("(a n) -> a n", a=1).to_broadcast([P, n])
        bcast = lambda a: a.rearrange("p (t f) -> p t f", t=1).to_broadcast([P, GT, H])

        @block.sync
        def _(sp):
            for k, a in enumerate((A.bias, A.gamma, A.beta)):
                sp.dma_start(bias[:, k, :], row(a, H)).then_inc(w_in, 16)
            sp.dma_start(gb[:, :], row(A.ffn_gate_b, EXPERTS)).then_inc(w_in, 16)
            sp.dma_start(gw[:], A.ffn_gate_w.rearrange("(c p) e -> p c e", p=128)).then_inc(w_in, 16)

            def load(g):
                for k, a in enumerate((K.xn_d, A.x, K.mix_d)):
                    rows_split(sp, xin[:, g % 3, k], grp(a)[g], x_in[g % 3])

            for g in range(3):
                load(g)
            for g in range(GROUPS):
                sp.wait_ge(x1_ready, g + 1)
                rows_split(sp, grp(K.x1_d)[g], x1[:, g % 2], x1_out[g % 2])
                if g + 3 < GROUPS:
                    load(g + 3)
            for b in range(2):
                sp.wait_ge(x1_out[b], 32 * ((GROUPS + 1 - b) // 2))

        @block.gpsimd
        def _(pool):
            pool.wait_ge(w_in, 80)
            for g in range(GROUPS):
                pool.wait_ge(x_in[g % 3], 96 * (g // 3 + 1))
                if g >= 2:
                    pool.wait_ge(x1_ready, g - 1)
                nc.gpsimd.tensor_tensor(base[:, g % 2], xin[:, g % 3, 1], xin[:, g % 3, 2], ALU.add).then_inc(base_half, 1)
                pool.wait_ge(base_half, g + 1)
                nc.gpsimd.tensor_tensor(base[:, g % 2], base[:, g % 2], bcast(bias[:, 2, :]), ALU.add).then_inc(base_ready, 1)

        @block.vector
        def _(dve):
            c = Chain(dve, dve_done)
            dve.wait_ge(w_in, 80)

            def logits(g):
                dve.wait_ge(log_psum, g + 1)
                nc.vector.tensor_tensor(K.logits[:, g * GT:(g + 1) * GT, :],
                                        ps[0:P, 2, 0:GT * EXPERTS].rearrange("p (t e) -> p t e", e=EXPERTS),
                                        gb[:].rearrange("p (a e) -> p a e", a=1).to_broadcast([P, GT, EXPERTS]),
                                        ALU.add).then_inc(log_ready, 1)

            for g in range(GROUPS):
                acc = K.acc[:, g * GT:(g + 1) * GT, :]
                c.did(nc.vector.reciprocal(rden[:], acc[:, :, H:ROW]))
                c.settle()
                for t in range(GT):
                    c.did(nc.vector.tensor_tensor(y[:, t, :].rearrange("p (h o) -> p h o", h=HEADS),
                                                  acc[:, t, 0:H].rearrange("p (h o) -> p h o", h=HEADS),
                                                  rden[:, t, :].rearrange("p (h o) -> p h o", o=1).to_broadcast([P, HEADS, OUT]),
                                                  ALU.mult))
                c.settle()
                c.did(nc.vector.tensor_tensor(y[:], y[:], bcast(bias[:, 0, :]), ALU.add))
                c.settle()
                dve.wait_ge(x_in[g % 3], 96 * (g // 3 + 1))
                c.did(nc.vector.scalar_tensor_tensor(y[:], y[:], 0.0, xin[:, g % 3, 0], ALU.max, ALU.add))
                c.settle()
                norm_stats(nc, c, y, stats, mv, var).then_inc(var_ready, 1)
                dve.wait_ge(std_ready, 2 * g + 1)
                for ins in norm_rows(nc, c, y, y, mv, std, rstd):
                    c.did(ins)
                c.settle()
                c.did(nc.vector.tensor_tensor(y[:], y[:], bcast(bias[:, 1, :]), ALU.mult))
                c.settle()
                dve.wait_ge(base_ready, g + 1)
                if g >= 2:
                    dve.wait_ge(x1_out[g % 2], 32 * (g // 2))
                nc.vector.tensor_tensor(x1[:, g % 2], y[:], base[:, g % 2], ALU.add).then_inc(x1_ready, 1)
                dve.wait_ge(x1_ready, g + 1)
                norm_stats(nc, c, x1[:, g % 2], stats, mv, var).then_inc(var_ready, 1)
                if g:
                    logits(g - 1)
                dve.wait_ge(std_ready, 2 * g + 2)
                for ins in norm_rows(nc, c, x1[:, g % 2], acc[:, :, 0:H], mv, std, rstd):
                    ins.then_inc(tok_ready, 1)
            logits(GROUPS - 1)

        @block.scalar
        def _(act):
            for g in range(GROUPS):
                for k in range(2):
                    act.wait_ge(var_ready, 2 * g + k + 1)
                    nc.scalar.activation(std[:, :], var[:, :], ACT.Sqrt).then_inc(std_ready, 1)
                act.wait_ge(tok_psum, g + 1)
                if g:
                    act.wait_ge(log_psum, g)
                nc.scalar.activation(tokt[:], ps[:, 0:2, 0:GN], ACT.Copy).then_inc(tokt_ready, 1)

        @block.tensor
        def _(pe):
            pe.wait_ge(w_in, 80)
            for g in range(GROUPS):
                pe.wait_ge(tok_ready, GT * (g + 1))
                if g:
                    pe.wait_ge(tokt_ready, g)
                for t in range(GT):
                    for k in range(HC):
                        mm = nc.tensor.transpose(ps[:, k, t * P:(t + 1) * P], K.acc[:, g * GT + t, k * 128:(k + 1) * 128],
                                                 K.ident[0:P, 0:P])
                mm.then_inc(tok_psum, 1)
                pe.wait_ge(tokt_ready, g + 1)
                if g:
                    pe.wait_ge(log_ready, g)
                for t in range(GT):
                    for k in range(HC):
                        mm = nc.tensor.matmul(ps[0:P, 2, t * EXPERTS:(t + 1) * EXPERTS], tokt[:, k, t * P:(t + 1) * P],
                                              gw[:, k, :], start=(k == 0), stop=(k == HC - 1))
                mm.then_inc(log_psum, 1)


def stage_route(nc, K):
    with Scope(nc, "route") as s:
        e = s.sb("e_r", [P, TILES, EXPERTS])
        one_hot = s.sb("one_hot", [P, TILES, EXPERTS])
        pos = s.sb("pos", [P, TILES, EXPERTS])
        tot = s.sb("tot", [P, TILES, EXPERTS])
        run = s.sb("run_r", [P, TILES, EXPERTS])
        top = s.sb("top", [P, TILES])
        tsum = s.sb("tsum", [P, TILES])
        inv = s.sb("inv", [P, TILES])
        best = s.sb("best", [P, TILES])
        slot = s.sb("slot", [P, TILES])
        kept = s.sb("kept", [P, TILES])
        rank = s.sb("rank", [P, EXPERTS])
        begin = s.sb("begin", [P, EXPERTS])
        ones = s.sb("ones_r", [P, P])
        ones_t = s.sb("ones_rt", [P, TILES])
        upto = s.sb("upto", [P, P])
        ps = s.ps("ps_route", [128, 4, 512])
        made = s.sem("made_r")
        arg_ready, e_ready, hot_ready, counted, slot_ready, tok_out = (s.sem(n) for n in (
            "arg_ready_r", "e_ready_r", "hot_ready", "counted_r", "slot_ready", "tok_out"))
        done = s.sem("dve_done5")
        block = s.block()
        per = lambda a: a.rearrange("p (t e) -> p t e", e=1).to_broadcast([P, TILES, EXPERTS])
        along = lambda a: a.rearrange("p (t e) -> p t e", t=1).to_broadcast([P, TILES, EXPERTS])

        @block.gpsimd
        def _(pool):
            nc.gpsimd.iota(rank[:], pattern=[[-1, EXPERTS]], base=EXPERTS, channel_multiplier=0,
                           allow_small_or_imprecise_dtypes=True).then_inc(made, 1)
            nc.gpsimd.iota(begin[:], pattern=[[CAP, EXPERTS]], base=-1, channel_multiplier=0,
                           allow_small_or_imprecise_dtypes=True).then_inc(made, 1)
            nc.gpsimd.memset(ones[:], 1.0).then_inc(made, 1)
            pool.wait_ge(made, 3)
            nc.gpsimd.affine_select(out=upto[:], in_=ones[:], compare_op=ALU.is_ge, fill=0.0, base=0,
                                    pattern=[[1, P]], channel_multiplier=-1).then_inc(made, 1)
            pool.wait_ge(slot_ready, 2)
            for t in range(TILES):
                nc.gpsimd.indirect_dma_start(
                    out=K.buf_d, out_offset=bass.IndirectOffsetOnAxis(ap=K.slot_i[:, t:t + 1], axis=0),
                    in_=K.acc[:, t, 0:TOKW], in_offset=None, bounds_check=SLOTS - 1, oob_is_err=False).then_inc(tok_out, 16)
            pool.wait_ge(tok_out, 16 * TILES)

        @block.scalar
        def _(act):
            act.wait_ge(arg_ready, 1)
            nc.scalar.activation(e[:], e[:], ACT.Exp).then_inc(e_ready, 1)

        @block.tensor
        def _(pe):
            pe.wait_ge(hot_ready, 1)
            flat = one_hot[:].rearrange("p t e -> p (t e)")
            half = TILES * EXPERTS // 2
            for k in range(2):
                nc.tensor.matmul(ps[0:P, k, 0:half], upto[:], flat[:, k * half:(k + 1) * half], start=True, stop=True)
                mm = nc.tensor.matmul(ps[0:P, 2 + k, 0:half], ones[:], flat[:, k * half:(k + 1) * half], start=True, stop=True)
            mm.then_inc(counted, 1)

        @block.vector
        def _(dve):
            c = Chain(dve, done)

            def step(ins):
                c.did(ins)
                c.settle()

            v = nc.vector
            c.did(v.memset(ones_t[:], 1.0))
            step(v.tensor_reduce(top[:], K.logits[:], X, ALU.max))
            v.tensor_tensor(e[:], K.logits[:], per(top[:]), ALU.subtract).then_inc(arg_ready, 1)
            dve.wait_ge(e_ready, 1)
            c.did(v.tensor_reduce(tsum[:], e[:], X, ALU.add))
            step(v.tensor_reduce(best[:], e[:], X, ALU.max))
            c.did(v.reciprocal(inv[:], tsum[:]))
            dve.wait_ge(made, 4)
            step(v.tensor_tensor(one_hot[:], e[:], per(best[:]), ALU.is_equal))
            step(v.tensor_tensor(one_hot[:], one_hot[:], along(rank[:]), ALU.mult))
            step(v.tensor_reduce(top[:], one_hot[:], X, ALU.max))
            c.did(v.tensor_tensor(best[:], best[:], inv[:], ALU.mult))
            v.tensor_tensor(one_hot[:], one_hot[:], per(top[:]), ALU.is_equal).then_inc(hot_ready, 1)
            c.settle()
            c.did(v.tensor_copy(K.acc[:, :, H:TOKW], best[:].rearrange("p (t e) -> p t e", e=1)))
            dve.wait_ge(counted, 1)
            halves = lambda a: a[:].rearrange("p (k t) e -> p k (t e)", k=2)
            c.did(v.tensor_copy(halves(pos), ps[0:P, 0:2, 0:TILES * EXPERTS // 2]))
            step(v.tensor_copy(halves(tot), ps[0:P, 2:4, 0:TILES * EXPERTS // 2]))
            for x in range(EXPERTS):
                c.did(v.tensor_tensor_scan(run[:, :, x], ones_t[:], tot[:, :, x], 0.0, ALU.mult, ALU.add))
            c.settle()
            step(v.tensor_tensor(run[:], run[:], tot[:], ALU.subtract))
            step(v.tensor_tensor(pos[:], pos[:], run[:], ALU.add))
            step(v.tensor_tensor(tot[:], pos[:], one_hot[:], ALU.mult))
            step(v.tensor_reduce(kept[:], tot[:], X, ALU.add))
            step(v.tensor_scalar(kept[:], kept[:], float(C_MAX), None, ALU.is_le))
            step(v.tensor_tensor(pos[:], pos[:], along(begin[:]), ALU.add))
            step(v.tensor_tensor(pos[:], pos[:], one_hot[:], ALU.mult))
            step(v.tensor_reduce(slot[:], pos[:], X, ALU.add))
            step(v.scalar_tensor_tensor(slot[:], slot[:], float(SLOTS), kept[:], ALU.subtract, ALU.mult))
            step(v.tensor_scalar(slot[:], slot[:], float(SLOTS), None, ALU.add))
            v.tensor_copy(K.slot_i[:], slot[:]).then_inc(slot_ready, 2)


def stage_experts(nc, K, A):
    FC = F // 128
    ring = 3
    per = 2 * CHUNKS
    n_turns = EXPERTS // 2
    with Scope(nc, "experts") as s:
        w1 = s.sb("w1", [128, 2, HC, F])
        w2 = s.sb("w2", [128, 2, FC, H])
        b1 = s.sb("b1", [128, 2, FC])
        b2 = s.sb("b2", [128, 2, H])
        rows = s.sb("rows_e", [128, per, 4, TOKW])
        bt = s.sb("bt", [128, 2, HC, 512])
        hm = s.sb("hm", [128, FC, 512])
        y = s.sb("y_e", [128, 2, 4, H])
        bad = s.sb("bad", [128, 4, H], I32)
        const = s.sb("const", [128, 3, 4, H])
        scrap = s.sb("scrap", [128, 2])
        ps = s.ps("ps_e", [128, 8, 512])
        w_in = s.sems("w_in4", 2)
        const_ready = s.sem("const_ready")
        rows_in = s.sems("rows_in4", per)
        bt_psum, bt_ready, h_psum, h_ready, y_psum, y_made, y_ready = (s.sem(n) for n in (
            "bt_psum", "bt_ready", "h_psum", "hm_ready", "y_psum", "y_made", "y_ready"))
        y_out = s.sems("y_out", 2)
        done = s.sem("dve_done6")
        block = s.block()
        bufc = K.buf_d.rearrange("(n t p) r -> n p t r", t=4, p=128)
        yc = K.y_d[0:SLOTS, :].rearrange("(n t p) r -> n p t r", t=4, p=128)

        @block.sync
        def _(sp):
            def weights(x, i):
                w1v = A.ffn_w1.rearrange("e (c p) f -> e p c f", p=128)
                w2v = A.ffn_w2.rearrange("e (c p) f -> e p c f", p=128)
                sp.dma_start(w1[:, i], one(w1v, x)).then_inc(w_in[i], 16)
                sp.dma_start(w2[:, i], one(w2v, x)).then_inc(w_in[i], 16)
                sp.dma_start(b2[:, i, :], A.ffn_b2[bass.ds(x, 1), :].to_broadcast([128, H])).then_inc(w_in[i], 16)
                with nc.allow_non_contiguous_dma(reason="b1 to columns"):
                    sp.dma_start(b1[:, i, :], one(A.ffn_b1.rearrange("e (f p) -> e p f", p=128), x)).then_inc(w_in[i], 16)

            weights(0, 0)
            for u in range(per):
                sp.dma_start(rows[:, u], bufc[u]).then_inc(rows_in[u], 16)
                if u == 0:
                    weights(1, 1)

            def body(it, more):
                for u in range(per):
                    j = it * per + u
                    sp.wait_ge(y_ready, j + 1)
                    sp.dma_start(one(yc, j), y[:, u % 2]).then_inc(y_out[u % 2], 16)
                    if more:
                        sp.dma_start(rows[:, u], one(bufc, j + per)).then_inc(rows_in[u], 16)
                        if u % CHUNKS == CHUNKS - 1:
                            weights(it * 2 + u // CHUNKS + 2, u // CHUNKS)

            with sp.Fori(0, n_turns - 1) as it:
                body(it, True)
            body(n_turns - 1, False)
            for b in range(2):
                sp.wait_ge(y_out[b], 16 * n_turns * CHUNKS)

        @block.tensor
        def _(pe):
            def turn_rows(it, u, first):
                pe.wait_ge(rows_in[u], it * 16 + 16)
                if not (first and u == 0):
                    pe.wait_ge(bt_ready, it * per + u)
                for t in range(4):
                    for k in range(HC):
                        mm = nc.tensor.transpose(ps[:, k, t * 128:(t + 1) * 128], rows[:, u, t, k * 128:(k + 1) * 128], K.ident[:])
                mm.then_inc(bt_psum, 1)

            def body(it, first):
                turn_rows(it, 0, first)
                for u in range(per):
                    j = it * per + u
                    x = u // CHUNKS
                    if u % CHUNKS == 0:
                        pe.wait_ge(w_in[x], it * 64 + 64)
                    pe.wait_ge(bt_ready, j + 1)
                    for f in range(FC):
                        i = j * FC + f
                        if not (first and i < 4):
                            pe.wait_ge(h_ready, i - 3)
                        for k in range(HC):
                            mm = nc.tensor.matmul(ps[:, 2 + f % 4, :], w1[:, x, k, f * 128:(f + 1) * 128], bt[:, u % 2, k, :],
                                                  start=(k == 0), stop=(k == HC - 1))
                        mm.then_inc(h_psum, 1)
                    if u < per - 1:
                        turn_rows(it, u + 1, first)
                    pe.wait_ge(h_ready, j * FC + FC)
                    if not (first and u == 0):
                        pe.wait_ge(y_made, j)
                    for t in range(4):
                        for f in range(FC):
                            mm = nc.tensor.matmul(ps[:, 6 + t // 2, (t % 2) * H:(t % 2 + 1) * H], hm[:, f, t * 128:(t + 1) * 128],
                                                  w2[:, x, f, :], start=(f == 0), stop=(f == FC - 1))
                    mm.then_inc(y_psum, 1)

            turns(pe, n_turns, body)

        @block.scalar
        def _(act):
            def body(it, first):
                for u in range(per):
                    j = it * per + u
                    for f in range(FC):
                        i = j * FC + f
                        act.wait_ge(h_psum, i + 1)
                        if f == 0 and not (first and u == 0):
                            act.wait_ge(y_psum, j)
                        if f == 0 and u % CHUNKS == 0:
                            act.wait_ge(w_in[u // CHUNKS], it * 64 + 64)
                        nc.scalar.activation(hm[:, f, :], ps[:, 2 + f % 4, :], ACT.Relu,
                                             bias=b1[:, u // CHUNKS, f:f + 1]).then_inc(h_ready, 1)

            turns(act, n_turns, body)

        @block.vector
        def _(dve):
            for k, x in enumerate((0.0, 1e4, -1e4)):
                nc.vector.memset(const[:, k], x).then_inc(const_ready, 1)
            nc.vector.memset(scrap[:], 0.0).then_inc(const_ready, 1)
            dve.wait_ge(const_ready, 4)

            def turn_copy(it, u, first):
                j = it * per + u
                dve.wait_ge(bt_psum, j + 1)
                nc.vector.tensor_copy(bt[:, u % 2], ps[:, 0:2, :]).then_inc(bt_ready, 1)

            def body(it, first):
                c = Chain(dve, done, per * 12, it)

                def carry_wait():
                    c.settle()
                    c.did(nc.vector.tensor_copy(scrap[:, 0:1], scrap[:, 1:2]))

                turn_copy(it, 0, first)
                for u in range(per):
                    j = it * per + u
                    if u < per - 1:
                        turn_copy(it, u + 1, first)
                    dve.wait_ge(y_psum, j + 1)
                    if u % CHUNKS == 0:
                        dve.wait_ge(w_in[u // CHUNKS], it * 64 + 64)
                    if not (first and u < 2):
                        dve.wait_ge(y_out[u % 2], it * (16 * CHUNKS) + u // 2 * 16)
                    yu = y[:, u % 2]
                    nc.vector.tensor_tensor(yu.rearrange("p (a b) f -> p a b f", a=2),
                                            ps[:, 6:8, :].rearrange("p a (b f) -> p a b f", b=2),
                                            b2[:, u // CHUNKS, :].rearrange("p (a b f) -> p a b f", a=1, b=1).to_broadcast([128, 2, 2, H]),
                                            ALU.add).then_inc(y_made, 1)
                    dve.wait_ge(y_made, j + 1)
                    for t in range(4):
                        c.did(nc.vector.tensor_scalar(yu[:, t, :], yu[:, t, :], rows[:, u, t, H:TOKW], None, ALU.mult))
                    c.settle()
                    c.did(nc.vector.tensor_tensor(bad[:], yu, yu, ALU.not_equal))
                    carry_wait()
                    c.did(nc.vector.copy_predicated(yu, bad[:], const[:, 0]))
                    c.settle()
                    c.did(nc.vector.tensor_scalar(bad[:], yu, FLT_MAX, None, ALU.is_gt))
                    carry_wait()
                    c.did(nc.vector.copy_predicated(yu, bad[:], const[:, 1]))
                    c.settle()
                    c.did(nc.vector.tensor_scalar(bad[:], yu, -FLT_MAX, None, ALU.is_lt))
                    carry_wait()
                    nc.vector.copy_predicated(yu, bad[:], const[:, 2]).then_inc(y_ready, 1)
                c.close()

            turns(dve, n_turns, body)


def stage_output(nc, K, A):
    U = UNROLL
    with Scope(nc, "output") as s:
        x1 = s.sb("x1_o", [P, U, GT, H])
        y = s.sb("y_o", [P, U, GT, H])
        x_in = s.sems("x_in5", U)
        y_in = s.sems("y_in5", U)
        o_ready = s.sem("o_ready")
        o_out = s.sems("o_out", U)
        block = s.block()
        grp = lambda a: a.rearrange("(g t p) f -> g p t f", p=P, t=GT)

        @block.sync
        def _(sp):
            for g in range(U):
                rows_split(sp, x1[:, g], grp(K.x1_d)[g], x_in[g])
            for g in range(GROUPS):
                sp.wait_ge(o_ready, g + 1)
                rows_split(sp, grp(A.out)[g], x1[:, g % U], o_out[g % U])
                if g + U < GROUPS:
                    sp.wait_ge(o_out[g % U], 32 * (g // U + 1))
                    rows_split(sp, x1[:, g % U], grp(K.x1_d)[g + U], x_in[g % U])
            for u in range(U):
                sp.wait_ge(o_out[u], 32 * TURNS)

        @block.gpsimd
        def _(pool):
            for g in range(GROUPS):
                if g >= U:
                    pool.wait_ge(o_ready, g - U + 1)
                for t in range(GT):
                    i = g * GT + t
                    nc.gpsimd.indirect_dma_start(
                        out=y[:, g % U, t, :], out_offset=None, in_=K.y_d,
                        in_offset=bass.IndirectOffsetOnAxis(ap=K.slot_i[:, i:i + 1], axis=0)).then_inc(y_in[g % U], 16)

        @block.vector
        def _(dve):
            for g in range(GROUPS):
                dve.wait_ge(x_in[g % U], 32 * (g // U + 1))
                dve.wait_ge(y_in[g % U], 64 * (g // U + 1))
                nc.vector.tensor_tensor(x1[:, g % U], x1[:, g % U], y[:, g % U], ALU.add).then_inc(o_ready, 1)


class Shared:
    pass


class Arguments:

    def __init__(self, aps, out):
        self.x = aps["x"]
        self.src = aps["src"]
        self.dst = aps["dst"]
        self.W = aps["L0_gnn_W"]
        self.att_src = aps["L0_gnn_att_src"]
        self.att_dst = aps["L0_gnn_att_dst"]
        self.bias = aps["L0_gnn_bias"]
        self.gamma = aps["L0_gnn_gamma"]
        self.beta = aps["L0_gnn_beta"]
        self.mix_Wqkv = aps["L0_mix_Wqkv"]
        self.mix_Wproj = aps["L0_mix_Wproj"]
        self.mix_bproj = aps["L0_mix_bproj"]
        self.mix_ln_g = aps["L0_mix_ln_g"]
        self.mix_ln_b = aps["L0_mix_ln_b"]
        self.mix_Wg1 = aps["L0_mix_Wg1"]
        self.mix_bg1 = aps["L0_mix_bg1"]
        self.mix_Wg2 = aps["L0_mix_Wg2"]
        self.mix_bg2 = aps["L0_mix_bg2"]
        self.ffn_gate_w = aps["L0_ffn_gate_w"]
        self.ffn_gate_b = aps["L0_ffn_gate_b"]
        self.ffn_w1 = aps["L0_ffn_w1"]
        self.ffn_b1 = aps["L0_ffn_b1"]
        self.ffn_w2 = aps["L0_ffn_w2"]
        self.ffn_b2 = aps["L0_ffn_b2"]
        self.out = out


def gps_layer(nc, A, kind="Internal"):
    K = Shared()
    made = {}

    def dram(name, shape, dt=F32):
        made[name] = nc.dram_tensor(name, shape, dt, kind=kind).ap()
        return made[name]

    K.xn_d = dram("xn_d", [N, H])
    K.xt_d = dram("xt_d", [GROUPS, 128, HC * GN])
    K.h_d = dram("h_d", [N, H])
    K.dst_d = dram("dst_d", [DST_ROWS * FAN], I32)
    K.src_d = dram("src_d", [EP], I32)
    K.top_d = dram("top_d", [PIVOTS, FAN], I32)
    K.rp_d = dram("rp_d", [N + 1])
    K.a_d = dram("a_d", [N, HEADS])
    K.as_d = dram("as_d", [EP, HEADS])
    K.gt_d = dram("gt_d", [GROUPS, 128, HC * GN])
    K.mix_d = dram("mix_d", [N, H])
    K.rec_d = dram("rec_d", [EP, 2 * HEADS])
    K.mx_d = dram("mx_d", [EP, HEADS])
    K.meta_d = dram("meta_d", [EP, 6])
    K.x1_d = dram("x1_d", [N, H])
    K.buf_d = dram("buf_d", [SLOTS, TOKW])
    K.y_d = dram("y_d", [SLOTS + 1, H])
    with Scope(nc, "gps_layer") as s:
        K.ident = s.sb("ident", [128, 128])
        K.iota_col = s.sb("iota_col", [128, 512])
        K.gate = s.sem("gate")
        K.node_id = s.sb("node_id", [P, TILES])
        K.asd = s.sb("asd", [P, TILES, 2 * HEADS])
        K.rend = s.sb("rend", [P, TILES])
        K.rstart = s.sb("rstart", [P, TILES])
        K.step_node = s.sb("step_node", [128, STEPS])
        K.step_tile = s.sb("step_tile", [1, STEPS], I32)
        K.step_group = s.sb("step_group", [1, STEPS], I32)
        K.exs = s.sb("exs", [P, TILES, HEADS])
        constants(nc, K)
        stage_embed(nc, K, A)
        stage_steps(nc, K)
        zero_fill(nc, K)
        stage_mix(nc, K, A)
        stage_alpha(nc, K)
        K.slot_i = s.sb("slot_i", [P, TILES], I32)
        with Scope(nc, "gps_layer") as t:
            K.acc = t.sb("acc", [P, TILES, ROW])
            K.logits = t.sb("logits", [P, TILES, EXPERTS])
            stage_aggregate(nc, K)
            stage_tokens(nc, K, A)
            stage_route(nc, K)
        stage_experts(nc, K, A)
        stage_output(nc, K, A)


_INS = ["x", "src", "dst", "L0_gnn_W", "L0_gnn_att_src", "L0_gnn_att_dst", "L0_gnn_bias", "L0_gnn_gamma",
        "L0_gnn_beta", "L0_mix_Wqkv", "L0_mix_Wproj", "L0_mix_bproj", "L0_mix_ln_g", "L0_mix_ln_b",
        "L0_mix_Wg1", "L0_mix_bg1", "L0_mix_Wg2", "L0_mix_bg2", "L0_ffn_gate_w", "L0_ffn_gate_b",
        "L0_ffn_w1", "L0_ffn_b1", "L0_ffn_w2", "L0_ffn_b2"]


def kernel(**inputs):
    import concourse.bacc as bacc
    from concourse.bass_utils import run_bass_kernel_spmd

    nc = bacc.Bacc("TRN2", target_bir_lowering=False, num_devices=1)
    arrays, aps = {}, {}
    for name in _INS:
        a = np.ascontiguousarray(inputs[name])
        arrays[f"in_{name}"] = a
        aps[name] = nc.dram_tensor(f"in_{name}", a.shape, mybir.dt.from_np(a.dtype), kind="ExternalInput").ap()
    out = nc.dram_tensor("out", [N, H], F32, kind="ExternalOutput").ap()
    A = Arguments(aps, out)
    gps_layer(nc, A)
    r = run_bass_kernel_spmd(nc, [arrays], core_ids=[0])
    return r.results[0]["out"]
```

```python
from contextlib import ExitStack

import numpy as np

import concourse.bass as bass
from concourse import mybir

F32 = mybir.dt.float32
BF16 = mybir.dt.bfloat16
I32 = mybir.dt.int32
ALU = mybir.AluOpType
ACT = mybir.ActivationFunctionType
X = mybir.AxisListType.X

N, H, E = 12500, 256, 200000
HEADS, OUT = 4, 64
NEG_SLOPE, EPS = 0.2, 1e-5

P = 125
TILES = N // P
GT = 4
GROUPS = TILES // GT
GN = GT * P
UNROLL = 5
TURNS = GROUPS // UNROLL
HC = H // 128
HW = H + 2 * HEADS
ROW = H + HEADS


def rows_split(eng, out, in_, sem):
    eng.dma_start(out[0:112], in_[0:112]).then_inc(sem, 16)
    eng.dma_start(out[112:P], in_[112:P]).then_inc(sem, 16)


EG = 512
EDGE_GROUPS = -(-E // EG)
EP = EDGE_GROUPS * EG
EC = EP // 128
NO_NODE = 16383
FAN = 64
DST_ROWS = -(-EP // (FAN * FAN)) * FAN
PIVOTS = DST_ROWS // FAN
CHUNK = TILES // TURNS
STEPS = EDGE_GROUPS + TILES - 1
STEP_BATCH = 5
BATCHES = STEPS // STEP_BATCH
META = HEADS + 3
NEVER = -1e30

EXPERTS, F = 8, 1024
C_MAX = -(-5 * N // (4 * EXPERTS))
CAP = -(-C_MAX // 512) * 512
SLOTS = EXPERTS * CAP
CHUNKS = CAP // 512
TOKW = H + 1
FLT_MAX = float(np.finfo(np.float32).max)


def pool_gate(nc, K):
    nc.gpsimd.sem_inc(K.gate, 1)


class Chain:

    def __init__(self, eng, sem, per=0, turn=0):
        self.eng, self.sem, self.per, self.turn, self.n = eng, sem, per, turn, 0

    def did(self, ins):
        ins.then_inc(self.sem, 1)
        self.n += 1
        return self.n

    def value(self, n):
        return self.turn * self.per + n if self.per else n

    def settle(self, n=None):
        self.eng.wait_ge(self.sem, self.value(self.n if n is None else n))

    def close(self):
        assert self.n == self.per, (self.n, self.per)


class Scope:

    def __init__(self, nc, stage):
        self.nc, self.stage, self.ctx, self.held = nc, stage, ExitStack(), []

    def __enter__(self):
        return self

    def __exit__(self, *a):
        self.ctx.__exit__(*a)
        if self.held and a[0] is None:
            self.nc.clear_and_free_semaphores(self.held)
            self.nc.all_engine_barrier()

    def sb(self, name, shape, dt=F32):
        return self.ctx.enter_context(self.nc.sbuf_tensor(f"{self.stage}_{name}", shape, dt))

    def ps(self, name, shape, dt=F32):
        return self.ctx.enter_context(self.nc.psum_tensor(f"{self.stage}_{name}", shape, dt))

    def sem(self, name):
        self.held.append(self.nc.alloc_semaphore(f"{self.stage}_{name}"))
        return self.held[-1]

    def sems(self, name, n):
        return [self.sem(f"{name}{i}") for i in range(n)]

    def block(self):
        return self.ctx.enter_context(self.nc.Block())


def constants(nc, K):
    with Scope(nc, "constants") as s:
        made = s.sem("made")
        block = s.block()

        @block.gpsimd
        def _(pool):
            c = Chain(pool, made)
            c.did(nc.gpsimd.memset(K.ident[:], 0.0))
            c.settle()
            c.did(nc.gpsimd.affine_select(out=K.ident[:], in_=K.ident[:], compare_op=ALU.not_equal, fill=1.0,
                                          base=0, pattern=[[-1, 128]], channel_multiplier=1))
            c.did(nc.gpsimd.iota(K.iota_col[:], pattern=[[1, 128]], base=0, channel_multiplier=0,
                                 allow_small_or_imprecise_dtypes=True))
            c.did(nc.gpsimd.iota(K.node_id[:], pattern=[[P, TILES]], base=0, channel_multiplier=1,
                                 allow_small_or_imprecise_dtypes=True))
            c.settle()



def norm_stats(nc, c, x, stats, mv, var):
    for t in range(GT):
        c.did(nc.vector.bn_stats(stats[:, t, :], x[:, t, :]))
    c.settle()
    nc.vector.tensor_copy(mv[:, 0, 2:3], stats[:, 0, 1:2])
    for t in range(GT):
        c.did(nc.vector.bn_aggr(mv[:, t, 0:2], stats[:, t, :]))
    c.settle()
    return nc.vector.tensor_scalar(var[:, :], mv[:, :, 1], EPS, None, ALU.add)


def norm_rows(nc, c, x, out, mv, std, rstd):
    c.did(nc.vector.reciprocal(rstd[:, :], std[:, :]))
    c.settle()
    return [nc.vector.tensor_scalar(out[:, t, :], x[:, t, :], mv[:, t, 0:1], rstd[:, t:t + 1],
                                    ALU.subtract, ALU.mult) for t in range(GT)]


def turns(eng, n, body):
    body(0, True)
    if n > 1:
        with eng.Fori(1, n) as it:
            body(it, False)


def one(ap, i):
    if isinstance(i, int):
        return ap[i]
    v = ap[bass.ds(i, 1)]
    names = " ".join(f"d{k}" for k in range(len(v.shape)))
    rest = names.split(" ")[1:]
    return v.rearrange(f"{names} -> ({'d0 ' + rest[0]}) {' '.join(rest[1:])}")


def heads(a):
    return a.rearrange("p (h o) -> p h o", h=HEADS)


class EdgeSearch:

    def __init__(self, nc, K, s):
        self.nc, self.K = nc, K
        self.piv = s.sb("piv", [P, PIVOTS], I32)
        self.pivf = s.sb("pivf", [P, PIVOTS])
        self.fill = s.sb("fill", [1, DST_ROWS * FAN - E], I32)
        self.zero = s.sb("zero", [1, EP - E], I32)
        self.nid1 = s.sb("nid1", [P, TILES])
        self.less = s.sb("less", [P, CHUNK, FAN])
        self.cnt = s.sb("cnt", [P, CHUNK])
        self.low = s.sb("low", [P, CHUNK])
        self.row = s.sb("row", [P, CHUNK])
        self.idx = s.sb("idx", [P, 2, CHUNK], I32)
        self.got = s.sb("got", [P, 2, CHUNK, FAN], I32)
        self.pad_ready = s.sem("pad_ready")
        self.dst_padded = s.sem("dst_padded")
        self.piv_in = s.sem("piv_in")
        self.table_in = s.sem("table_in")
        self.idx_ready = s.sem("idx_ready")
        self.rows_in = s.sems("rows_in", 2)
        self.counted = s.sem("counted")

    def load(self, sp, A):
        K = self.K
        sp.wait_ge(self.pad_ready, 2)
        sp.dma_start(K.dst_d[0:E], A.dst).then_inc(self.dst_padded, 16)
        sp.dma_start(K.src_d[0:E], A.src).then_inc(self.dst_padded, 16)
        sp.dma_start(K.dst_d[E:DST_ROWS * FAN], self.fill[0, :]).then_inc(self.dst_padded, 16)
        sp.dma_start(K.src_d[E:EP], self.zero[0, :]).then_inc(self.dst_padded, 16)
        sp.wait_ge(self.dst_padded, 64)
        firsts = K.dst_d.rearrange("(a b c) -> a b c", b=FAN, c=FAN)
        with self.nc.allow_non_contiguous_dma(reason="first entries of rows, once"):
            sp.dma_start(self.piv[:, :], firsts[:, 0, 0].rearrange("(a r) -> a r", a=1).to_broadcast([P, PIVOTS])).then_inc(self.piv_in, 16)
            sp.dma_start(K.top_d, firsts[:, :, 0]).then_inc(self.table_in, 16)

    def prepare(self, dve):
        nc = self.nc
        nc.vector.memset(self.fill[:], NO_NODE).then_inc(self.pad_ready, 1)
        nc.vector.memset(self.zero[:], 0).then_inc(self.pad_ready, 1)
        nc.vector.tensor_scalar(self.nid1[:], self.K.node_id[:], 1.0, None, ALU.add).then_inc(self.counted, 1)

    def pivots(self, dve):
        nc = self.nc
        dve.wait_ge(self.piv_in, 16)
        nc.vector.tensor_copy(self.pivf[:], self.piv[:]).then_inc(self.counted, 1)
        dve.wait_ge(self.counted, 2)

    def count(self, dve, level, it):
        nc, base = self.nc, 2 + it * 10 + (0, 3, 7)[level]
        nodes = self.nid1[:, bass.ds(it * CHUNK, CHUNK)]
        if level == 0:
            n, entries = PIVOTS, self.pivf[:, :].rearrange("p (a f) -> p a f", a=1).to_broadcast([P, CHUNK, PIVOTS])
        else:
            n, entries = FAN, self.got[:, level - 1]
            dve.wait_ge(self.rows_in[level - 1], it * 16 * CHUNK + 16 * CHUNK)
        less = self.less[:, :, 0:n]
        nc.vector.tensor_tensor(less, entries, nodes.rearrange("p (t f) -> p t f", f=1).to_broadcast([P, CHUNK, n]),
                                ALU.is_lt).then_inc(self.counted, 1)
        dve.wait_ge(self.counted, base + 1)
        nc.vector.tensor_reduce(self.cnt[:, :], less, X, ALU.add).then_inc(self.counted, 1)
        dve.wait_ge(self.counted, base + 2)
        if level == 2:
            nc.vector.scalar_tensor_tensor(self.K.rend[:, bass.ds(it * CHUNK, CHUNK)], self.row[:, :], float(FAN),
                                           self.cnt[:, :], ALU.mult, ALU.add).then_inc(self.counted, 1)
            return
        nc.vector.tensor_scalar(self.low[:, :] if level else self.row[:, :], self.cnt[:, :], 1.0, 0.0,
                                ALU.subtract, ALU.max).then_inc(self.counted, 1)
        dve.wait_ge(self.counted, base + 3)
        if level:
            nc.vector.scalar_tensor_tensor(self.row[:, :], self.row[:, :], float(FAN), self.low[:, :],
                                           ALU.mult, ALU.add).then_inc(self.counted, 1)
            dve.wait_ge(self.counted, base + 4)
        nc.vector.tensor_copy(self.idx[:, level, :], self.row[:, :]).then_inc(self.idx_ready, 1)

    def gathers(self, pool):
        nc = self.nc
        pool.wait_ge(self.table_in, 16)
        with pool.Fori(0, TURNS) as it:
            for level in range(2):
                pool.wait_ge(self.idx_ready, it * 2 + (level + 1))
                pool_gate(nc, self.K)
                table = self.K.top_d if level == 0 else self.K.dst_d.rearrange("(r f) -> r f", f=FAN)
                for t in range(CHUNK):
                    nc.gpsimd.indirect_dma_start(
                        out=self.got[:, level, t, :], out_offset=None, in_=table,
                        in_offset=bass.IndirectOffsetOnAxis(ap=self.idx[:, level, t:t + 1], axis=0),
                    ).then_inc(self.rows_in[level], 16)


def stage_steps(nc, K):
    with Scope(nc, "steps") as s:
        rendT = s.sb("rendT", [TILES, P])
        rstartT = s.sb("rstartT", [TILES, P])
        zero = s.sb("zero1", [1, 1])
        part = s.sb("part", [TILES, 1])
        thr = s.sb("thr", [TILES, 1])
        ends = s.sb("ends", [TILES, STEPS])
        reach = s.sb("reach", [TILES, STEPS])
        ones = s.sb("ones_t", [TILES, 128])
        stepf = s.sb("stepf", [128, STEPS])
        group = s.sb("groupf", [1, STEPS])
        first = s.sb("first", [P, TILES])
        ps = s.ps("ps_steps", [128, 3, 512])
        made = s.sem("made")
        turned = s.sem("turned")
        rend_ready = s.sem("rend_ready")
        stored = s.sem("stored")
        loaded = s.sem("loaded")
        dve_done = s.sem("dve_done")
        counted = s.sem("counted")
        block = s.block()

        @block.gpsimd
        def _(pool):
            nc.gpsimd.iota(ends[:], pattern=[[EG, STEPS]], base=EG, channel_multiplier=0,
                           allow_small_or_imprecise_dtypes=True).then_inc(made, 1)
            nc.gpsimd.iota(part[:], pattern=[[0, 1]], base=0, channel_multiplier=EG,
                           allow_small_or_imprecise_dtypes=True).then_inc(made, 1)
            nc.gpsimd.iota(stepf[:], pattern=[[1, STEPS]], base=0, channel_multiplier=0,
                           allow_small_or_imprecise_dtypes=True).then_inc(made, 1)

        @block.tensor
        def _(pe):
            nc.tensor.transpose(ps[0:TILES, 0, 0:P], K.rend[:], K.ident[0:P, 0:P]).then_inc(turned, 1)
            pe.wait_ge(loaded, 16)
            nc.tensor.transpose(ps[0:P, 1, 0:TILES], rstartT[:], K.ident[0:TILES, 0:TILES]).then_inc(turned, 1)
            pe.wait_ge(counted, 1)
            nc.tensor.matmul(ps[:, 2, 0:STEPS], ones[:], reach[:], start=True, stop=True).then_inc(turned, 1)

        @block.sync
        def _(sp):
            sp.wait_ge(rend_ready, 2)
            sp.dma_start(K.rp_d[1:N + 1], rendT[:, :]).then_inc(stored, 16)
            sp.dma_start(K.rp_d[0:1], zero[0, :]).then_inc(stored, 16)
            sp.wait_ge(stored, 32)
            sp.dma_start(rstartT[:, :], K.rp_d[0:N].rearrange("(t p) -> t p", p=P)).then_inc(loaded, 16)

        @block.vector
        def _(dve):
            c = Chain(dve, dve_done)
            c.did(nc.vector.memset(ones[:], 1.0))
            nc.vector.memset(zero[:], 0.0).then_inc(rend_ready, 1)
            dve.wait_ge(turned, 1)
            nc.vector.tensor_copy(rendT[:, :], ps[0:TILES, 0, 0:P]).then_inc(rend_ready, 1)
            dve.wait_ge(made, 3)
            dve.wait_ge(loaded, 16)
            c.did(nc.vector.tensor_tensor(thr[:], rstartT[:, 0:1], part[:], ALU.add))
            c.settle()
            nc.vector.tensor_scalar(reach[:], ends[:], thr[:, 0:1], None, ALU.is_gt).then_inc(counted, 1)
            dve.wait_ge(turned, 2)
            dve.wait_ge(turned, 3)
            c.did(nc.vector.tensor_tensor(first[:], K.rend[:], ps[0:P, 1, 0:TILES], ALU.is_gt))
            c.settle()
            c.did(nc.vector.tensor_scalar(first[:], first[:], -4194304.0, 4194304.0, ALU.mult, ALU.add))
            c.settle()
            c.did(nc.vector.tensor_tensor(first[:], first[:], ps[0:P, 1, 0:TILES], ALU.add))
            c.settle()
            c.did(nc.vector.tensor_copy(K.firsti[:], first[:]))
            c.did(nc.vector.tensor_scalar(K.step_node[:, :], ps[:, 2, 0:STEPS], float(P), float(P), ALU.mult, ALU.subtract))
            c.did(nc.vector.tensor_scalar(K.step_tile[:, :], ps[0:1, 2, 0:STEPS], 1.0, None, ALU.subtract))
            c.did(nc.vector.tensor_tensor(group[:, :], stepf[0:1, :], ps[0:1, 2, 0:STEPS], ALU.subtract))
            c.settle()
            c.did(nc.vector.tensor_scalar(K.step_group[:, :], group[:, :], 1.0, None, ALU.add))
            c.settle()


def stage_embed(nc, K, A):
    U = UNROLL
    with Scope(nc, "embed") as s:
        wx = s.sb("wx", [128, HC, HW])
        att = s.sb("att", [128, 2, H])
        wtmp = s.sb("wtmp", [128, HC, 2, H])
        x = s.sb("x_in", [P, U, GT, H])
        xn = s.sb("xn", [P, U, GT, H])
        xt = s.sb("xt", [128, U, HC, GN])
        hs = s.sb("hs", [P, U, GT, ROW])
        stats = s.sb("stats", [P, GT, 6])
        mv = s.sb("mv", [P, GT, 3])
        var = s.sb("var", [P, GT])
        std = s.sb("std", [P, GT])
        rstd = s.sb("rstd", [P, GT])
        tp = s.ps("tp", [128, 2, HC, 512])
        hp = s.ps("hp", [128, GT, 512])
        w_in = s.sem("w_in")
        wx_ready = s.sem("wx_ready")
        x_in = s.sems("x_in", U)
        var_ready = s.sem("var_ready")
        std_ready = s.sem("std_ready")
        xn_ready = s.sem("xn_ready")
        xn_out = s.sems("xn_out", U)
        tp_ready = s.sem("tp_ready")
        xt_ready = s.sem("xt_ready")
        xt_out = s.sems("xt_out", U)
        h_ready = s.sem("h_ready")
        hs_ready = s.sem("hs_ready")
        h_out = s.sems("h_out", U)
        asd_ready = s.sem("asd_ready")
        dve_done = s.sem("dve_done")
        block = s.block()
        xg = A.x.rearrange("(g t p) f -> g p t f", p=P, t=GT)
        xng = K.xn_d.rearrange("(g t p) f -> g p t f", p=P, t=GT)
        hg = K.h_d.rearrange("(g t p) f -> g p t f", p=P, t=GT)
        find = EdgeSearch(nc, K, s)

        @block.gpsimd
        def _(pool):
            find.gathers(pool)

        @block.sync
        def _(sp):
            for c in range(HC):
                sp.dma_start(heads(wx[:, c, 0:ROW])[:, :, 0:OUT],
                             A.W[c * 128:(c + 1) * 128, :].rearrange("p (h o) -> p h o", o=OUT)).then_inc(w_in, 16)
            for k, a in enumerate((A.att_src, A.att_dst)):
                sp.dma_start(att[:, k, :], a.rearrange("(a h) o -> a (h o)", a=1).to_broadcast([128, H])).then_inc(w_in, 16)
            for u in range(U):
                rows_split(sp, x[:, u], xg[u], x_in[u])

            find.load(sp, A)

            def body(it, more):
                for u in range(U):
                    g = it * U + u
                    sp.wait_ge(xn_ready, g * GT + GT)
                    if more:
                        rows_split(sp, x[:, u], one(xg, g + U), x_in[u])
                    rows_split(sp, one(xng, g), xn[:, u], xn_out[u])
                    sp.wait_ge(xt_ready, g + 1)
                    sp.dma_start(one(K.xt_d, g), xt[:, u].rearrange("p c n -> p (c n)")).then_inc(xt_out[u], 16)
                    sp.wait_ge(hs_ready, g + 1)
                    rows_split(sp, one(hg, g), hs[:, u], h_out[u])

            with sp.Fori(0, TURNS - 1) as it:
                body(it, True)
            body(TURNS - 1, False)
            for u in range(U):
                sp.wait_ge(xn_out[u], 32 * TURNS)
                sp.wait_ge(xt_out[u], 16 * TURNS)
                sp.wait_ge(h_out[u], 32 * TURNS)

        @block.vector
        def _(dve):
            find.prepare(dve)
            dve.wait_ge(w_in, 64)
            for k in range(2):
                for c in range(HC):
                    nc.vector.tensor_tensor(wtmp[:, c, k, :].rearrange("p (h o) -> p h o", o=OUT), heads(wx[:, c, 0:ROW])[:, :, 0:OUT],
                                            att[:, k, :].rearrange("p (h o) -> p h o", o=OUT), ALU.mult).then_inc(wx_ready, 1)
            dve.wait_ge(wx_ready, 4)
            for k in range(2):
                for c in range(HC):
                    nc.vector.tensor_reduce(wx[:, c, ROW:HW] if k else wx[:, c, OUT:ROW:OUT + 1],
                                            wtmp[:, c, k, :].rearrange("p (h o) -> p h o", h=HEADS), X, ALU.add).then_inc(wx_ready, 1)

            def h_copy(g, v, stored, fresh):
                dve.wait_ge(h_ready, g + 1)
                if not fresh:
                    dve.wait_ge(h_out[v], stored)
                tiles = K.asd[:, bass.ds(g * GT, GT), :]
                nc.vector.tensor_copy(tiles[:, :, 0:HEADS], hp[0:P, :, OUT:ROW:OUT + 1]).then_inc(asd_ready, 1)
                nc.vector.tensor_copy(tiles[:, :, HEADS:], hp[0:P, :, ROW:HW]).then_inc(asd_ready, 1)
                nc.vector.tensor_copy(hs[:, v], hp[0:P, :, 0:ROW]).then_inc(hs_ready, 1)

            find.pivots(dve)
            per = U * (2 * GT + 1)

            def body(it, first):
                c = Chain(dve, dve_done, per, it)
                for u in range(U):
                    g = it * U + u
                    dve.wait_ge(x_in[u], it * 32 + 32)
                    norm_stats(nc, c, x[:, u], stats, mv, var).then_inc(var_ready, 1)
                    if not (first and u < 2):
                        h_copy(g - 2, (u - 2) % U, it * 32 if u >= 2 else (it - 1) * 32, first or (u < 2 and first))
                    if u % 2 == 0:
                        find.count(dve, u // 2, it)
                    dve.wait_ge(std_ready, g + 1)
                    if not first:
                        dve.wait_ge(xn_out[u], it * 32)
                        dve.wait_ge(tp_ready, g - U + 1)
                    for ins in norm_rows(nc, c, x[:, u], xn[:, u], mv, std, rstd):
                        ins.then_inc(xn_ready, 1)
                c.close()

            turns(dve, TURNS, body)
            for g in (GROUPS - 2, GROUPS - 1):
                h_copy(g, g % U, 32 * (TURNS - 1), False)

        @block.scalar
        def _(act):
            def body(it, first):
                for u in range(U):
                    g = it * U + u
                    act.wait_ge(var_ready, g + 1)
                    nc.scalar.activation(std[:, :], var[:, :], ACT.Sqrt).then_inc(std_ready, 1)
                    act.wait_ge(tp_ready, g + 1)
                    if not first:
                        act.wait_ge(xt_out[u], it * 16)
                        act.wait_ge(h_ready, g - U + 1)
                    nc.scalar.activation(xt[:, u], tp[:, u % 2, :, 0:GN], ACT.Copy).then_inc(xt_ready, 1)

            turns(act, TURNS, body)

        @block.tensor
        def _(pe):
            pe.wait_ge(wx_ready, 8)

            def project(g, u, first):
                pe.wait_ge(xt_ready, g + 1)
                if not first:
                    pe.wait_ge(hs_ready, g)
                for t in range(GT):
                    for k in range(HC):
                        mm = nc.tensor.matmul(hp[0:P, t, 0:HW], xt[:, u, k, t * P:(t + 1) * P], wx[:, k, :],
                                              start=(k == 0), stop=(k == HC - 1))
                mm.then_inc(h_ready, 1)

            def body(it, first):
                for u in range(U):
                    g = it * U + u
                    pe.wait_ge(xn_ready, g * GT + GT)
                    if not (first and u < 2):
                        pe.wait_ge(xt_ready, g if u == 0 else g - 1)
                    for t in range(GT):
                        for k in range(HC):
                            mm = nc.tensor.transpose(tp[:, u % 2, k, t * P:(t + 1) * P],
                                                     xn[:, u, t, k * 128:(k + 1) * 128], K.ident[0:P, 0:P])
                    mm.then_inc(tp_ready, 1)
                    if not (first and u == 0):
                        project(g - 1, (u - 1) % U, first and u == 1)

            turns(pe, TURNS, body)
            project(GROUPS - 1, U - 1, False)


class EdgeScatter:

    ZERO = 4096

    def __init__(self, nc, K, s):
        self.nc, self.K = nc, K
        self.idx = s.sb("first_idx", [P, CHUNK], I32)
        self.a_d = s.sb("a_d_rows", [P, CHUNK, HEADS])
        self.zeros = s.sb("zeros_b", [128, self.ZERO])
        self.copied = s.sem("first_copied")
        self.rec_out = s.sem("rec_out")
        self.zero_ready = s.sem("zero_ready")
        self.zero_out = s.sem("zero_out")

    def run(self, pool):
        nc, K = self.nc, self.K
        nc.gpsimd.memset(self.zeros[:], 0.0).then_inc(self.zero_ready, 1)

        def body(it, first):
            chunk = bass.ds(it * CHUNK, CHUNK)
            nc.gpsimd.tensor_copy(self.idx[:], K.firsti[:, chunk]).then_inc(self.copied, 1)
            nc.gpsimd.tensor_copy(self.a_d[:], K.asd[:, chunk, HEADS:]).then_inc(self.copied, 1)
            pool.wait_ge(self.copied, it * 2 + 2)
            pool_gate(nc, K)
            for t in range(CHUNK):
                nc.gpsimd.indirect_dma_start(
                    out=K.rec_d, out_offset=bass.IndirectOffsetOnAxis(ap=self.idx[:, t:t + 1], axis=0),
                    in_=self.a_d[:, t, :], in_offset=None, bounds_check=EP - 1, oob_is_err=False).then_inc(self.rec_out, 16)
            pool.wait_ge(self.rec_out, it * (16 * CHUNK) + 16 * CHUNK)
            pool_gate(nc, K)

        turns(pool, TURNS, body)
        pool.wait_ge(self.zero_ready, 1)
        flat = K.buf_d.rearrange("(p j) r -> p (j r)", p=128)
        n = SLOTS // 128 * TOKW
        count = 0
        for k in range(0, n, self.ZERO):
            w = min(self.ZERO, n - k)
            pool.dma_start(flat[:, k:k + w], self.zeros[:, 0:w]).then_inc(self.zero_out, 16)
            count += 16
        pool.wait_ge(self.zero_out, count)


def stage_mix(nc, K, A):
    U = UNROLL
    C = H
    GH = C // 4
    D = 32
    with Scope(nc, "mix") as s:
        scatter = EdgeScatter(nc, K, s)
        wqkv = s.sb("wqkv", [128, HC, 3 * C])
        wg1 = s.sb("wg1", [128, HC, GH])
        wg1g = s.sb("wg1g", [128, HC, GH])
        lng = s.sb("lng", [128, HC])
        lnb = s.sb("lnb", [128, HC])
        bg1 = s.sb("bg1", [GH, 1])
        bias1 = s.sb("bias1", [GH, 1])
        wg2 = s.sb("wg2", [GH, C])
        bg2 = s.sb("bg2", [128, HC])
        wproj = s.sb("wproj", [128, HC, C])
        bproj = s.sb("bproj", [P, C])
        kmax_g = s.sb("kmax_g", [128, HC, GROUPS])
        kmax = s.sb("kmax", [128, HC])
        nkmax = s.sb("nkmax", [1, C])
        ones = s.sb("ones1", [1, P])
        wqT = s.sb("wqT", [128, HC, C])
        ctx_acc = s.sb("ctx_acc", [128, HC, 129])
        ctx_inv = s.sb("ctx_inv", [128, HC])
        ctx_bd = s.sb("ctx_bd", [128, HC, 128])
        wqc = s.sb("wqc", [128, HC, C])
        xt = s.sb("xt2", [128, U, HC * GN])
        io = s.sb("io2", [128, U, GT * H])
        z = s.sb("z", [P, GT, H])
        zt = s.sb("zt", [128, HC, GN])
        hgt = s.sb("hgt", [GH, GN])
        gt = s.sb("gt", [128, 2, HC * GN])
        pk = s.sb("pk", [P, 2, C])
        vx = s.sb("vx", [P, 2, HC, 129])
        og = s.sb("og", [128, HC * GN])
        mo = s.sb("mo", [P, 2, GT, C])
        stats = s.sb("stats2", [P, GT, 6])
        mv = s.sb("mv2", [P, GT, 3])
        var = s.sb("var2", [P, GT])
        std = s.sb("std2", [P, GT])
        rstd = s.sb("rstd2", [P, GT])
        ps = s.ps("ps_mix", [128, 8, 512])
        w_in = s.sem("w_in2")
        set_up = s.sem("set_up")
        in_a = s.sems("in_a", U)
        in_b = s.sems("in_b", U)
        in_c = s.sems("in_c", U)
        var_ready, std_ready, z_ready, zt_psum, zt_ready = (s.sem(n) for n in (
            "var_ready2", "std_ready2", "z_ready", "zt_psum", "zt_ready"))
        kt_ready, kt_used, hg_psum, hg_ready, gate_psum, gate_ready = (s.sem(n) for n in (
            "kt_ready", "kt_used", "hg_psum", "hg_ready", "gate_psum", "gate_ready"))
        gate_out = s.sems("gate_out", 2)
        kmax_ready, kmax_row, nkmax_ready = s.sem("kmax_ready"), s.sem("kmax_row"), s.sem("nkmax_ready")
        kv_psum, p_ready, v_ready, ctx_psum, ctx_added = (s.sem(n) for n in (
            "kv_psum", "p_ready", "v_ready", "ctx_psum", "ctx_added"))
        bd_ready, wqc_psum, wqc_ready = s.sem("bd_ready"), s.sem("wqc_psum"), s.sem("wqc_ready")
        out_psum, og_ready, mix_psum, mix_ready = (s.sem(n) for n in ("out_psum", "og_ready", "mix_psum", "mix_ready"))
        mix_out = s.sems("mix_out", 2)
        dve_done = s.sem("dve_done2")
        dve_end = s.sem("dve_end2")
        block = s.block()
        xng = K.xn_d.rearrange("(g t p) f -> g p t f", p=P, t=GT)
        mixg = K.mix_d.rearrange("(g t p) f -> g p t f", p=P, t=GT)
        rows = lambda u: io[0:P, u, :].rearrange("p (t f) -> p t f", t=GT)
        fm = lambda t, k: t.rearrange("p (k n) -> p k n", k=HC)[:, k, :]

        @block.gpsimd
        def _(pool):
            scatter.run(pool)

        @block.sync
        def _(sp):
            with nc.allow_non_contiguous_dma(reason="biases to columns, once"):
                for t, a in ((wqkv, A.mix_Wqkv), (wg1, A.mix_Wg1), (wproj, A.mix_Wproj)):
                    sp.dma_start(t[:], a.rearrange("(c p) n -> p c n", p=128)).then_inc(w_in, 16)
                for t, a in ((lng, A.mix_ln_g), (lnb, A.mix_ln_b), (bg2, A.mix_bg2)):
                    sp.dma_start(t[:], a.rearrange("(c p) -> p c", p=128)).then_inc(w_in, 16)
                sp.dma_start(bg1[:, :], A.mix_bg1.rearrange("(p a) -> p a", a=1)).then_inc(w_in, 16)
            sp.dma_start(wg2[:, :], A.mix_Wg2).then_inc(w_in, 16)
            sp.dma_start(bproj[:, :], A.mix_bproj.rearrange("(a n) -> a n", a=1).to_broadcast([P, C])).then_inc(w_in, 16)

            def load_a(g, u):
                sp.dma_start(xt[:, u, :], one(K.xt_d, g)).then_inc(in_a[u], 16)
                rows_split(sp, rows(u), one(xng, g), in_a[u])

            def load_b(g, u):
                sp.dma_start(xt[:, u, :], one(K.xt_d, g)).then_inc(in_b[u], 16)

            def load_c(g, u):
                sp.dma_start(xt[:, u, :], one(K.xt_d, g)).then_inc(in_c[u], 16)
                sp.dma_start(io[:, u, 0:HC * GN], one(K.gt_d, g)).then_inc(in_c[u], 16)

            for u in range(U):
                load_a(u, u)

            def gates(it, more):
                for u in range(U):
                    g = it * U + u
                    sp.wait_ge(kt_ready, g + 1)
                    sp.wait_ge(z_ready, g * GT + GT)
                    (load_a if more else load_b)(g + U if more else u, u)
                    sp.wait_ge(gate_ready, g + 1)
                    if isinstance(g, int):
                        sp.dma_start(K.gt_d[g], gt[:, u % 2, :]).then_inc(gate_out[u % 2], 16)
                    else:
                        sp.dma_start(one(K.gt_d, g), gt[:, u % 2, :]).then_inc(gate_out[u % 2], 16)

            with sp.Fori(0, TURNS - 1) as it:
                gates(it, True)
            gates(TURNS - 1, False)

            def context(it, more):
                for u in range(U):
                    g = it * U + u
                    sp.wait_ge(kv_psum, g * GT + GT)
                    if more:
                        load_b(g + U, u)
                    else:
                        if u == 0:
                            for b in range(2):
                                sp.wait_ge(gate_out[b], 16 * (3 - b) * TURNS)
                        load_c(u, u)

            with sp.Fori(0, TURNS - 1) as it:
                context(it, True)
            context(TURNS - 1, False)

            def output(it, more):
                for u in range(U):
                    g = it * U + u
                    sp.wait_ge(og_ready, g + 1)
                    if more:
                        load_c(g + U, u)
                    sp.wait_ge(mix_ready, g + 1)
                    rows_split(sp, one(mixg, g), mo[:, u % 2], mix_out[u % 2])

            with sp.Fori(0, TURNS - 1) as it:
                output(it, True)
            output(TURNS - 1, False)
            for b in range(2):
                sp.wait_ge(mix_out[b], 32 * (3 - b) * TURNS)

        def stored(it, u, per):
            return (it * (3 if u % 2 == 0 else 2) + u // 2) * per

        @block.vector
        def _(dve):
            c = Chain(dve, dve_end)
            dve.wait_ge(w_in, 144)
            for k in range(HC):
                nc.vector.tensor_scalar(wg1g[:, k, :], wg1[:, k, :], lng[:, k:k + 1], None, ALU.mult).then_inc(set_up, 1)
            nc.vector.memset(ones[:], 1.0).then_inc(set_up, 1)
            nc.vector.memset(ctx_acc[:], 0.0).then_inc(set_up, 1)
            nc.vector.memset(ctx_bd[:], 0.0).then_inc(set_up, 1)
            for b in range(2):
                nc.vector.memset(vx[:, b, :, 128:129], 1.0).then_inc(set_up, 1)
            dve.wait_ge(wqc_psum, 1)
            nc.vector.tensor_tensor(bias1[:], ps[0:GH, 7, 0:1], bg1[:], ALU.add).then_inc(set_up, 1)
            for k in range(HC):
                nc.vector.tensor_copy(wqT[:, k, :], ps[:, k, 0:C]).then_inc(set_up, 1)

            per = U * (2 * GT + 1)

            def gates(it, first):
                c = Chain(dve, dve_done, per, it)
                for u in range(U):
                    g = it * U + u
                    dve.wait_ge(in_a[u], it * 48 + 48)
                    norm_stats(nc, c, rows(u), stats, mv, var).then_inc(var_ready, 1)
                    dve.wait_ge(kt_ready, g + 1)
                    nc.vector.tensor_reduce(kmax_g[:, :, bass.ds(g, 1)], ps[:, 0:2, 0:GN], X, ALU.max).then_inc(kt_used, 1)
                    dve.wait_ge(std_ready, g + 1)
                    if not (first and u == 0):
                        dve.wait_ge(zt_psum, g)
                    for ins in norm_rows(nc, c, rows(u), z, mv, std, rstd):
                        ins.then_inc(z_ready, 1)
                c.close()

            turns(dve, TURNS, gates)
            dve.wait_ge(kt_used, GROUPS)
            nc.vector.tensor_reduce(kmax[:], kmax_g[:], X, ALU.max).then_inc(kmax_ready, 1)
            dve.wait_ge(kmax_row, 1)
            nc.vector.tensor_scalar(nkmax[:], ps[0:1, 7, 0:C], -1.0, None, ALU.mult).then_inc(nkmax_ready, 1)

            def context(it, first):
                for u in range(U):
                    g = it * U + u
                    for t in range(GT):
                        i = g * GT + t
                        dve.wait_ge(kv_psum, i + 1)
                        if not (first and u == 0 and t < 2):
                            dve.wait_ge(ctx_psum, i - 1)
                        nc.vector.tensor_copy(vx[:, t % 2, :, 0:128],
                                              ps[0:P, 2 + t % 2, 0:C].rearrange("p (c v) -> p c v", c=HC)).then_inc(v_ready, 1)
                    dve.wait_ge(ctx_psum, g * GT + GT)
                    if not (first and u == 0):
                        dve.wait_ge(ctx_added, g)
                    nc.vector.tensor_tensor(ctx_acc[:], ctx_acc[:], ps[:, 4:6, 0:129], ALU.add).then_inc(ctx_added, 1)

            dve.wait_ge(set_up, 7)
            turns(dve, TURNS, context)
            dve.wait_ge(ctx_added, GROUPS)
            c.did(nc.vector.reciprocal(ctx_inv[:], ctx_acc[:, :, 128]))
            c.settle()
            for k in range(HC):
                for h in range(128 // D):
                    q = slice(h * D, h * D + D)
                    nc.vector.tensor_scalar(ctx_bd[q, k, q], ctx_acc[q, k, q], ctx_inv[q, k:k + 1], None,
                                            ALU.mult).then_inc(bd_ready, 1)
            dve.wait_ge(wqc_psum, 2)
            nc.vector.tensor_copy(wqc[:], ps[:, 6:8, 0:C]).then_inc(wqc_ready, 1)

            def output(it, first):
                for u in range(U):
                    g = it * U + u
                    dve.wait_ge(in_c[u], it * 32 + 32)
                    dve.wait_ge(out_psum, g + 1)
                    if not (first and u == 0):
                        dve.wait_ge(mix_psum, g)
                    nc.vector.tensor_tensor(og[:].rearrange("p (k n) -> p k n", k=HC), ps[:, 0:2, 0:GN],
                                            io[:, u, 0:HC * GN].rearrange("p (k n) -> p k n", k=HC), ALU.mult).then_inc(og_ready, 1)
                    dve.wait_ge(mix_psum, g + 1)
                    if not (first and u < 2):
                        dve.wait_ge(mix_out[u % 2], stored(it, u, 32))
                    nc.vector.tensor_tensor(mo[:, u % 2].rearrange("p (a b) f -> p a b f", a=2),
                                            ps[0:P, 2:4, :].rearrange("p a (b f) -> p a b f", b=2),
                                            bproj[:].rearrange("p (a b f) -> p a b f", a=1, b=1).to_broadcast([P, 2, 2, C]),
                                            ALU.add).then_inc(mix_ready, 1)

            turns(dve, TURNS, output)

        @block.scalar
        def _(act):
            act.wait_ge(set_up, 8)

            def gates(it, first):
                for u in range(U):
                    g = it * U + u
                    act.wait_ge(var_ready, g + 1)
                    nc.scalar.activation(std[:, :], var[:, :], ACT.Sqrt).then_inc(std_ready, 1)
                    act.wait_ge(zt_psum, g + 1)
                    if not (first and u == 0):
                        act.wait_ge(hg_psum, g)
                    nc.scalar.activation(zt[:], ps[:, 2:4, 0:GN], ACT.Copy).then_inc(zt_ready, 1)
                    act.wait_ge(hg_psum, g + 1)
                    nc.scalar.activation(hgt[:], ps[0:GH, 4, 0:GN], ACT.Gelu, bias=bias1[:, 0:1]).then_inc(hg_ready, 1)
                    act.wait_ge(gate_psum, g + 1)
                    if not (first and u < 2):
                        act.wait_ge(gate_out[u % 2], stored(it, u, 16))
                    nc.scalar.activation(fm(gt[:, u % 2, :], 0), ps[:, 5, 0:GN], ACT.Sigmoid, bias=bg2[:, 0:1])
                    nc.scalar.activation(fm(gt[:, u % 2, :], 1), ps[:, 6, 0:GN], ACT.Sigmoid, bias=bg2[:, 1:2]).then_inc(gate_ready, 1)

            turns(act, TURNS, gates)

            def context(it, first):
                for u in range(U):
                    for t in range(GT):
                        i = (it * U + u) * GT + t
                        act.wait_ge(kv_psum, i + 1)
                        if not (first and u == 0 and t < 2):
                            act.wait_ge(ctx_psum, i - 1)
                        nc.scalar.activation(pk[:, t % 2, :], ps[0:P, t % 2, 0:C], ACT.Exp).then_inc(p_ready, 1)

            turns(act, TURNS, context)

        @block.tensor
        def _(pe):
            pe.wait_ge(w_in, 144)
            for i in range(HC):
                for k in range(HC):
                    nc.tensor.transpose(ps[:, k, i * 128:(i + 1) * 128], wqkv[:, i, k * 128:(k + 1) * 128], K.ident[:])
            for k in range(HC):
                mm = nc.tensor.matmul(ps[0:GH, 7, 0:1], wg1[:, k, :], lnb[:, k:k + 1], start=(k == 0), stop=(k == HC - 1))
            mm.then_inc(wqc_psum, 1)
            pe.wait_ge(set_up, 10)

            def gates(it, first):
                for u in range(U):
                    g = it * U + u
                    pe.wait_ge(in_a[u], it * 48 + 48)
                    if not (first and u == 0):
                        pe.wait_ge(kt_used, g)
                    for m in range(HC):
                        for k in range(HC):
                            mm = nc.tensor.matmul(ps[:, m, 0:GN], wqkv[:, k, C + m * 128:C + (m + 1) * 128],
                                                  fm(xt[:, u, :], k), start=(k == 0), stop=(k == HC - 1))
                    mm.then_inc(kt_ready, 1)
                    pe.wait_ge(z_ready, g * GT + GT)
                    if not (first and u == 0):
                        pe.wait_ge(zt_ready, g)
                    for t in range(GT):
                        for k in range(HC):
                            mm = nc.tensor.transpose(ps[:, 2 + k, t * P:(t + 1) * P], z[:, t, k * 128:(k + 1) * 128],
                                                     K.ident[0:P, 0:P])
                    mm.then_inc(zt_psum, 1)
                    pe.wait_ge(zt_ready, g + 1)
                    if not (first and u == 0):
                        pe.wait_ge(hg_ready, g)
                    for k in range(HC):
                        mm = nc.tensor.matmul(ps[0:GH, 4, 0:GN], wg1g[:, k, :], zt[:, k, :], start=(k == 0), stop=(k == HC - 1))
                    mm.then_inc(hg_psum, 1)
                    pe.wait_ge(hg_ready, g + 1)
                    if not (first and u == 0):
                        pe.wait_ge(gate_ready, g)
                    for m in range(HC):
                        mm = nc.tensor.matmul(ps[:, 5 + m, 0:GN], wg2[:, m * 128:(m + 1) * 128], hgt[:], start=True, stop=True)
                    mm.then_inc(gate_psum, 1)

            turns(pe, TURNS, gates)
            pe.wait_ge(kmax_ready, 1)
            for k in range(HC):
                mm = nc.tensor.transpose(ps[0:1, 7, k * 128:(k + 1) * 128], kmax[:, k:k + 1], K.ident[:])
            mm.then_inc(kmax_row, 1)
            pe.wait_ge(nkmax_ready, 1)
            pe.wait_ge(gate_ready, GROUPS)

            def context(it, first):
                for u in range(U):
                    for t in range(GT):
                        i = (it * U + u) * GT + t
                        if t == 0:
                            pe.wait_ge(in_b[u], it * 16 + 16)
                        if not (first and u == 0 and t < 2):
                            pe.wait_ge(p_ready, i - 1)
                            pe.wait_ge(v_ready, i - 1)
                        for k in range(HC):
                            nc.tensor.matmul(ps[0:P, t % 2, 0:C], fm(xt[:, u, :], k)[:, t * P:(t + 1) * P],
                                             wqkv[:, k, C:2 * C], start=(k == 0), stop=False)
                        nc.tensor.matmul(ps[0:P, t % 2, 0:C], ones[:], nkmax[:], start=False, stop=True)
                        for k in range(HC):
                            mm = nc.tensor.matmul(ps[0:P, 2 + t % 2, 0:C], fm(xt[:, u, :], k)[:, t * P:(t + 1) * P],
                                                  wqkv[:, k, 2 * C:3 * C], start=(k == 0), stop=(k == HC - 1))
                        mm.then_inc(kv_psum, 1)
                        pe.wait_ge(p_ready, i + 1)
                        pe.wait_ge(v_ready, i + 1)
                        if t == 0 and not (first and u == 0):
                            pe.wait_ge(ctx_added, it * U + u)
                        for k in range(HC):
                            mm = nc.tensor.matmul(ps[:, 4 + k, 0:129], pk[:, t % 2, k * 128:(k + 1) * 128],
                                                  vx[:, t % 2, k, :], start=(t == 0), stop=(t == GT - 1))
                        mm.then_inc(ctx_psum, 1)

            turns(pe, TURNS, context)
            pe.wait_ge(bd_ready, HC * 128 // D)
            for m in range(HC):
                for k in range(HC):
                    mm = nc.tensor.matmul(ps[:, 6 + m, k * 128:(k + 1) * 128], wqT[:, k, m * 128:(m + 1) * 128],
                                          ctx_bd[:, k, :], start=True, stop=True)
            mm.then_inc(wqc_psum, 1)
            pe.wait_ge(wqc_ready, 1)

            def output(it, first):
                for u in range(U):
                    g = it * U + u
                    pe.wait_ge(in_c[u], it * 32 + 32)
                    if not (first and u == 0):
                        pe.wait_ge(og_ready, g)
                    for m in range(HC):
                        for k in range(HC):
                            mm = nc.tensor.matmul(ps[:, m, 0:GN], wqc[:, k, m * 128:(m + 1) * 128],
                                                  fm(xt[:, u, :], k), start=(k == 0), stop=(k == HC - 1))
                    mm.then_inc(out_psum, 1)
                    pe.wait_ge(og_ready, g + 1)
                    if not (first and u == 0):
                        pe.wait_ge(mix_ready, g)
                    for t in range(GT):
                        for k in range(HC):
                            mm = nc.tensor.matmul(ps[0:P, 2 + t // 2, (t % 2) * C:(t % 2 + 1) * C],
                                                  fm(og[:], k)[:, t * P:(t + 1) * P], wproj[:, k, :],
                                                  start=(k == 0), stop=(k == HC - 1))
                    mm.then_inc(mix_psum, 1)

            turns(pe, TURNS, output)


def zero_fill(nc, K):
    with Scope(nc, "zero_fill") as s:
        zeros = s.sb("zeros", [128, HEADS * EC])
        ready = s.sem("zeros_ready")
        out = s.sem("zeros_out")
        block = s.block()

        @block.vector
        def _(dve):
            nc.vector.memset(zeros[:], 0.0).then_inc(ready, 1)

        @block.sync
        def _(sp):
            sp.wait_ge(ready, 1)
            sp.dma_start(K.rec_d.rearrange("(p j) r -> p (j r)", p=128), zeros[:, :]).then_inc(out, 16)
            sp.dma_start(K.y_d[SLOTS:SLOTS + 1, :], zeros[0:1, 0:H]).then_inc(out, 16)
            sp.wait_ge(out, 32)


def stage_edges(nc, K):
    with Scope(nc, "edges") as s:
        rec = s.sb("rec", [128, EC, HEADS])
        meta = s.sb("meta", [128, EC, META])
        dst = s.sb("dst_b", [128, EC], I32)
        prev = s.sb("prev_b", [128, EC], I32)
        follow = s.sb("follow_b", [128, EC], I32)
        src = s.sb("src_b", [128, EC], I32)
        same = s.sb("same", [128, EC])
        same_next = s.sb("same_next", [128, EC])
        pen = s.sb("pen", [128, 2, EC])
        head = s.sb("head", [128, EC])
        tail = s.sb("tail", [128, 2, HEADS])
        rows = s.sb("rows", [HEADS, 2, 128])
        run = s.sb("run", [HEADS, 128])
        carry = s.sb("carry", [128, HEADS])
        one_row = s.sb("one_row", [1, EDGE_GROUPS])
        ps = s.ps("ps_edges", [128, 2, 512])
        edges_in = s.sem("edges_in")
        rec_in = s.sem("rec_in")
        tail_ready = s.sem("tail_ready")
        tail_turned = s.sem("tail_turned")
        run_ready = s.sem("run_ready")
        run_turned = s.sem("run_turned")
        pen_ready, pen_out = s.sem("pen_ready"), s.sem("pen_out")
        meta_ready, meta_out = s.sem("meta_ready"), s.sem("meta_out")
        done = s.sem("dve_done")
        block = s.block()
        flat = K.dst_d
        per_edge = lambda a: a.rearrange("(p j) -> p j", p=128)

        @block.sync
        def _(sp):
            sp.dma_start(dst[:, :], per_edge(flat[0:EP])).then_inc(edges_in, 16)
            sp.dma_start(prev[1:128, :], flat[EC - 1:EP - 1].rearrange("(p j) -> p j", p=127)).then_inc(edges_in, 16)
            sp.dma_start(prev[0:1, 1:EC], flat[0:EC - 1].rearrange("(p j) -> p j", p=1)).then_inc(edges_in, 16)
            sp.dma_start(follow[:, :], per_edge(flat[1:EP + 1])).then_inc(edges_in, 16)
            sp.dma_start(src[:, :], per_edge(K.src_d)).then_inc(edges_in, 16)
            sp.dma_start(rec[:], K.rec_d.rearrange("(p j) h -> p j h", p=128)).then_inc(rec_in, 16)
            sp.wait_ge(pen_ready, 2)
            for k in range(2):
                sp.dma_start(per_edge(K.pen_d[k]), pen[:, k, :]).then_inc(pen_out, 16)
            sp.wait_ge(meta_ready, 4 + HEADS)
            sp.dma_start(K.meta_d.rearrange("(p j) r -> p j r", p=128), meta[:]).then_inc(meta_out, 16)
            sp.wait_ge(meta_out, 16)
            with nc.allow_non_contiguous_dma(reason="one number of each group, once"):
                ends = K.meta_d.rearrange("(g n) r -> g n r", n=EG)[:, EG - 1, HEADS]
                sp.dma_start(ends.rearrange("(a g) -> a g", a=1), one_row[:, :]).then_inc(meta_out, 16)
            sp.wait_ge(meta_out, 32)
            sp.wait_ge(pen_out, 32)

        @block.tensor
        def _(pe):
            pe.wait_ge(tail_ready, 2)
            for q in range(2):
                mm = nc.tensor.transpose(ps[0:HEADS, 0, q * 128:(q + 1) * 128], tail[:, q, :], K.ident[:])
            mm.then_inc(tail_turned, 1)
            pe.wait_ge(run_ready, 2)
            nc.tensor.transpose(ps[:, 1, 0:HEADS], run[:, :], K.ident[0:HEADS, 0:HEADS]).then_inc(run_turned, 1)

        @block.vector
        def _(dve):
            c = Chain(dve, done)
            v = nc.vector
            v.memset(one_row[:], 1.0).then_inc(meta_ready, 1)
            dve.wait_ge(edges_in, 80)
            c.did(v.memset(prev[0:1, 0:1], -1))
            c.settle()
            c.did(v.tensor_tensor(same[:], dst[:], prev[:], ALU.is_equal))
            c.did(v.tensor_tensor(same_next[:], dst[:], follow[:], ALU.is_equal))
            v.tensor_copy(meta[:, :, HEADS + 1], dst[:]).then_inc(meta_ready, 1)
            v.tensor_copy(meta[:, :, HEADS + 2].bitcast(I32), src[:]).then_inc(meta_ready, 1)
            c.settle()
            v.tensor_scalar(pen[:, 0, :], same[:], 1.0, -NEVER, ALU.subtract, ALU.mult).then_inc(pen_ready, 1)
            v.tensor_scalar(pen[:, 1, :], same_next[:], 1.0, -NEVER, ALU.subtract, ALU.mult).then_inc(pen_ready, 1)
            v.tensor_scalar(meta[:, :, HEADS], same_next[:], -1.0, 1.0, ALU.mult, ALU.add).then_inc(meta_ready, 1)
            c.did(v.tensor_tensor_scan(head[:], same[:], same[:], 1.0, ALU.mult, ALU.mult))
            dve.wait_ge(rec_in, 16)
            for h in range(HEADS):
                c.did(v.tensor_tensor_scan(rec[:, :, h], same[:], rec[:, :, h], 0.0, ALU.mult, ALU.add))
            c.settle()
            v.tensor_copy(tail[:, 0, :], rec[:, EC - 1, :]).then_inc(tail_ready, 1)
            v.tensor_copy(tail[:, 1, :], head[:, EC - 1:EC].to_broadcast([128, HEADS])).then_inc(tail_ready, 1)
            dve.wait_ge(tail_turned, 1)
            c.did(v.tensor_copy(rows[:, :, :], ps[0:HEADS, 0, 0:256].rearrange("p (a b) -> p a b", a=2)))
            c.settle()
            v.memset(run[:, 0:1], 0.0).then_inc(run_ready, 1)
            v.tensor_tensor_scan(run[:, 1:128], rows[:, 1, 0:127], rows[:, 0, 0:127], 0.0,
                                 ALU.mult, ALU.add).then_inc(run_ready, 1)
            dve.wait_ge(run_turned, 1)
            c.did(v.tensor_copy(carry[:, :], ps[:, 1, 0:HEADS]))
            c.settle()
            for h in range(HEADS):
                v.scalar_tensor_tensor(meta[:, :, h], head[:], carry[:, h:h + 1], rec[:, :, h],
                                       ALU.mult, ALU.add).then_inc(meta_ready, 1)


def stage_aggregate(nc, K):
    B, R = STEP_BATCH, 3
    W = ROW + HEADS + 1
    BIG = float(2.0 ** 100)
    full, rest = BATCHES // R, BATCHES % R
    assert STEPS % B == 0 and rest
    with Scope(nc, "aggregate") as s:
        meta = s.sb("meta_s", [128, R, B, 4, META])
        pen = s.sb("pen_s", [B * HEADS, R, 2, EG])
        g = s.sb("g", [128, R, B, 4, W])
        alpha = s.sb("alpha", [128, 4, B, HEADS])
        below = s.sb("below", [128, 4, B, HEADS])
        run_on = s.sb("run_on", [B * HEADS, EG])
        run_back = s.sb("run_back", [B * HEADS, EG])
        local = s.sb("local", [128, R, B, 4])
        pick = s.sb("pick", [128, R, 4, P])
        ends = s.sb("ends", [P, HEADS + 1])
        found = s.sb("found", [P, HEADS])
        top = s.sb("top_n", [P, HEADS])
        lower = s.sb("lower", [P, R, 2, HEADS])
        factor = s.sb("factor", [P, R, 2, HEADS])
        scaled = s.sb("scaled", [P, R, ROW])
        ps = s.ps("ps_agg", [128, B, 512])
        ps_rows = s.ps("ps_rows", [128, 512])
        ps_back = s.ps("ps_back", [128, 512])
        self_in, self_done = s.sem("self_in"), s.sem("self_done")
        meta_in = s.sems("meta_in", R)
        g_in = s.sems("g_in", R)
        alpha_sum, alpha_ready, local_ready, alpha_turned = (s.sem(n) for n in (
            "alpha_sum", "alpha_ready", "local_ready", "alpha_turned"))
        ran, max_ready, max_turned, below_ready, ends_ready, weight_ready = (s.sem(n) for n in (
            "ran", "max_ready", "max_turned", "below_ready", "ends_ready", "weight_ready"))
        pick_ready, msg_ready, agg_ready = s.sem("pick_ready"), s.sem("msg_ready"), s.sem("agg_ready")
        node_steps, lower_ready, factor_ready, scaled_ready, merged = (s.sem(n) for n in (
            "node_steps", "lower_ready", "factor_ready", "scaled_ready", "merged"))
        block = s.block()
        groups = K.meta_d.rearrange("(g p i) r -> g p (i r)", p=128, i=4)
        pens = K.pen_d.rearrange("k (g n) -> g k n", n=EG)

        def walk(eng, batch):

            def body(it, first, n, end):
                for b in range(n):
                    last = end and b == n - 1
                    batch(it, first, b, None if last else (it, b + 1) if b + 1 < R else (it + 1, 0))

            body(0, True, R, False)
            with eng.Fori(1, full) as it:
                body(it, False, R, False)
            body(full, False, rest, True)

        @block.sync
        def _(sp):
            rows_split(sp, K.acc[:, :, :], K.h_d.rearrange("(t p) f -> p t f", p=P), self_in)

            def batch(it, first, b, ahead):
                for j in range(B):
                    i = (it * R + b) * B + j
                    t = sp.value_load(K.step_group[0:1, bass.ds(i, 1)], min_val=0, max_val=EDGE_GROUPS - 1)
                    if not first:
                        sp.wait_ge(agg_ready, i - (R * B - 1))
                    sp.dma_start(meta[:, b, j].rearrange("p i r -> p (i r)"), one(groups, t)).then_inc(meta_in[b], 16)
                    sp.dma_start(pen[j * HEADS:(j + 1) * HEADS, b], pens[bass.ds(t, 1)].to_broadcast([HEADS, 2, EG])
                                 ).then_inc(meta_in[b], 16)

            walk(sp, batch)

        @block.gpsimd
        def _(pool):
            def batch(it, first, b, ahead):
                pool.wait_ge(meta_in[b], it * (32 * B) + 32 * B)
                pool_gate(nc, K)
                for j in range(B):
                    if not first:
                        pool.wait_ge(agg_ready, (it * R + b) * B + (j + 1 - R * B))
                        pool_gate(nc, K)
                    for i in range(4):
                        nc.gpsimd.indirect_dma_start(
                            out=g[:, b, j, i, 0:ROW], out_offset=None, in_=K.h_d,
                            in_offset=bass.IndirectOffsetOnAxis(ap=meta[:, b, j, i, META - 1:META].bitcast(I32), axis=0),
                        ).then_inc(g_in[b], 16)

            walk(pool, batch)

        @block.vector
        def _(dve):
            v = nc.vector
            dve.wait_ge(self_in, 32)
            v.memset(K.acc[:, :, OUT:ROW:OUT + 1], 1.0).then_inc(self_done, 1)
            v.tensor_tensor(K.run_max[:], K.asd[:, :, 0:HEADS], K.asd[:, :, HEADS:], ALU.add).then_inc(self_done, 1)
            dve.wait_ge(self_done, 2)
            v.scalar_tensor_tensor(K.run_max[:], K.run_max[:], NEG_SLOPE, K.run_max[:], ALU.mult, ALU.max).then_inc(self_done, 1)
            dve.wait_ge(self_done, 3)

            def sum_alpha(it, b):
                k = it * R + b
                dve.wait_ge(g_in[b], it * (64 * B) + 64 * B)
                if not (isinstance(k, int) and k == 0):
                    dve.wait_ge(below_ready, k)
                v.tensor_tensor(alpha[:].rearrange("p i j h -> p j i h"), g[:, b, :, :, OUT:ROW:OUT + 1],
                                meta[:, b, :, :, 0:HEADS], ALU.add).then_inc(alpha_sum, 1)
                v.tensor_tensor(local[:, b], meta[:, b, :, :, HEADS + 1],
                                K.step_node[:, bass.ds(k * B, B)].rearrange("p (j a) -> p j a", a=1).to_broadcast([128, B, 4]),
                                ALU.subtract).then_inc(local_ready, 1)
                dve.wait_ge(alpha_sum, k + 1)
                v.scalar_tensor_tensor(alpha[:], alpha[:], NEG_SLOPE, alpha[:], ALU.mult, ALU.max).then_inc(alpha_ready, 1)

            def run_maxima(it, b):
                k = it * R + b
                rows = ps_rows[0:B * HEADS, :]
                dve.wait_ge(alpha_turned, k + 1)
                v.tensor_tensor_scan(run_on[:], pen[:, b, 0, :], rows, NEVER, ALU.add, ALU.max).then_inc(ran, 1)
                v.tensor_tensor_scan(run_back[:, ::-1], pen[:, b, 1, ::-1], rows[:, ::-1], NEVER,
                                     ALU.add, ALU.max).then_inc(ran, 1)
                dve.wait_ge(ran, k * 2 + 2)
                v.tensor_tensor(run_on[:], run_on[:], run_back[:], ALU.max).then_inc(max_ready, 1)

            def split_alpha(it, b):
                k = it * R + b
                back = ps_back[:, 0:4 * B * HEADS].rearrange("p (i j h) -> p i j h", i=4, j=B)
                dve.wait_ge(max_turned, k + 1)
                v.tensor_tensor(below[:], alpha[:], back, ALU.subtract).then_inc(below_ready, 1)
                last = meta[:, b, :, :, HEADS:HEADS + 1]
                v.tensor_tensor(g[:, b, :, :, ROW:ROW + HEADS], back.rearrange("p i j h -> p j i h"),
                                last.to_broadcast([128, B, 4, HEADS]), ALU.mult).then_inc(ends_ready, 1)
                v.tensor_scalar(g[:, b, :, :, ROW + HEADS:W], last, BIG, None, ALU.mult).then_inc(ends_ready, 1)

            def messages(it, first, b, j):
                i = (it * R + b) * B + j
                q = (b * B + j) % R
                if not (first and b * B + j < R):
                    dve.wait_ge(agg_ready, i - (R - 1))
                if j == 0:
                    dve.wait_ge(local_ready, it * R + b + 1)
                v.tensor_tensor(pick[:, q], K.iota_col[:, 0:P].rearrange("p (a n) -> p a n", a=1).to_broadcast([128, 4, P]),
                                local[:, b, j, :].rearrange("p (i a) -> p i a", a=1).to_broadcast([128, 4, P]),
                                ALU.is_equal).then_inc(pick_ready, 1)
                if j == 0:
                    dve.wait_ge(weight_ready, it * R + b + 1)
                rows = g[:, b, j, :, 0:ROW].rearrange("p i (h o) -> p i h o", h=HEADS)
                v.tensor_tensor(rows[:, :, :, 0:OUT], rows[:, :, :, 0:OUT],
                                rows[:, :, :, OUT:OUT + 1].to_broadcast([128, 4, HEADS, OUT]), ALU.mult).then_inc(msg_ready, 1)

            def maxima(i, n):
                tile = dve.value_load(K.step_tile[0:1, bass.ds(i, 1)], min_val=0, max_val=TILES - 1)
                m = K.run_max[:, bass.ds(tile, 1), :].rearrange("p a h -> p (a h)")
                got, q = ps[0:P, n % B], n % R
                dve.wait_ge(agg_ready, i + 1)
                v.tensor_copy(ends[:], got[:, ROW:W]).then_inc(node_steps, 1)
                dve.wait_ge(node_steps, i * 4 + 1)
                v.scalar_tensor_tensor(found[:], ends[:, HEADS:].to_broadcast([P, HEADS]), BIG, ends[:, 0:HEADS],
                                       ALU.subtract, ALU.add).then_inc(node_steps, 1)
                dve.wait_ge(node_steps, i * 4 + 2)
                v.tensor_tensor(top[:], found[:], m, ALU.max).then_inc(node_steps, 1)
                dve.wait_ge(node_steps, i * 4 + 3)
                v.tensor_tensor(lower[:, q, 0], m, top[:], ALU.subtract).then_inc(lower_ready, 1)
                v.tensor_tensor(lower[:, q, 1], found[:], top[:], ALU.subtract).then_inc(lower_ready, 1)
                dve.wait_ge(lower_ready, i * 2 + 2)
                v.tensor_tensor(m, top[:], found[:], ALU.max).then_inc(node_steps, 1)

            def merge(i, n):
                tile = dve.value_load(K.step_tile[0:1, bass.ds(i, 1)], min_val=0, max_val=TILES - 1)
                q = n % R
                dve.wait_ge(scaled_ready, i * HEADS + HEADS)
                if not (isinstance(i, int) and i == 0):
                    dve.wait_ge(merged, i * HEADS)
                for h in range(HEADS):
                    cols = slice(h * (OUT + 1), (h + 1) * (OUT + 1))
                    a = K.acc[:, bass.ds(tile, 1), cols].rearrange("p a f -> p (a f)")
                    v.scalar_tensor_tensor(a, a, factor[:, q, 0, h:h + 1], scaled[:, q, cols],
                                           ALU.mult, ALU.add).then_inc(merged, 1)

            sum_alpha(0, 0)
            run_maxima(0, 0)
            split_alpha(0, 0)

            def batch(it, first, b, ahead):
                if ahead:
                    sum_alpha(*ahead)
                for j in range(B):
                    i, n = (it * R + b) * B + j, b * B + j
                    messages(it, first, b, j)
                    if not (first and n < 2):
                        maxima(i - 2, n - 2)
                    if not (first and n < 3):
                        merge(i - 3, n - 3)
                    if ahead and j == 0:
                        run_maxima(*ahead)
                    if ahead and j == 1:
                        split_alpha(*ahead)

            walk(dve, batch)
            n = rest * B
            maxima(STEPS - 2, n - 2)
            merge(STEPS - 3, n - 3)
            maxima(STEPS - 1, n - 1)
            merge(STEPS - 2, n - 2)
            merge(STEPS - 1, n - 1)
            dve.wait_ge(merged, STEPS * HEADS)

        @block.scalar
        def _(act):
            def weights(it, b):
                k = it * R + b
                act.wait_ge(below_ready, k + 1)
                nc.scalar.activation(g[:, b, :, :, OUT:ROW:OUT + 1], below[:].rearrange("p i j h -> p j i h"),
                                     ACT.Exp).then_inc(weight_ready, 1)

            def scale(i, n, first):
                q = n % R
                act.wait_ge(lower_ready, i * 2 + 2)
                if not (first and n < R):
                    act.wait_ge(merged, i * HEADS - (R - 1) * HEADS)
                nc.scalar.activation(factor[:, q], lower[:, q], ACT.Exp).then_inc(factor_ready, 1)
                act.wait_ge(factor_ready, i + 1)
                for h in range(HEADS):
                    cols = slice(h * (OUT + 1), (h + 1) * (OUT + 1))
                    nc.scalar.activation(scaled[:, q, cols], ps[0:P, n % B, cols], ACT.Copy,
                                         scale=factor[:, q, 1, h:h + 1]).then_inc(scaled_ready, 1)

            weights(0, 0)

            def batch(it, first, b, ahead):
                if ahead:
                    weights(*ahead)
                for j in range(B):
                    scale((it * R + b) * B + j, b * B + j, first)

            walk(act, batch)

        @block.tensor
        def _(pe):
            rows_of = B * HEADS

            def turn_alpha(it, b, start):
                k = it * R + b
                pe.wait_ge(alpha_ready, k + 1)
                if not start:
                    pe.wait_ge(max_ready, k)
                for i in range(4):
                    mm = nc.tensor.transpose(ps_rows[0:rows_of, i:EG:4], alpha[:, i].rearrange("p j h -> p (j h)"), K.ident[:])
                mm.then_inc(alpha_turned, 1)

            def turn_maxima(it, b):
                k = it * R + b
                pe.wait_ge(max_ready, k + 1)
                for i in range(4):
                    mm = nc.tensor.matmul(ps_back[:, i * rows_of:(i + 1) * rows_of], run_on[:, i:EG:4],
                                          K.ident[0:rows_of, 0:rows_of], start=True, stop=True)
                mm.then_inc(max_turned, 1)

            turn_alpha(0, 0, True)
            turn_maxima(0, 0)

            def batch(it, first, b, ahead):
                if ahead:
                    turn_alpha(*ahead, False)
                for j in range(B):
                    i, n = (it * R + b) * B + j, b * B + j
                    q = n % R
                    pe.wait_ge(pick_ready, i + 1)
                    pe.wait_ge(msg_ready, i + 1)
                    if j == 0:
                        pe.wait_ge(ends_ready, (it * R + b) * 2 + 2)
                    if not (first and n < B):
                        pe.wait_ge(scaled_ready, i * HEADS - (B - 1) * HEADS)
                    for k in range(4):
                        mm = nc.tensor.matmul(ps[0:P, j, 0:W], pick[:, q, k, :], g[:, b, j, k, :], start=(k == 0), stop=(k == 3))
                    mm.then_inc(agg_ready, 1)
                    if ahead and j == 0:
                        turn_maxima(*ahead)

            walk(pe, batch)

def stage_tokens(nc, K, A):
    U = UNROLL
    with Scope(nc, "tokens") as s:
        bias = s.sb("bias_b", [P, 3, H])
        xin = s.sb("xin", [P, 3, 3, GT, H])
        y = s.sb("y_t", [P, GT, H])
        base = s.sb("base", [P, 2, GT, H])
        x1 = s.sb("x1", [P, 2, GT, H])
        rden = s.sb("rden", [P, GT, HEADS])
        gw = s.sb("gw", [128, HC, EXPERTS])
        gb = s.sb("gb", [P, EXPERTS])
        tokt = s.sb("tokt", [128, HC, GN])
        stats = s.sb("stats3", [P, GT, 6])
        mv = s.sb("mv3", [P, GT, 3])
        var = s.sb("var3", [P, GT])
        std = s.sb("std3", [P, GT])
        rstd = s.sb("rstd3", [P, GT])
        ps = s.ps("ps_tok", [128, 3, 512])
        w_in = s.sem("w_in3")
        x_in = s.sems("x_in3", 3)
        var_ready, std_ready = s.sem("var_ready3"), s.sem("std_ready3")
        base_half, base_ready, x1_ready, tok_ready = (s.sem(n) for n in ("base_half", "base_ready", "x1_ready", "tok_ready"))
        x1_out = s.sems("x1_out", 2)
        tok_psum, tokt_ready, log_psum, log_ready = (s.sem(n) for n in ("tok_psum", "tokt_ready", "log_psum", "log_ready"))
        dve_done = s.sem("dve_done4")
        block = s.block()
        grp = lambda a: a.rearrange("(g t p) f -> g p t f", p=P, t=GT)
        row = lambda a, n: a.rearrange("(a n) -> a n", a=1).to_broadcast([P, n])
        bcast = lambda a: a.rearrange("p (t f) -> p t f", t=1).to_broadcast([P, GT, H])

        @block.sync
        def _(sp):
            for k, a in enumerate((A.bias, A.gamma, A.beta)):
                sp.dma_start(bias[:, k, :], row(a, H)).then_inc(w_in, 16)
            sp.dma_start(gb[:, :], row(A.ffn_gate_b, EXPERTS)).then_inc(w_in, 16)
            sp.dma_start(gw[:], A.ffn_gate_w.rearrange("(c p) e -> p c e", p=128)).then_inc(w_in, 16)

            def load(g):
                for k, a in enumerate((K.xn_d, A.x, K.mix_d)):
                    rows_split(sp, xin[:, g % 3, k], grp(a)[g], x_in[g % 3])

            for g in range(3):
                load(g)
            for g in range(GROUPS):
                sp.wait_ge(x1_ready, g + 1)
                rows_split(sp, grp(K.x1_d)[g], x1[:, g % 2], x1_out[g % 2])
                if g + 3 < GROUPS:
                    load(g + 3)
            for b in range(2):
                sp.wait_ge(x1_out[b], 32 * ((GROUPS + 1 - b) // 2))

        @block.gpsimd
        def _(pool):
            pool.wait_ge(w_in, 80)
            for g in range(GROUPS):
                pool.wait_ge(x_in[g % 3], 96 * (g // 3 + 1))
                if g >= 2:
                    pool.wait_ge(x1_ready, g - 1)
                nc.gpsimd.tensor_tensor(base[:, g % 2], xin[:, g % 3, 1], xin[:, g % 3, 2], ALU.add).then_inc(base_half, 1)
                pool.wait_ge(base_half, g + 1)
                nc.gpsimd.tensor_tensor(base[:, g % 2], base[:, g % 2], bcast(bias[:, 2, :]), ALU.add).then_inc(base_ready, 1)

        @block.vector
        def _(dve):
            c = Chain(dve, dve_done)
            dve.wait_ge(w_in, 80)

            def logits(g):
                dve.wait_ge(log_psum, g + 1)
                nc.vector.tensor_tensor(K.logits[:, g * GT:(g + 1) * GT, :],
                                        ps[0:P, 2, 0:GT * EXPERTS].rearrange("p (t e) -> p t e", e=EXPERTS),
                                        gb[:].rearrange("p (a e) -> p a e", a=1).to_broadcast([P, GT, EXPERTS]),
                                        ALU.add).then_inc(log_ready, 1)

            for g in range(GROUPS):
                acc = K.acc[:, g * GT:(g + 1) * GT, :]
                c.did(nc.vector.reciprocal(rden[:], acc[:, :, OUT:ROW:OUT + 1]))
                c.settle()
                for t in range(GT):
                    c.did(nc.vector.tensor_tensor(y[:, t, :].rearrange("p (h o) -> p h o", h=HEADS),
                                                  heads(acc[:, t, :])[:, :, 0:OUT],
                                                  rden[:, t, :].rearrange("p (h o) -> p h o", o=1).to_broadcast([P, HEADS, OUT]),
                                                  ALU.mult))
                c.settle()
                c.did(nc.vector.tensor_tensor(y[:], y[:], bcast(bias[:, 0, :]), ALU.add))
                c.settle()
                dve.wait_ge(x_in[g % 3], 96 * (g // 3 + 1))
                c.did(nc.vector.scalar_tensor_tensor(y[:], y[:], 0.0, xin[:, g % 3, 0], ALU.max, ALU.add))
                c.settle()
                norm_stats(nc, c, y, stats, mv, var).then_inc(var_ready, 1)
                dve.wait_ge(std_ready, 2 * g + 1)
                for ins in norm_rows(nc, c, y, y, mv, std, rstd):
                    c.did(ins)
                c.settle()
                c.did(nc.vector.tensor_tensor(y[:], y[:], bcast(bias[:, 1, :]), ALU.mult))
                c.settle()
                dve.wait_ge(base_ready, g + 1)
                if g >= 2:
                    dve.wait_ge(x1_out[g % 2], 32 * (g // 2))
                nc.vector.tensor_tensor(x1[:, g % 2], y[:], base[:, g % 2], ALU.add).then_inc(x1_ready, 1)
                dve.wait_ge(x1_ready, g + 1)
                norm_stats(nc, c, x1[:, g % 2], stats, mv, var).then_inc(var_ready, 1)
                if g:
                    logits(g - 1)
                dve.wait_ge(std_ready, 2 * g + 2)
                for ins in norm_rows(nc, c, x1[:, g % 2], acc[:, :, 0:H], mv, std, rstd):
                    ins.then_inc(tok_ready, 1)
            logits(GROUPS - 1)

        @block.scalar
        def _(act):
            for g in range(GROUPS):
                for k in range(2):
                    act.wait_ge(var_ready, 2 * g + k + 1)
                    nc.scalar.activation(std[:, :], var[:, :], ACT.Sqrt).then_inc(std_ready, 1)
                act.wait_ge(tok_psum, g + 1)
                if g:
                    act.wait_ge(log_psum, g)
                nc.scalar.activation(tokt[:], ps[:, 0:2, 0:GN], ACT.Copy).then_inc(tokt_ready, 1)

        @block.tensor
        def _(pe):
            pe.wait_ge(w_in, 80)
            for g in range(GROUPS):
                pe.wait_ge(tok_ready, GT * (g + 1))
                if g:
                    pe.wait_ge(tokt_ready, g)
                for t in range(GT):
                    for k in range(HC):
                        mm = nc.tensor.transpose(ps[:, k, t * P:(t + 1) * P], K.acc[:, g * GT + t, k * 128:(k + 1) * 128],
                                                 K.ident[0:P, 0:P])
                mm.then_inc(tok_psum, 1)
                pe.wait_ge(tokt_ready, g + 1)
                if g:
                    pe.wait_ge(log_ready, g)
                for t in range(GT):
                    for k in range(HC):
                        mm = nc.tensor.matmul(ps[0:P, 2, t * EXPERTS:(t + 1) * EXPERTS], tokt[:, k, t * P:(t + 1) * P],
                                              gw[:, k, :], start=(k == 0), stop=(k == HC - 1))
                mm.then_inc(log_psum, 1)


def stage_route(nc, K):
    with Scope(nc, "route") as s:
        e = s.sb("e_r", [P, TILES, EXPERTS])
        one_hot = s.sb("one_hot", [P, TILES, EXPERTS])
        pos = s.sb("pos", [P, TILES, EXPERTS])
        tot = s.sb("tot", [P, TILES, EXPERTS])
        run = s.sb("run_r", [P, TILES, EXPERTS])
        top = s.sb("top", [P, TILES])
        tsum = s.sb("tsum", [P, TILES])
        inv = s.sb("inv", [P, TILES])
        best = s.sb("best", [P, TILES])
        slot = s.sb("slot", [P, TILES])
        kept = s.sb("kept", [P, TILES])
        rank = s.sb("rank", [P, EXPERTS])
        begin = s.sb("begin", [P, EXPERTS])
        ones = s.sb("ones_r", [P, P])
        ones_t = s.sb("ones_rt", [P, TILES])
        upto = s.sb("upto", [P, P])
        ps = s.ps("ps_route", [128, 4, 512])
        made = s.sem("made_r")
        arg_ready, e_ready, hot_ready, counted, slot_ready, tok_out = (s.sem(n) for n in (
            "arg_ready_r", "e_ready_r", "hot_ready", "counted_r", "slot_ready", "tok_out"))
        done = s.sem("dve_done5")
        block = s.block()
        per = lambda a: a.rearrange("p (t e) -> p t e", e=1).to_broadcast([P, TILES, EXPERTS])
        along = lambda a: a.rearrange("p (t e) -> p t e", t=1).to_broadcast([P, TILES, EXPERTS])

        @block.gpsimd
        def _(pool):
            nc.gpsimd.iota(rank[:], pattern=[[-1, EXPERTS]], base=EXPERTS, channel_multiplier=0,
                           allow_small_or_imprecise_dtypes=True).then_inc(made, 1)
            nc.gpsimd.iota(begin[:], pattern=[[CAP, EXPERTS]], base=-1, channel_multiplier=0,
                           allow_small_or_imprecise_dtypes=True).then_inc(made, 1)
            nc.gpsimd.memset(ones[:], 1.0).then_inc(made, 1)
            pool.wait_ge(made, 3)
            nc.gpsimd.affine_select(out=upto[:], in_=ones[:], compare_op=ALU.is_ge, fill=0.0, base=0,
                                    pattern=[[1, P]], channel_multiplier=-1).then_inc(made, 1)
            pool.wait_ge(slot_ready, 2)
            for t in range(TILES):
                nc.gpsimd.indirect_dma_start(
                    out=K.buf_d, out_offset=bass.IndirectOffsetOnAxis(ap=K.slot_i[:, t:t + 1], axis=0),
                    in_=K.acc[:, t, 0:TOKW], in_offset=None, bounds_check=SLOTS - 1, oob_is_err=False).then_inc(tok_out, 16)
            pool.wait_ge(tok_out, 16 * TILES)

        @block.scalar
        def _(act):
            act.wait_ge(arg_ready, 1)
            nc.scalar.activation(e[:], e[:], ACT.Exp).then_inc(e_ready, 1)

        @block.tensor
        def _(pe):
            pe.wait_ge(hot_ready, 1)
            flat = one_hot[:].rearrange("p t e -> p (t e)")
            half = TILES * EXPERTS // 2
            for k in range(2):
                nc.tensor.matmul(ps[0:P, k, 0:half], upto[:], flat[:, k * half:(k + 1) * half], start=True, stop=True)
                mm = nc.tensor.matmul(ps[0:P, 2 + k, 0:half], ones[:], flat[:, k * half:(k + 1) * half], start=True, stop=True)
            mm.then_inc(counted, 1)

        @block.vector
        def _(dve):
            c = Chain(dve, done)

            def step(ins):
                c.did(ins)
                c.settle()

            v = nc.vector
            c.did(v.memset(ones_t[:], 1.0))
            step(v.tensor_reduce(top[:], K.logits[:], X, ALU.max))
            v.tensor_tensor(e[:], K.logits[:], per(top[:]), ALU.subtract).then_inc(arg_ready, 1)
            dve.wait_ge(e_ready, 1)
            c.did(v.tensor_reduce(tsum[:], e[:], X, ALU.add))
            step(v.tensor_reduce(best[:], e[:], X, ALU.max))
            c.did(v.reciprocal(inv[:], tsum[:]))
            dve.wait_ge(made, 4)
            step(v.tensor_tensor(one_hot[:], e[:], per(best[:]), ALU.is_equal))
            step(v.tensor_tensor(one_hot[:], one_hot[:], along(rank[:]), ALU.mult))
            step(v.tensor_reduce(top[:], one_hot[:], X, ALU.max))
            c.did(v.tensor_tensor(best[:], best[:], inv[:], ALU.mult))
            v.tensor_tensor(one_hot[:], one_hot[:], per(top[:]), ALU.is_equal).then_inc(hot_ready, 1)
            c.settle()
            c.did(v.tensor_copy(K.acc[:, :, H:TOKW], best[:].rearrange("p (t e) -> p t e", e=1)))
            dve.wait_ge(counted, 1)
            halves = lambda a: a[:].rearrange("p (k t) e -> p k (t e)", k=2)
            c.did(v.tensor_copy(halves(pos), ps[0:P, 0:2, 0:TILES * EXPERTS // 2]))
            step(v.tensor_copy(halves(tot), ps[0:P, 2:4, 0:TILES * EXPERTS // 2]))
            for x in range(EXPERTS):
                c.did(v.tensor_tensor_scan(run[:, :, x], ones_t[:], tot[:, :, x], 0.0, ALU.mult, ALU.add))
            c.settle()
            step(v.tensor_tensor(run[:], run[:], tot[:], ALU.subtract))
            step(v.tensor_tensor(pos[:], pos[:], run[:], ALU.add))
            step(v.tensor_tensor(tot[:], pos[:], one_hot[:], ALU.mult))
            step(v.tensor_reduce(kept[:], tot[:], X, ALU.add))
            step(v.tensor_scalar(kept[:], kept[:], float(C_MAX), None, ALU.is_le))
            step(v.tensor_tensor(pos[:], pos[:], along(begin[:]), ALU.add))
            step(v.tensor_tensor(pos[:], pos[:], one_hot[:], ALU.mult))
            step(v.tensor_reduce(slot[:], pos[:], X, ALU.add))
            step(v.scalar_tensor_tensor(slot[:], slot[:], float(SLOTS), kept[:], ALU.subtract, ALU.mult))
            step(v.tensor_scalar(slot[:], slot[:], float(SLOTS), None, ALU.add))
            v.tensor_copy(K.slot_i[:], slot[:]).then_inc(slot_ready, 2)


def stage_experts(nc, K, A):
    FC = F // 128
    ring = 3
    per = 2 * CHUNKS
    n_turns = EXPERTS // 2
    with Scope(nc, "experts") as s:
        w1 = s.sb("w1", [128, 2, HC, F])
        w2 = s.sb("w2", [128, 2, FC, H])
        b1 = s.sb("b1", [128, 2, FC])
        b2 = s.sb("b2", [128, 2, H])
        rows = s.sb("rows_e", [128, per, 4, TOKW])
        bt = s.sb("bt", [128, 2, HC, 512])
        hm = s.sb("hm", [128, FC, 512])
        y = s.sb("y_e", [128, 2, 4, H])
        bad = s.sb("bad", [128, 4, H], I32)
        const = s.sb("const", [128, 3, 4, H])
        scrap = s.sb("scrap", [128, 2])
        ps = s.ps("ps_e", [128, 8, 512])
        w_in = s.sems("w_in4", 2)
        const_ready = s.sem("const_ready")
        rows_in = s.sems("rows_in4", per)
        bt_psum, bt_ready, h_psum, h_ready, y_psum, y_made, y_ready = (s.sem(n) for n in (
            "bt_psum", "bt_ready", "h_psum", "hm_ready", "y_psum", "y_made", "y_ready"))
        y_out = s.sems("y_out", 2)
        done = s.sem("dve_done6")
        block = s.block()
        bufc = K.buf_d.rearrange("(n t p) r -> n p t r", t=4, p=128)
        yc = K.y_d[0:SLOTS, :].rearrange("(n t p) r -> n p t r", t=4, p=128)

        @block.sync
        def _(sp):
            def weights(x, i):
                w1v = A.ffn_w1.rearrange("e (c p) f -> e p c f", p=128)
                w2v = A.ffn_w2.rearrange("e (c p) f -> e p c f", p=128)
                sp.dma_start(w1[:, i], one(w1v, x)).then_inc(w_in[i], 16)
                sp.dma_start(w2[:, i], one(w2v, x)).then_inc(w_in[i], 16)
                sp.dma_start(b2[:, i, :], A.ffn_b2[bass.ds(x, 1), :].to_broadcast([128, H])).then_inc(w_in[i], 16)
                with nc.allow_non_contiguous_dma(reason="b1 to columns"):
                    sp.dma_start(b1[:, i, :], one(A.ffn_b1.rearrange("e (f p) -> e p f", p=128), x)).then_inc(w_in[i], 16)

            weights(0, 0)
            for u in range(per):
                sp.dma_start(rows[:, u], bufc[u]).then_inc(rows_in[u], 16)
                if u == 0:
                    weights(1, 1)

            def body(it, more):
                for u in range(per):
                    j = it * per + u
                    sp.wait_ge(y_ready, j + 1)
                    sp.dma_start(one(yc, j), y[:, u % 2]).then_inc(y_out[u % 2], 16)
                    if more:
                        sp.dma_start(rows[:, u], one(bufc, j + per)).then_inc(rows_in[u], 16)
                        if u % CHUNKS == CHUNKS - 1:
                            weights(it * 2 + u // CHUNKS + 2, u // CHUNKS)

            with sp.Fori(0, n_turns - 1) as it:
                body(it, True)
            body(n_turns - 1, False)
            for b in range(2):
                sp.wait_ge(y_out[b], 16 * n_turns * CHUNKS)

        @block.tensor
        def _(pe):
            def turn_rows(it, u, first):
                pe.wait_ge(rows_in[u], it * 16 + 16)
                if not (first and u == 0):
                    pe.wait_ge(bt_ready, it * per + u)
                for t in range(4):
                    for k in range(HC):
                        mm = nc.tensor.transpose(ps[:, k, t * 128:(t + 1) * 128], rows[:, u, t, k * 128:(k + 1) * 128], K.ident[:])
                mm.then_inc(bt_psum, 1)

            def body(it, first):
                turn_rows(it, 0, first)
                for u in range(per):
                    j = it * per + u
                    x = u // CHUNKS
                    if u % CHUNKS == 0:
                        pe.wait_ge(w_in[x], it * 64 + 64)
                    pe.wait_ge(bt_ready, j + 1)
                    for f in range(FC):
                        i = j * FC + f
                        if not (first and i < 4):
                            pe.wait_ge(h_ready, i - 3)
                        for k in range(HC):
                            mm = nc.tensor.matmul(ps[:, 2 + f % 4, :], w1[:, x, k, f * 128:(f + 1) * 128], bt[:, u % 2, k, :],
                                                  start=(k == 0), stop=(k == HC - 1))
                        mm.then_inc(h_psum, 1)
                    if u < per - 1:
                        turn_rows(it, u + 1, first)
                    pe.wait_ge(h_ready, j * FC + FC)
                    if not (first and u == 0):
                        pe.wait_ge(y_made, j)
                    for t in range(4):
                        for f in range(FC):
                            mm = nc.tensor.matmul(ps[:, 6 + t // 2, (t % 2) * H:(t % 2 + 1) * H], hm[:, f, t * 128:(t + 1) * 128],
                                                  w2[:, x, f, :], start=(f == 0), stop=(f == FC - 1))
                    mm.then_inc(y_psum, 1)

            turns(pe, n_turns, body)

        @block.scalar
        def _(act):
            def body(it, first):
                for u in range(per):
                    j = it * per + u
                    for f in range(FC):
                        i = j * FC + f
                        act.wait_ge(h_psum, i + 1)
                        if f == 0 and not (first and u == 0):
                            act.wait_ge(y_psum, j)
                        if f == 0 and u % CHUNKS == 0:
                            act.wait_ge(w_in[u // CHUNKS], it * 64 + 64)
                        nc.scalar.activation(hm[:, f, :], ps[:, 2 + f % 4, :], ACT.Relu,
                                             bias=b1[:, u // CHUNKS, f:f + 1]).then_inc(h_ready, 1)

            turns(act, n_turns, body)

        @block.vector
        def _(dve):
            for k, x in enumerate((0.0, 1e4, -1e4)):
                nc.vector.memset(const[:, k], x).then_inc(const_ready, 1)
            nc.vector.memset(scrap[:], 0.0).then_inc(const_ready, 1)
            dve.wait_ge(const_ready, 4)

            def turn_copy(it, u, first):
                j = it * per + u
                dve.wait_ge(bt_psum, j + 1)
                nc.vector.tensor_copy(bt[:, u % 2], ps[:, 0:2, :]).then_inc(bt_ready, 1)

            def body(it, first):
                c = Chain(dve, done, per * 12, it)

                def carry_wait():
                    c.settle()
                    c.did(nc.vector.tensor_copy(scrap[:, 0:1], scrap[:, 1:2]))

                turn_copy(it, 0, first)
                for u in range(per):
                    j = it * per + u
                    if u < per - 1:
                        turn_copy(it, u + 1, first)
                    dve.wait_ge(y_psum, j + 1)
                    if u % CHUNKS == 0:
                        dve.wait_ge(w_in[u // CHUNKS], it * 64 + 64)
                    if not (first and u < 2):
                        dve.wait_ge(y_out[u % 2], it * (16 * CHUNKS) + u // 2 * 16)
                    yu = y[:, u % 2]
                    nc.vector.tensor_tensor(yu.rearrange("p (a b) f -> p a b f", a=2),
                                            ps[:, 6:8, :].rearrange("p a (b f) -> p a b f", b=2),
                                            b2[:, u // CHUNKS, :].rearrange("p (a b f) -> p a b f", a=1, b=1).to_broadcast([128, 2, 2, H]),
                                            ALU.add).then_inc(y_made, 1)
                    dve.wait_ge(y_made, j + 1)
                    for t in range(4):
                        c.did(nc.vector.tensor_scalar(yu[:, t, :], yu[:, t, :], rows[:, u, t, H:TOKW], None, ALU.mult))
                    c.settle()
                    c.did(nc.vector.tensor_tensor(bad[:], yu, yu, ALU.not_equal))
                    carry_wait()
                    c.did(nc.vector.copy_predicated(yu, bad[:], const[:, 0]))
                    c.settle()
                    c.did(nc.vector.tensor_scalar(bad[:], yu, FLT_MAX, None, ALU.is_gt))
                    carry_wait()
                    c.did(nc.vector.copy_predicated(yu, bad[:], const[:, 1]))
                    c.settle()
                    c.did(nc.vector.tensor_scalar(bad[:], yu, -FLT_MAX, None, ALU.is_lt))
                    carry_wait()
                    nc.vector.copy_predicated(yu, bad[:], const[:, 2]).then_inc(y_ready, 1)
                c.close()

            turns(dve, n_turns, body)


def stage_output(nc, K, A):
    U = UNROLL
    with Scope(nc, "output") as s:
        x1 = s.sb("x1_o", [P, U, GT, H])
        y = s.sb("y_o", [P, U, GT, H])
        x_in = s.sems("x_in5", U)
        y_in = s.sems("y_in5", U)
        o_ready = s.sem("o_ready")
        o_out = s.sems("o_out", U)
        block = s.block()
        grp = lambda a: a.rearrange("(g t p) f -> g p t f", p=P, t=GT)

        @block.sync
        def _(sp):
            for g in range(U):
                rows_split(sp, x1[:, g], grp(K.x1_d)[g], x_in[g])
            for g in range(GROUPS):
                sp.wait_ge(o_ready, g + 1)
                rows_split(sp, grp(A.out)[g], x1[:, g % U], o_out[g % U])
                if g + U < GROUPS:
                    sp.wait_ge(o_out[g % U], 32 * (g // U + 1))
                    rows_split(sp, x1[:, g % U], grp(K.x1_d)[g + U], x_in[g % U])
            for u in range(U):
                sp.wait_ge(o_out[u], 32 * TURNS)

        @block.gpsimd
        def _(pool):
            for g in range(GROUPS):
                if g >= U:
                    pool.wait_ge(o_ready, g - U + 1)
                for t in range(GT):
                    i = g * GT + t
                    nc.gpsimd.indirect_dma_start(
                        out=y[:, g % U, t, :], out_offset=None, in_=K.y_d,
                        in_offset=bass.IndirectOffsetOnAxis(ap=K.slot_i[:, i:i + 1], axis=0)).then_inc(y_in[g % U], 16)

        @block.vector
        def _(dve):
            for g in range(GROUPS):
                dve.wait_ge(x_in[g % U], 32 * (g // U + 1))
                dve.wait_ge(y_in[g % U], 64 * (g // U + 1))
                nc.vector.tensor_tensor(x1[:, g % U], x1[:, g % U], y[:, g % U], ALU.add).then_inc(o_ready, 1)


class Shared:
    pass


class Arguments:

    def __init__(self, aps, out):
        self.x = aps["x"]
        self.src = aps["src"]
        self.dst = aps["dst"]
        self.W = aps["L0_gnn_W"]
        self.att_src = aps["L0_gnn_att_src"]
        self.att_dst = aps["L0_gnn_att_dst"]
        self.bias = aps["L0_gnn_bias"]
        self.gamma = aps["L0_gnn_gamma"]
        self.beta = aps["L0_gnn_beta"]
        self.mix_Wqkv = aps["L0_mix_Wqkv"]
        self.mix_Wproj = aps["L0_mix_Wproj"]
        self.mix_bproj = aps["L0_mix_bproj"]
        self.mix_ln_g = aps["L0_mix_ln_g"]
        self.mix_ln_b = aps["L0_mix_ln_b"]
        self.mix_Wg1 = aps["L0_mix_Wg1"]
        self.mix_bg1 = aps["L0_mix_bg1"]
        self.mix_Wg2 = aps["L0_mix_Wg2"]
        self.mix_bg2 = aps["L0_mix_bg2"]
        self.ffn_gate_w = aps["L0_ffn_gate_w"]
        self.ffn_gate_b = aps["L0_ffn_gate_b"]
        self.ffn_w1 = aps["L0_ffn_w1"]
        self.ffn_b1 = aps["L0_ffn_b1"]
        self.ffn_w2 = aps["L0_ffn_w2"]
        self.ffn_b2 = aps["L0_ffn_b2"]
        self.out = out


def gps_layer(nc, A, kind="Internal"):
    K = Shared()
    made = {}

    def dram(name, shape, dt=F32):
        made[name] = nc.dram_tensor(name, shape, dt, kind=kind).ap()
        return made[name]

    K.xn_d = dram("xn_d", [N, H])
    K.xt_d = dram("xt_d", [GROUPS, 128, HC * GN])
    K.h_d = dram("h_d", [N, ROW])
    K.dst_d = dram("dst_d", [DST_ROWS * FAN], I32)
    K.src_d = dram("src_d", [EP], I32)
    K.top_d = dram("top_d", [PIVOTS, FAN], I32)
    K.rp_d = dram("rp_d", [N + 1])
    K.gt_d = dram("gt_d", [GROUPS, 128, HC * GN])
    K.mix_d = dram("mix_d", [N, H])
    K.rec_d = dram("rec_d", [EP, HEADS])
    K.pen_d = dram("pen_d", [2, EP])
    K.meta_d = dram("meta_d", [EP, META])
    K.x1_d = dram("x1_d", [N, H])
    K.buf_d = dram("buf_d", [SLOTS, TOKW])
    K.y_d = dram("y_d", [SLOTS + 1, H])
    with Scope(nc, "gps_layer") as s:
        K.ident = s.sb("ident", [128, 128])
        K.iota_col = s.sb("iota_col", [128, 128])
        K.gate = s.sem("gate")
        K.node_id = s.sb("node_id", [P, TILES])
        K.asd = s.sb("asd", [P, TILES, 2 * HEADS])
        K.rend = s.sb("rend", [P, TILES])
        K.step_node = s.sb("step_node", [128, STEPS])
        K.step_tile = s.sb("step_tile", [1, STEPS], I32)
        K.step_group = s.sb("step_group", [1, STEPS], I32)
        K.firsti = s.sb("firsti", [P, TILES], I32)
        constants(nc, K)
        stage_embed(nc, K, A)
        stage_steps(nc, K)
        zero_fill(nc, K)
        stage_mix(nc, K, A)
        stage_edges(nc, K)
        K.slot_i = s.sb("slot_i", [P, TILES], I32)
        with Scope(nc, "gps_layer") as t:
            K.acc = t.sb("acc", [P, TILES, ROW])
            K.run_max = t.sb("run_max", [P, TILES, HEADS])
            K.logits = t.sb("logits", [P, TILES, EXPERTS])
            stage_aggregate(nc, K)
            stage_tokens(nc, K, A)
            stage_route(nc, K)
        stage_experts(nc, K, A)
        stage_output(nc, K, A)


_INS = ["x", "src", "dst", "L0_gnn_W", "L0_gnn_att_src", "L0_gnn_att_dst", "L0_gnn_bias", "L0_gnn_gamma",
        "L0_gnn_beta", "L0_mix_Wqkv", "L0_mix_Wproj", "L0_mix_bproj", "L0_mix_ln_g", "L0_mix_ln_b",
        "L0_mix_Wg1", "L0_mix_bg1", "L0_mix_Wg2", "L0_mix_bg2", "L0_ffn_gate_w", "L0_ffn_gate_b",
        "L0_ffn_w1", "L0_ffn_b1", "L0_ffn_w2", "L0_ffn_b2"]


def kernel(**inputs):
    import concourse.bacc as bacc
    from concourse.bass_utils import run_bass_kernel_spmd

    nc = bacc.Bacc("TRN2", target_bir_lowering=False, num_devices=1)
    arrays, aps = {}, {}
    for name in _INS:
        a = np.ascontiguousarray(inputs[name])
        arrays[f"in_{name}"] = a
        aps[name] = nc.dram_tensor(f"in_{name}", a.shape, mybir.dt.from_np(a.dtype), kind="ExternalInput").ap()
    out = nc.dram_tensor("out", [N, H], F32, kind="ExternalOutput").ap()
    A = Arguments(aps, out)
    gps_layer(nc, A)
    r = run_bass_kernel_spmd(nc, [arrays], core_ids=[0])
    return r.results[0]["out"]
```

```python
from contextlib import ExitStack

import numpy as np

import concourse.bass as bass
from concourse import mybir

F32 = mybir.dt.float32
BF16 = mybir.dt.bfloat16
I32 = mybir.dt.int32
ALU = mybir.AluOpType
ACT = mybir.ActivationFunctionType
X = mybir.AxisListType.X

N, H, E = 12500, 256, 200000
HEADS, OUT = 4, 64
NEG_SLOPE, EPS = 0.2, 1e-5

P = 125
TILES = N // P
GT = 4
GROUPS = TILES // GT
GN = GT * P
UNROLL = 5
TURNS = GROUPS // UNROLL
HC = H // 128
HW = H + 2 * HEADS
ROW = H + HEADS


def rows_split(eng, out, in_, sem):
    eng.dma_start(out[0:112], in_[0:112]).then_inc(sem, 16)
    eng.dma_start(out[112:P], in_[112:P]).then_inc(sem, 16)


EG = 512
EDGE_GROUPS = -(-E // EG)
EP = EDGE_GROUPS * EG
EC = EP // 128
NO_NODE = 16383
FAN = 64
DST_ROWS = -(-EP // (FAN * FAN)) * FAN
PIVOTS = DST_ROWS // FAN
CHUNK = TILES // TURNS
STEPS = EDGE_GROUPS + TILES - 1
STEP_BATCH = 5
BATCHES = STEPS // STEP_BATCH
META = HEADS + 3
NEVER = -1e30

EXPERTS, F = 8, 1024
C_MAX = -(-5 * N // (4 * EXPERTS))
CAP = -(-C_MAX // 512) * 512
SLOTS = EXPERTS * CAP
CHUNKS = CAP // 512
TOKW = H + 1
FLT_MAX = float(np.finfo(np.float32).max)


def pool_gate(nc, K):
    nc.gpsimd.sem_inc(K.gate, 1)


class Chain:

    def __init__(self, eng, sem, per=0, turn=0):
        self.eng, self.sem, self.per, self.turn, self.n = eng, sem, per, turn, 0

    def did(self, ins):
        ins.then_inc(self.sem, 1)
        self.n += 1
        return self.n

    def value(self, n):
        return self.turn * self.per + n if self.per else n

    def settle(self, n=None):
        self.eng.wait_ge(self.sem, self.value(self.n if n is None else n))

    def close(self):
        assert self.n == self.per, (self.n, self.per)


class Scope:

    def __init__(self, nc, stage):
        self.nc, self.stage, self.ctx, self.held = nc, stage, ExitStack(), []

    def __enter__(self):
        return self

    def __exit__(self, *a):
        self.ctx.__exit__(*a)
        if self.held and a[0] is None:
            self.nc.clear_and_free_semaphores(self.held)
            self.nc.all_engine_barrier()

    def sb(self, name, shape, dt=F32):
        return self.ctx.enter_context(self.nc.sbuf_tensor(f"{self.stage}_{name}", shape, dt))

    def ps(self, name, shape, dt=F32):
        return self.ctx.enter_context(self.nc.psum_tensor(f"{self.stage}_{name}", shape, dt))

    def sem(self, name):
        self.held.append(self.nc.alloc_semaphore(f"{self.stage}_{name}"))
        return self.held[-1]

    def sems(self, name, n):
        return [self.sem(f"{name}{i}") for i in range(n)]

    def block(self):
        return self.ctx.enter_context(self.nc.Block())


def constants(nc, K):
    with Scope(nc, "constants") as s:
        made = s.sem("made")
        block = s.block()

        @block.gpsimd
        def _(pool):
            c = Chain(pool, made)
            c.did(nc.gpsimd.memset(K.ident[:], 0.0))
            c.settle()
            c.did(nc.gpsimd.affine_select(out=K.ident[:], in_=K.ident[:], compare_op=ALU.not_equal, fill=1.0,
                                          base=0, pattern=[[-1, 128]], channel_multiplier=1))
            c.did(nc.gpsimd.iota(K.iota_col[:], pattern=[[1, 128]], base=0, channel_multiplier=0,
                                 allow_small_or_imprecise_dtypes=True))
            c.did(nc.gpsimd.iota(K.node_id[:], pattern=[[P, TILES]], base=0, channel_multiplier=1,
                                 allow_small_or_imprecise_dtypes=True))
            c.settle()



def norm_stats(nc, c, x, stats, mv, var):
    for t in range(GT):
        c.did(nc.vector.bn_stats(stats[:, t, :], x[:, t, :]))
    c.settle()
    nc.vector.tensor_copy(mv[:, 0, 2:3], stats[:, 0, 1:2])
    for t in range(GT):
        c.did(nc.vector.bn_aggr(mv[:, t, 0:2], stats[:, t, :]))
    c.settle()
    return nc.vector.tensor_scalar(var[:, :], mv[:, :, 1], EPS, None, ALU.add)


def norm_rows(nc, c, x, out, mv, std, rstd):
    c.did(nc.vector.reciprocal(rstd[:, :], std[:, :]))
    c.settle()
    return [nc.vector.tensor_scalar(out[:, t, :], x[:, t, :], mv[:, t, 0:1], rstd[:, t:t + 1],
                                    ALU.subtract, ALU.mult) for t in range(GT)]


def turns(eng, n, body):
    body(0, True)
    if n > 1:
        with eng.Fori(1, n) as it:
            body(it, False)


def one(ap, i):
    if isinstance(i, int):
        return ap[i]
    v = ap[bass.ds(i, 1)]
    names = " ".join(f"d{k}" for k in range(len(v.shape)))
    rest = names.split(" ")[1:]
    return v.rearrange(f"{names} -> ({'d0 ' + rest[0]}) {' '.join(rest[1:])}")


def heads(a):
    return a.rearrange("p (h o) -> p h o", h=HEADS)


class EdgeTables:

    def __init__(self, nc, K, s):
        self.nc, self.K = nc, K
        self.fill = s.sb("fill", [1, DST_ROWS * FAN - E], I32)
        self.zeros = s.sb("zeros", [128, HEADS * EC])
        self.made = s.sem("fill_made")
        self.stored = s.sem("tables_stored")

    def run(self, pool, A):
        nc, K = self.nc, self.K
        pool.dma_start(K.dst_d[0:E], A.dst).then_inc(self.stored, 16)
        pool.dma_start(K.src_d[0:E], A.src).then_inc(self.stored, 16)
        nc.gpsimd.memset(self.fill[:], NO_NODE).then_inc(self.made, 1)
        nc.gpsimd.memset(self.zeros[:], 0.0).then_inc(self.made, 1)
        pool.wait_ge(self.made, 2)
        zero = self.zeros[0:1, :]
        pool.dma_start(K.dst_d[E:DST_ROWS * FAN].rearrange("(a n) -> a n", a=1), self.fill[:, :]).then_inc(self.stored, 16)
        pool.dma_start(K.src_d[E:EP].rearrange("(a n) -> a n", a=1), zero[:, 0:EP - E].bitcast(I32)).then_inc(self.stored, 16)
        pool.dma_start(K.rp_d[0:1].rearrange("(a n) -> a n", a=1), zero[:, 0:1]).then_inc(self.stored, 16)
        pool.dma_start(K.y_d[SLOTS:SLOTS + 1, :], zero[:, 0:H]).then_inc(self.stored, 16)
        pool.dma_start(K.rec_d.rearrange("(p j) r -> p (j r)", p=128), self.zeros[:, :]).then_inc(self.stored, 16)
        pool.wait_ge(self.stored, 112)
        with nc.allow_non_contiguous_dma(reason="first entries of rows, once"):
            pool.dma_start(K.top_d, K.dst_d.rearrange("(a b c) -> a b c", b=FAN, c=FAN)[:, :, 0]).then_inc(self.stored, 16)
            pool.dma_start(K.piv_d, K.dst_d.rearrange("(a n) -> a n", n=FAN * FAN)[:, 0]).then_inc(self.stored, 16)
        pool.wait_ge(self.stored, 144)


class EdgeSearch:

    ZERO = 4096
    STEPS = 37

    def __init__(self, nc, K, s):
        self.nc, self.K = nc, K
        self.piv = s.sb("piv", [P, PIVOTS], I32)
        self.nid1 = s.sb("nid1", [P, TILES])
        self.node = s.sb("node_b", [P, CHUNK])
        self.less = s.sb("less", [P, CHUNK, FAN])
        self.cnt = s.sb("cnt", [P, CHUNK])
        self.row = s.sb("row", [P, CHUNK])
        self.idx = s.sb("idx", [P, 2, CHUNK], I32)
        self.got = s.sb("got", [P, 2, CHUNK, FAN], I32)
        self.rend = s.sb("rend", [P, TILES])
        self.rstart = s.sb("rstart", [P, TILES])
        self.first = s.sb("first", [P, TILES])
        self.first_idx = s.sb("first_idx", [P, CHUNK], I32)
        self.a_d = s.sb("a_d_rows", [P, CHUNK, HEADS])
        self.zeros = s.sb("zeros_b", [128, self.ZERO])
        self.piv_in = s.sem("piv_in")
        self.rows_in = s.sems("rows_in", 2)
        self.done = s.sem("pool_done")
        self.search_done = s.sem("search_done")
        self.ends_out, self.starts_in = s.sem("ends_out"), s.sem("starts_in")
        self.copied = s.sem("first_copied")
        self.rec_out = s.sem("rec_out")
        self.zero_out = s.sem("zero_out")

    def search(self, pool):
        nc, K, g = self.nc, self.K, self.nc.gpsimd
        dst = K.dst_d.rearrange("(r f) -> r f", f=FAN)
        spread = lambda a, n: a.rearrange("p (t f) -> p t f", f=1).to_broadcast([P, CHUNK, n])

        def body(it, first):
            c = Chain(pool, self.search_done, self.STEPS, it)

            def step(ins):
                c.did(ins)
                c.settle()
                pool_gate(nc, K)

            step(g.tensor_copy(self.node[:], self.nid1[:, bass.ds(it * CHUNK, CHUNK)]))
            for level in range(3):
                if level:
                    pool.wait_ge(self.rows_in[level - 1], it * (16 * CHUNK) + 16 * CHUNK)
                    pool_gate(nc, K)
                    entries, n = self.got[:, level - 1], FAN
                else:
                    entries, n = self.piv[:, :].rearrange("p (a f) -> p a f", a=1).to_broadcast([P, CHUNK, PIVOTS]), PIVOTS
                less = self.less[:, :, 0:n]
                step(g.tensor_copy(less, entries))
                step(g.tensor_tensor(less, spread(self.node[:], n), less, ALU.subtract))
                step(g.tensor_scalar(less, less, 0.0, 1.0, ALU.max, ALU.min))
                while n > 1:
                    half = n // 2
                    step(g.tensor_tensor(self.less[:, :, 0:half], self.less[:, :, 0:half], self.less[:, :, n - half:n], ALU.add))
                    n -= half
                count = self.less[:, :, 0]
                if level == 2:
                    break
                step(g.tensor_scalar(self.cnt[:, :], count, 1.0, 0.0, ALU.subtract, ALU.max))
                if level == 0:
                    step(g.tensor_copy(self.row[:], self.cnt[:]))
                else:
                    step(g.tensor_scalar(self.row[:], self.row[:], float(FAN), None, ALU.mult))
                    step(g.tensor_tensor(self.row[:], self.row[:], self.cnt[:], ALU.add))
                step(g.tensor_copy(self.idx[:, level, :], self.row[:, :]))
                for t in range(CHUNK):
                    g.indirect_dma_start(
                        out=self.got[:, level, t, :], out_offset=None, in_=K.top_d if level == 0 else dst,
                        in_offset=bass.IndirectOffsetOnAxis(ap=self.idx[:, level, t:t + 1], axis=0),
                    ).then_inc(self.rows_in[level], 16)
            step(g.tensor_scalar(self.row[:], self.row[:], float(FAN), None, ALU.mult))
            step(g.tensor_tensor(self.rend[:, bass.ds(it * CHUNK, CHUNK)], self.row[:], count, ALU.add))
            c.close()

        turns(pool, TURNS, body)

    def run(self, pool):
        nc, K, g = self.nc, self.K, self.nc.gpsimd
        pool.dma_start(self.piv[:, :], K.piv_d.rearrange("(a r) -> a r", a=1).to_broadcast([P, PIVOTS])).then_inc(self.piv_in, 16)
        c = Chain(pool, self.done)

        def step(ins):
            c.did(ins)
            c.settle()

        c.did(g.memset(self.zeros[:], 0.0))
        step(g.tensor_scalar(self.nid1[:], K.node_id[:], 1.0, None, ALU.add))
        pool.wait_ge(self.piv_in, 16)
        self.search(pool)
        with nc.allow_non_contiguous_dma(reason="one number of each node, once"):
            after = K.rp_d[1:N + 1].rearrange("(t p) -> p t", p=P)
            for t in range(0, TILES, CHUNK):
                pool.dma_start(after[:, t:t + CHUNK], self.rend[:, t:t + CHUNK]).then_inc(self.ends_out, 16)
            flat = K.buf_d.rearrange("(p j) r -> p (j r)", p=128)
            n = SLOTS // 128 * TOKW
            count = 0
            for k in range(0, n, self.ZERO):
                w = min(self.ZERO, n - k)
                pool.dma_start(flat[:, k:k + w], self.zeros[:, 0:w]).then_inc(self.zero_out, 16)
                count += 16
            pool.wait_ge(self.ends_out, 16 * TURNS)
            before = K.rp_d[0:N].rearrange("(t p) -> p t", p=P)
            for t in range(0, TILES, CHUNK):
                pool.dma_start(self.rstart[:, t:t + CHUNK], before[:, t:t + CHUNK]).then_inc(self.starts_in, 16)
        pool.wait_ge(self.starts_in, 16 * TURNS)
        step(g.tensor_tensor(self.first[:], self.rend[:], self.rstart[:], ALU.subtract))
        step(g.tensor_scalar(self.first[:], self.first[:], 1.0, None, ALU.min))
        step(g.tensor_scalar(self.first[:], self.first[:], -4194304.0, 4194304.0, ALU.mult, ALU.add))
        step(g.tensor_tensor(self.first[:], self.first[:], self.rstart[:], ALU.add))

        def body(it, first):
            chunk = bass.ds(it * CHUNK, CHUNK)
            g.tensor_copy(self.first_idx[:], self.first[:, chunk]).then_inc(self.copied, 1)
            g.tensor_copy(self.a_d[:], K.asd[:, chunk, HEADS:]).then_inc(self.copied, 1)
            pool.wait_ge(self.copied, it * 2 + 2)
            pool_gate(nc, K)
            for t in range(CHUNK):
                g.indirect_dma_start(
                    out=K.rec_d, out_offset=bass.IndirectOffsetOnAxis(ap=self.first_idx[:, t:t + 1], axis=0),
                    in_=self.a_d[:, t, :], in_offset=None, bounds_check=EP - 1, oob_is_err=False).then_inc(self.rec_out, 16)
            pool.wait_ge(self.rec_out, it * (16 * CHUNK) + 16 * CHUNK)
            pool_gate(nc, K)

        turns(pool, TURNS, body)
        pool.wait_ge(self.zero_out, count)


def stage_steps(nc, K):
    with Scope(nc, "steps") as s:
        start = s.sb("start", [TILES, 1])
        part = s.sb("part", [TILES, 1])
        thr = s.sb("thr", [TILES, 1])
        ends = s.sb("ends", [TILES, STEPS])
        reach = s.sb("reach", [TILES, STEPS])
        ones = s.sb("ones_t", [TILES, 128])
        stepf = s.sb("stepf", [1, STEPS])
        group = s.sb("groupf", [1, STEPS])
        ps = s.ps("ps_steps", [128, 512])
        made = s.sem("made")
        loaded = s.sem("loaded")
        reach_ready = s.sem("reach_ready")
        entered = s.sem("entered")
        dve_done = s.sem("dve_done")
        block = s.block()

        @block.gpsimd
        def _(pool):
            nc.gpsimd.iota(ends[:], pattern=[[EG, STEPS]], base=EG, channel_multiplier=0,
                           allow_small_or_imprecise_dtypes=True).then_inc(made, 1)
            nc.gpsimd.iota(part[:], pattern=[[0, 1]], base=0, channel_multiplier=EG,
                           allow_small_or_imprecise_dtypes=True).then_inc(made, 1)
            nc.gpsimd.iota(stepf[:], pattern=[[1, STEPS]], base=0, channel_multiplier=0,
                           allow_small_or_imprecise_dtypes=True).then_inc(made, 1)

        @block.sync
        def _(sp):
            with nc.allow_non_contiguous_dma(reason="one number of each tile, once"):
                sp.dma_start(start[:, :], K.rp_d[0:N].rearrange("(t p) -> t p", p=P)[:, 0:1]).then_inc(loaded, 16)

        @block.tensor
        def _(pe):
            pe.wait_ge(reach_ready, 1)
            nc.tensor.matmul(ps[:, 0:STEPS], ones[:], reach[:], start=True, stop=True).then_inc(entered, 1)

        @block.vector
        def _(dve):
            c = Chain(dve, dve_done)
            c.did(nc.vector.memset(ones[:], 1.0))
            dve.wait_ge(made, 3)
            dve.wait_ge(loaded, 16)
            c.did(nc.vector.tensor_tensor(thr[:], start[:], part[:], ALU.add))
            c.settle()
            nc.vector.tensor_scalar(reach[:], ends[:], thr[:, 0:1], None, ALU.is_gt).then_inc(reach_ready, 1)
            dve.wait_ge(entered, 1)
            c.did(nc.vector.tensor_scalar(K.step_node[:, :], ps[:, 0:STEPS], float(P), float(P), ALU.mult, ALU.subtract))
            c.did(nc.vector.tensor_scalar(K.step_tile[:, :], ps[0:1, 0:STEPS], 1.0, None, ALU.subtract))
            c.did(nc.vector.tensor_tensor(group[:, :], stepf[0:1, :], ps[0:1, 0:STEPS], ALU.subtract))
            c.settle()
            c.did(nc.vector.tensor_scalar(K.step_group[:, :], group[:, :], 1.0, None, ALU.add))
            c.settle()


def stage_embed(nc, K, A):
    U = UNROLL
    with Scope(nc, "embed") as s:
        wx = s.sb("wx", [128, HC, HW])
        att = s.sb("att", [128, 2, H])
        wtmp = s.sb("wtmp", [128, HC, 2, H])
        x = s.sb("x_in", [P, U, GT, H])
        xn = s.sb("xn", [P, U, GT, H])
        xt = s.sb("xt", [128, U, HC, GN])
        hs = s.sb("hs", [P, U, GT, ROW])
        stats = s.sb("stats", [P, GT, 6])
        mv = s.sb("mv", [P, GT, 3])
        var = s.sb("var", [P, GT])
        std = s.sb("std", [P, GT])
        rstd = s.sb("rstd", [P, GT])
        tp = s.ps("tp", [128, 2, HC, 512])
        hp = s.ps("hp", [128, GT, 512])
        w_in = s.sem("w_in")
        wx_ready = s.sem("wx_ready")
        x_in = s.sems("x_in", U)
        var_ready = s.sem("var_ready")
        std_ready = s.sem("std_ready")
        xn_ready = s.sem("xn_ready")
        xn_out = s.sems("xn_out", U)
        tp_ready = s.sem("tp_ready")
        xt_ready = s.sem("xt_ready")
        xt_out = s.sems("xt_out", U)
        h_ready = s.sem("h_ready")
        hs_ready = s.sem("hs_ready")
        h_out = s.sems("h_out", U)
        asd_ready = s.sem("asd_ready")
        dve_done = s.sem("dve_done")
        block = s.block()
        xg = A.x.rearrange("(g t p) f -> g p t f", p=P, t=GT)
        xng = K.xn_d.rearrange("(g t p) f -> g p t f", p=P, t=GT)
        hg = K.h_d.rearrange("(g t p) f -> g p t f", p=P, t=GT)
        tables = EdgeTables(nc, K, s)

        @block.gpsimd
        def _(pool):
            tables.run(pool, A)

        @block.sync
        def _(sp):
            for c in range(HC):
                sp.dma_start(heads(wx[:, c, 0:ROW])[:, :, 0:OUT],
                             A.W[c * 128:(c + 1) * 128, :].rearrange("p (h o) -> p h o", o=OUT)).then_inc(w_in, 16)
            for k, a in enumerate((A.att_src, A.att_dst)):
                sp.dma_start(att[:, k, :], a.rearrange("(a h) o -> a (h o)", a=1).to_broadcast([128, H])).then_inc(w_in, 16)
            for u in range(U):
                rows_split(sp, x[:, u], xg[u], x_in[u])

            def body(it, more):
                for u in range(U):
                    g = it * U + u
                    sp.wait_ge(xn_ready, g * GT + GT)
                    if more:
                        rows_split(sp, x[:, u], one(xg, g + U), x_in[u])
                    rows_split(sp, one(xng, g), xn[:, u], xn_out[u])
                    sp.wait_ge(xt_ready, g + 1)
                    sp.dma_start(one(K.xt_d, g), xt[:, u].rearrange("p c n -> p (c n)")).then_inc(xt_out[u], 16)
                    sp.wait_ge(hs_ready, g + 1)
                    rows_split(sp, one(hg, g), hs[:, u], h_out[u])

            with sp.Fori(0, TURNS - 1) as it:
                body(it, True)
            body(TURNS - 1, False)
            for u in range(U):
                sp.wait_ge(xn_out[u], 32 * TURNS)
                sp.wait_ge(xt_out[u], 16 * TURNS)
                sp.wait_ge(h_out[u], 32 * TURNS)

        @block.vector
        def _(dve):
            dve.wait_ge(w_in, 64)
            for k in range(2):
                for c in range(HC):
                    nc.vector.tensor_tensor(wtmp[:, c, k, :].rearrange("p (h o) -> p h o", o=OUT), heads(wx[:, c, 0:ROW])[:, :, 0:OUT],
                                            att[:, k, :].rearrange("p (h o) -> p h o", o=OUT), ALU.mult).then_inc(wx_ready, 1)
            dve.wait_ge(wx_ready, 4)
            for k in range(2):
                for c in range(HC):
                    nc.vector.tensor_reduce(wx[:, c, ROW:HW] if k else wx[:, c, OUT:ROW:OUT + 1],
                                            wtmp[:, c, k, :].rearrange("p (h o) -> p h o", h=HEADS), X, ALU.add).then_inc(wx_ready, 1)

            def h_copy(g, v, stored, fresh):
                dve.wait_ge(h_ready, g + 1)
                if not fresh:
                    dve.wait_ge(h_out[v], stored)
                tiles = K.asd[:, bass.ds(g * GT, GT), :]
                nc.vector.tensor_copy(tiles[:, :, 0:HEADS], hp[0:P, :, OUT:ROW:OUT + 1]).then_inc(asd_ready, 1)
                nc.vector.tensor_copy(tiles[:, :, HEADS:], hp[0:P, :, ROW:HW]).then_inc(asd_ready, 1)
                nc.vector.tensor_copy(hs[:, v], hp[0:P, :, 0:ROW]).then_inc(hs_ready, 1)

            per = U * (2 * GT + 1)

            def body(it, first):
                c = Chain(dve, dve_done, per, it)
                for u in range(U):
                    g = it * U + u
                    dve.wait_ge(x_in[u], it * 32 + 32)
                    norm_stats(nc, c, x[:, u], stats, mv, var).then_inc(var_ready, 1)
                    if not (first and u < 2):
                        h_copy(g - 2, (u - 2) % U, it * 32 if u >= 2 else (it - 1) * 32, first or (u < 2 and first))
                    dve.wait_ge(std_ready, g + 1)
                    if not first:
                        dve.wait_ge(xn_out[u], it * 32)
                        dve.wait_ge(tp_ready, g - U + 1)
                    for ins in norm_rows(nc, c, x[:, u], xn[:, u], mv, std, rstd):
                        ins.then_inc(xn_ready, 1)
                c.close()

            turns(dve, TURNS, body)
            for g in (GROUPS - 2, GROUPS - 1):
                h_copy(g, g % U, 32 * (TURNS - 1), False)

        @block.scalar
        def _(act):
            def body(it, first):
                for u in range(U):
                    g = it * U + u
                    act.wait_ge(var_ready, g + 1)
                    nc.scalar.activation(std[:, :], var[:, :], ACT.Sqrt).then_inc(std_ready, 1)
                    act.wait_ge(tp_ready, g + 1)
                    if not first:
                        act.wait_ge(xt_out[u], it * 16)
                        act.wait_ge(h_ready, g - U + 1)
                    nc.scalar.activation(xt[:, u], tp[:, u % 2, :, 0:GN], ACT.Copy).then_inc(xt_ready, 1)

            turns(act, TURNS, body)

        @block.tensor
        def _(pe):
            pe.wait_ge(wx_ready, 8)

            def project(g, u, first):
                pe.wait_ge(xt_ready, g + 1)
                if not first:
                    pe.wait_ge(hs_ready, g)
                for t in range(GT):
                    for k in range(HC):
                        mm = nc.tensor.matmul(hp[0:P, t, 0:HW], xt[:, u, k, t * P:(t + 1) * P], wx[:, k, :],
                                              start=(k == 0), stop=(k == HC - 1))
                mm.then_inc(h_ready, 1)

            def body(it, first):
                for u in range(U):
                    g = it * U + u
                    pe.wait_ge(xn_ready, g * GT + GT)
                    if not (first and u < 2):
                        pe.wait_ge(xt_ready, g if u == 0 else g - 1)
                    for t in range(GT):
                        for k in range(HC):
                            mm = nc.tensor.transpose(tp[:, u % 2, k, t * P:(t + 1) * P],
                                                     xn[:, u, t, k * 128:(k + 1) * 128], K.ident[0:P, 0:P])
                    mm.then_inc(tp_ready, 1)
                    if not (first and u == 0):
                        project(g - 1, (u - 1) % U, first and u == 1)

            turns(pe, TURNS, body)
            project(GROUPS - 1, U - 1, False)


def stage_mix(nc, K, A):
    U = UNROLL
    C = H
    GH = C // 4
    D = 32
    with Scope(nc, "mix") as s:
        search = EdgeSearch(nc, K, s)
        wqkv = s.sb("wqkv", [128, HC, 3 * C])
        wg1 = s.sb("wg1", [128, HC, GH])
        wg1g = s.sb("wg1g", [128, HC, GH])
        lng = s.sb("lng", [128, HC])
        lnb = s.sb("lnb", [128, HC])
        bg1 = s.sb("bg1", [GH, 1])
        bias1 = s.sb("bias1", [GH, 1])
        wg2 = s.sb("wg2", [GH, C])
        bg2 = s.sb("bg2", [128, HC])
        wproj = s.sb("wproj", [128, HC, C])
        bproj = s.sb("bproj", [P, C])
        beta = s.sb("beta", [P, C])
        x_rows = s.sb("x_rows", [P, U, GT, C])
        mo_half = s.sem("mo_half")
        kmax_g = s.sb("kmax_g", [128, HC, GROUPS])
        kmax = s.sb("kmax", [128, HC])
        nkmax = s.sb("nkmax", [1, C])
        ones = s.sb("ones1", [1, P])
        wqT = s.sb("wqT", [128, HC, C])
        ctx_acc = s.sb("ctx_acc", [128, HC, 129])
        ctx_inv = s.sb("ctx_inv", [128, HC])
        ctx_bd = s.sb("ctx_bd", [128, HC, 128])
        wqc = s.sb("wqc", [128, HC, C])
        xt = s.sb("xt2", [128, U, HC * GN])
        io = s.sb("io2", [128, U, GT * H])
        z = s.sb("z", [P, GT, H])
        zt = s.sb("zt", [128, HC, GN])
        hgt = s.sb("hgt", [GH, GN])
        gt = s.sb("gt", [128, 2, HC * GN])
        pk = s.sb("pk", [P, 2, C])
        vx = s.sb("vx", [P, 2, HC, 129])
        og = s.sb("og", [128, U, HC * GN])
        mo = s.sb("mo", [P, 2, GT, C])
        stats = s.sb("stats2", [P, GT, 6])
        mv = s.sb("mv2", [P, GT, 3])
        var = s.sb("var2", [P, GT])
        std = s.sb("std2", [P, GT])
        rstd = s.sb("rstd2", [P, GT])
        ps = s.ps("ps_mix", [128, 8, 512])
        w_in = s.sem("w_in2")
        set_up = s.sem("set_up")
        in_a = s.sems("in_a", U)
        in_b = s.sems("in_b", U)
        in_c = s.sems("in_c", U)
        var_ready, std_ready, z_ready, zt_psum, zt_ready = (s.sem(n) for n in (
            "var_ready2", "std_ready2", "z_ready", "zt_psum", "zt_ready"))
        kt_ready, kt_used, hg_psum, hg_ready, gate_psum, gate_ready = (s.sem(n) for n in (
            "kt_ready", "kt_used", "hg_psum", "hg_ready", "gate_psum", "gate_ready"))
        gate_out = s.sems("gate_out", 2)
        kmax_ready, kmax_row, nkmax_ready = s.sem("kmax_ready"), s.sem("kmax_row"), s.sem("nkmax_ready")
        kv_psum, p_ready, v_ready, ctx_psum, ctx_added = (s.sem(n) for n in (
            "kv_psum", "p_ready", "v_ready", "ctx_psum", "ctx_added"))
        bd_ready, wqc_psum, wqc_ready = s.sem("bd_ready"), s.sem("wqc_psum"), s.sem("wqc_ready")
        out_psum, og_ready, mix_psum, mix_ready = (s.sem(n) for n in ("out_psum", "og_ready", "mix_psum", "mix_ready"))
        mix_out = s.sems("mix_out", 2)
        dve_done = s.sem("dve_done2")
        dve_end = s.sem("dve_end2")
        block = s.block()
        xng = K.xn_d.rearrange("(g t p) f -> g p t f", p=P, t=GT)
        mixg = K.mix_d.rearrange("(g t p) f -> g p t f", p=P, t=GT)
        rows = lambda u: io[0:P, u, :].rearrange("p (t f) -> p t f", t=GT)
        fm = lambda t, k: t.rearrange("p (k n) -> p k n", k=HC)[:, k, :]

        @block.gpsimd
        def _(pool):
            search.run(pool)

        @block.sync
        def _(sp):
            with nc.allow_non_contiguous_dma(reason="biases to columns, once"):
                for t, a in ((wqkv, A.mix_Wqkv), (wg1, A.mix_Wg1), (wproj, A.mix_Wproj)):
                    sp.dma_start(t[:], a.rearrange("(c p) n -> p c n", p=128)).then_inc(w_in, 16)
                for t, a in ((lng, A.mix_ln_g), (lnb, A.mix_ln_b), (bg2, A.mix_bg2)):
                    sp.dma_start(t[:], a.rearrange("(c p) -> p c", p=128)).then_inc(w_in, 16)
                sp.dma_start(bg1[:, :], A.mix_bg1.rearrange("(p a) -> p a", a=1)).then_inc(w_in, 16)
            sp.dma_start(wg2[:, :], A.mix_Wg2).then_inc(w_in, 16)
            for t, a in ((bproj, A.mix_bproj), (beta, A.beta)):
                sp.dma_start(t[:, :], a.rearrange("(a n) -> a n", a=1).to_broadcast([P, C])).then_inc(w_in, 16)

            def load_a(g, u):
                sp.dma_start(xt[:, u, :], one(K.xt_d, g)).then_inc(in_a[u], 16)
                rows_split(sp, rows(u), one(xng, g), in_a[u])

            def load_b(g, u):
                sp.dma_start(xt[:, u, :], one(K.xt_d, g)).then_inc(in_b[u], 16)

            def load_c(g, u):
                sp.dma_start(xt[:, u, :], one(K.xt_d, g)).then_inc(in_c[u], 16)
                sp.dma_start(io[:, u, 0:HC * GN], one(K.gt_d, g)).then_inc(in_c[u], 16)
                rows_split(sp, x_rows[:, u], one(A.x.rearrange("(g t p) f -> g p t f", p=P, t=GT), g), in_c[u])

            for u in range(U):
                load_a(u, u)

            def gates(it, more):
                for u in range(U):
                    g = it * U + u
                    sp.wait_ge(kt_ready, g + 1)
                    sp.wait_ge(z_ready, g * GT + GT)
                    (load_a if more else load_b)(g + U if more else u, u)
                    sp.wait_ge(gate_ready, g + 1)
                    if isinstance(g, int):
                        sp.dma_start(K.gt_d[g], gt[:, u % 2, :]).then_inc(gate_out[u % 2], 16)
                    else:
                        sp.dma_start(one(K.gt_d, g), gt[:, u % 2, :]).then_inc(gate_out[u % 2], 16)

            with sp.Fori(0, TURNS - 1) as it:
                gates(it, True)
            gates(TURNS - 1, False)

            def context(it, more):
                for u in range(U):
                    g = it * U + u
                    sp.wait_ge(kv_psum, g * GT + GT)
                    if more:
                        load_b(g + U, u)
                    else:
                        if u == 0:
                            for b in range(2):
                                sp.wait_ge(gate_out[b], 16 * (3 - b) * TURNS)
                        load_c(u, u)

            with sp.Fori(0, TURNS - 1) as it:
                context(it, True)
            context(TURNS - 1, False)

            def output(it, more):
                for u in range(U):
                    g = it * U + u
                    sp.wait_ge(mix_ready, g + 1)
                    rows_split(sp, one(mixg, g), mo[:, u % 2], mix_out[u % 2])
                    if more:
                        load_c(g + U, u)

            with sp.Fori(0, TURNS - 1) as it:
                output(it, True)
            output(TURNS - 1, False)
            for b in range(2):
                sp.wait_ge(mix_out[b], 32 * (3 - b) * TURNS)

        def stored(it, u, per):
            return (it * (3 if u % 2 == 0 else 2) + u // 2) * per

        @block.vector
        def _(dve):
            c = Chain(dve, dve_end)
            dve.wait_ge(w_in, 160)
            for k in range(HC):
                nc.vector.tensor_scalar(wg1g[:, k, :], wg1[:, k, :], lng[:, k:k + 1], None, ALU.mult).then_inc(set_up, 1)
            nc.vector.memset(ones[:], 1.0).then_inc(set_up, 1)
            nc.vector.memset(ctx_acc[:], 0.0).then_inc(set_up, 1)
            nc.vector.memset(ctx_bd[:], 0.0).then_inc(set_up, 1)
            for b in range(2):
                nc.vector.memset(vx[:, b, :, 128:129], 1.0).then_inc(set_up, 1)
            nc.vector.tensor_tensor(bproj[:], bproj[:], beta[:], ALU.add).then_inc(set_up, 1)
            dve.wait_ge(wqc_psum, 1)
            nc.vector.tensor_tensor(bias1[:], ps[0:GH, 7, 0:1], bg1[:], ALU.add).then_inc(set_up, 1)
            for k in range(HC):
                nc.vector.tensor_copy(wqT[:, k, :], ps[:, k, 0:C]).then_inc(set_up, 1)

            per = U * (2 * GT + 1)

            def gates(it, first):
                c = Chain(dve, dve_done, per, it)
                for u in range(U):
                    g = it * U + u
                    dve.wait_ge(in_a[u], it * 48 + 48)
                    norm_stats(nc, c, rows(u), stats, mv, var).then_inc(var_ready, 1)
                    dve.wait_ge(kt_ready, g + 1)
                    nc.vector.tensor_reduce(kmax_g[:, :, bass.ds(g, 1)], ps[:, 0:2, 0:GN], X, ALU.max).then_inc(kt_used, 1)
                    dve.wait_ge(std_ready, g + 1)
                    if not (first and u == 0):
                        dve.wait_ge(zt_psum, g)
                    for ins in norm_rows(nc, c, rows(u), z, mv, std, rstd):
                        ins.then_inc(z_ready, 1)
                c.close()

            turns(dve, TURNS, gates)
            dve.wait_ge(kt_used, GROUPS)
            nc.vector.tensor_reduce(kmax[:], kmax_g[:], X, ALU.max).then_inc(kmax_ready, 1)
            dve.wait_ge(kmax_row, 1)
            nc.vector.tensor_scalar(nkmax[:], ps[0:1, 7, 0:C], -1.0, None, ALU.mult).then_inc(nkmax_ready, 1)

            def add_group(g, start):
                dve.wait_ge(ctx_psum, g * GT + GT)
                if not start:
                    dve.wait_ge(ctx_added, g)
                nc.vector.tensor_tensor(ctx_acc[:], ctx_acc[:], ps[:, 4:6, 0:129], ALU.add).then_inc(ctx_added, 1)

            def context(it, first):
                for u in range(U):
                    g = it * U + u
                    for t in range(GT):
                        i = g * GT + t
                        dve.wait_ge(kv_psum, i + 1)
                        if not (first and u == 0 and t < 2):
                            dve.wait_ge(ctx_psum, i - 1)
                        nc.vector.tensor_copy(vx[:, t % 2, :, 0:128],
                                              ps[0:P, 2 + t % 2, 0:C].rearrange("p (c v) -> p c v", c=HC)).then_inc(v_ready, 1)
                        if t == 0 and not (first and u == 0):
                            add_group(g - 1, first and u == 1)

            dve.wait_ge(set_up, 8)
            turns(dve, TURNS, context)
            add_group(GROUPS - 1, False)
            dve.wait_ge(ctx_added, GROUPS)
            c.did(nc.vector.reciprocal(ctx_inv[:], ctx_acc[:, :, 128]))
            c.settle()
            for k in range(HC):
                for h in range(128 // D):
                    q = slice(h * D, h * D + D)
                    nc.vector.tensor_scalar(ctx_bd[q, k, q], ctx_acc[q, k, q], ctx_inv[q, k:k + 1], None,
                                            ALU.mult).then_inc(bd_ready, 1)
            dve.wait_ge(wqc_psum, 2)
            nc.vector.tensor_copy(wqc[:], ps[:, 6:8, 0:C]).then_inc(wqc_ready, 1)

            def add_bias(it, u, fresh):
                g = it * U + u
                dve.wait_ge(mix_psum, g + 1)
                if not fresh:
                    dve.wait_ge(mix_out[u % 2], stored(it, u, 32))
                nc.vector.tensor_tensor(mo[:, u % 2].rearrange("p (a b) f -> p a b f", a=2),
                                        ps[0:P, 2:4, :].rearrange("p a (b f) -> p a b f", b=2),
                                        bproj[:].rearrange("p (a b f) -> p a b f", a=1, b=1).to_broadcast([P, 2, 2, C]),
                                        ALU.add).then_inc(mo_half, 1)
                dve.wait_ge(mo_half, g + 1)
                nc.vector.tensor_tensor(mo[:, u % 2], mo[:, u % 2], x_rows[:, u], ALU.add).then_inc(mix_ready, 1)

            def output(it, first):
                for u in range(U):
                    g = it * U + u
                    dve.wait_ge(in_c[u], it * 64 + 64)
                    dve.wait_ge(out_psum, g + 1)
                    if not first:
                        dve.wait_ge(mix_psum, g - (U - 1))
                    nc.vector.tensor_tensor(og[:, u, :].rearrange("p (k n) -> p k n", k=HC), ps[:, 0:2, 0:GN],
                                            io[:, u, 0:HC * GN].rearrange("p (k n) -> p k n", k=HC), ALU.mult).then_inc(og_ready, 1)
                    if u:
                        add_bias(it, u - 1, first and u < 3)
                    elif not first:
                        add_bias(it - 1, U - 1, False)

            turns(dve, TURNS, output)
            add_bias(TURNS - 1, U - 1, False)

        @block.scalar
        def _(act):
            act.wait_ge(set_up, 9)

            def gates(it, first):
                for u in range(U):
                    g = it * U + u
                    act.wait_ge(var_ready, g + 1)
                    nc.scalar.activation(std[:, :], var[:, :], ACT.Sqrt).then_inc(std_ready, 1)
                    act.wait_ge(zt_psum, g + 1)
                    if not (first and u == 0):
                        act.wait_ge(hg_psum, g)
                    nc.scalar.activation(zt[:], ps[:, 2:4, 0:GN], ACT.Copy).then_inc(zt_ready, 1)
                    act.wait_ge(hg_psum, g + 1)
                    nc.scalar.activation(hgt[:], ps[0:GH, 4, 0:GN], ACT.Gelu, bias=bias1[:, 0:1]).then_inc(hg_ready, 1)
                    act.wait_ge(gate_psum, g + 1)
                    if not (first and u < 2):
                        act.wait_ge(gate_out[u % 2], stored(it, u, 16))
                    nc.scalar.activation(fm(gt[:, u % 2, :], 0), ps[:, 5, 0:GN], ACT.Sigmoid, bias=bg2[:, 0:1])
                    nc.scalar.activation(fm(gt[:, u % 2, :], 1), ps[:, 6, 0:GN], ACT.Sigmoid, bias=bg2[:, 1:2]).then_inc(gate_ready, 1)

            turns(act, TURNS, gates)

            def context(it, first):
                for u in range(U):
                    for t in range(GT):
                        i = (it * U + u) * GT + t
                        act.wait_ge(kv_psum, i + 1)
                        if not (first and u == 0 and t < 2):
                            act.wait_ge(ctx_psum, i - 1)
                        nc.scalar.activation(pk[:, t % 2, :], ps[0:P, t % 2, 0:C], ACT.Exp).then_inc(p_ready, 1)

            turns(act, TURNS, context)

        @block.tensor
        def _(pe):
            pe.wait_ge(w_in, 160)
            for i in range(HC):
                for k in range(HC):
                    nc.tensor.transpose(ps[:, k, i * 128:(i + 1) * 128], wqkv[:, i, k * 128:(k + 1) * 128], K.ident[:])
            for k in range(HC):
                mm = nc.tensor.matmul(ps[0:GH, 7, 0:1], wg1[:, k, :], lnb[:, k:k + 1], start=(k == 0), stop=(k == HC - 1))
            mm.then_inc(wqc_psum, 1)
            pe.wait_ge(set_up, 11)

            def keys(it, u, start):
                pe.wait_ge(in_a[u], it * 48 + 48)
                if not start:
                    pe.wait_ge(kt_used, it * U + u)
                for m in range(HC):
                    for k in range(HC):
                        mm = nc.tensor.matmul(ps[:, m, 0:GN], wqkv[:, k, C + m * 128:C + (m + 1) * 128],
                                              fm(xt[:, u, :], k), start=(k == 0), stop=(k == HC - 1))
                mm.then_inc(kt_ready, 1)

            keys(0, 0, True)

            def gates(it, first, end=False):
                for u in range(U):
                    g = it * U + u
                    pe.wait_ge(z_ready, g * GT + GT)
                    if not (first and u == 0):
                        pe.wait_ge(zt_ready, g)
                    for t in range(GT):
                        for k in range(HC):
                            mm = nc.tensor.transpose(ps[:, 2 + k, t * P:(t + 1) * P], z[:, t, k * 128:(k + 1) * 128],
                                                     K.ident[0:P, 0:P])
                    mm.then_inc(zt_psum, 1)
                    if u + 1 < U:
                        keys(it, u + 1, False)
                    elif not end:
                        keys(it + 1, 0, False)
                    pe.wait_ge(zt_ready, g + 1)
                    if not (first and u == 0):
                        pe.wait_ge(hg_ready, g)
                    for k in range(HC):
                        mm = nc.tensor.matmul(ps[0:GH, 4, 0:GN], wg1g[:, k, :], zt[:, k, :], start=(k == 0), stop=(k == HC - 1))
                    mm.then_inc(hg_psum, 1)
                    pe.wait_ge(hg_ready, g + 1)
                    if not (first and u == 0):
                        pe.wait_ge(gate_ready, g)
                    for m in range(HC):
                        mm = nc.tensor.matmul(ps[:, 5 + m, 0:GN], wg2[:, m * 128:(m + 1) * 128], hgt[:], start=True, stop=True)
                    mm.then_inc(gate_psum, 1)

            gates(0, True)
            with pe.Fori(1, TURNS - 1) as it:
                gates(it, False)
            gates(TURNS - 1, False, True)
            pe.wait_ge(kmax_ready, 1)
            for k in range(HC):
                mm = nc.tensor.transpose(ps[0:1, 7, k * 128:(k + 1) * 128], kmax[:, k:k + 1], K.ident[:])
            mm.then_inc(kmax_row, 1)
            pe.wait_ge(nkmax_ready, 1)
            pe.wait_ge(gate_ready, GROUPS)

            def add_context(g, t, begin):
                i = g * GT + t
                pe.wait_ge(p_ready, i + 1)
                pe.wait_ge(v_ready, i + 1)
                if t == 0 and not begin:
                    pe.wait_ge(ctx_added, g)
                for k in range(HC):
                    mm = nc.tensor.matmul(ps[:, 4 + k, 0:129], pk[:, t % 2, k * 128:(k + 1) * 128],
                                          vx[:, t % 2, k, :], start=(t == 0), stop=(t == GT - 1))
                mm.then_inc(ctx_psum, 1)

            def context(it, first):
                for u in range(U):
                    for t in range(GT):
                        g = it * U + u
                        i = g * GT + t
                        if t == 0:
                            pe.wait_ge(in_b[u], it * 16 + 16)
                        if not (first and u == 0 and t < 2):
                            pe.wait_ge(p_ready, i - 1)
                            pe.wait_ge(v_ready, i - 1)
                        for k in range(HC):
                            nc.tensor.matmul(ps[0:P, t % 2, 0:C], fm(xt[:, u, :], k)[:, t * P:(t + 1) * P],
                                             wqkv[:, k, C:2 * C], start=(k == 0), stop=False)
                        nc.tensor.matmul(ps[0:P, t % 2, 0:C], ones[:], nkmax[:], start=False, stop=True)
                        for k in range(HC):
                            mm = nc.tensor.matmul(ps[0:P, 2 + t % 2, 0:C], fm(xt[:, u, :], k)[:, t * P:(t + 1) * P],
                                                  wqkv[:, k, 2 * C:3 * C], start=(k == 0), stop=(k == HC - 1))
                        mm.then_inc(kv_psum, 1)
                        if t > 0:
                            add_context(g, t - 1, first and u == 0)
                        elif not (first and u == 0):
                            add_context(g - 1, GT - 1, False)

            turns(pe, TURNS, context)
            add_context(GROUPS - 1, GT - 1, False)
            pe.wait_ge(bd_ready, HC * 128 // D)
            for m in range(HC):
                for k in range(HC):
                    mm = nc.tensor.matmul(ps[:, 6 + m, k * 128:(k + 1) * 128], wqT[:, k, m * 128:(m + 1) * 128],
                                          ctx_bd[:, k, :], start=True, stop=True)
            mm.then_inc(wqc_psum, 1)
            pe.wait_ge(wqc_ready, 1)

            def attend(it, u, start):
                pe.wait_ge(in_c[u], it * 64 + 64)
                if not start:
                    pe.wait_ge(og_ready, it * U + u)
                for m in range(HC):
                    for k in range(HC):
                        mm = nc.tensor.matmul(ps[:, m, 0:GN], wqc[:, k, m * 128:(m + 1) * 128],
                                              fm(xt[:, u, :], k), start=(k == 0), stop=(k == HC - 1))
                mm.then_inc(out_psum, 1)

            def project(g, u, start):
                pe.wait_ge(og_ready, g + 1)
                if not start:
                    pe.wait_ge(mix_ready, g)
                for t in range(GT):
                    for k in range(HC):
                        mm = nc.tensor.matmul(ps[0:P, 2 + t // 2, (t % 2) * C:(t % 2 + 1) * C],
                                              fm(og[:, u, :], k)[:, t * P:(t + 1) * P], wproj[:, k, :],
                                              start=(k == 0), stop=(k == HC - 1))
                mm.then_inc(mix_psum, 1)

            def output(it, first):
                for u in range(U):
                    attend(it, u, first and u == 0)
                    if not (first and u == 0):
                        project(it * U + u - 1, (u - 1) % U, first and u == 1)

            turns(pe, TURNS, output)
            project(GROUPS - 1, U - 1, False)


def stage_edges(nc, K):
    with Scope(nc, "edges") as s:
        rec = s.sb("rec", [128, EC, HEADS])
        meta = s.sb("meta", [128, EC, META])
        dst = s.sb("dst_b", [128, EC], I32)
        prev = s.sb("prev_b", [128, EC], I32)
        follow = s.sb("follow_b", [128, EC], I32)
        src = s.sb("src_b", [128, EC], I32)
        same = s.sb("same", [128, EC])
        same_next = s.sb("same_next", [128, EC])
        pen = s.sb("pen", [128, 2, EC])
        head = s.sb("head", [128, EC])
        tail = s.sb("tail", [128, 2, HEADS])
        rows = s.sb("rows", [HEADS, 2, 128])
        run = s.sb("run", [HEADS, 128])
        carry = s.sb("carry", [128, HEADS])
        one_row = s.sb("one_row", [1, EDGE_GROUPS])
        ps = s.ps("ps_edges", [128, 2, 512])
        edges_in = s.sem("edges_in")
        rec_in = s.sem("rec_in")
        tail_ready = s.sem("tail_ready")
        tail_turned = s.sem("tail_turned")
        run_ready = s.sem("run_ready")
        run_turned = s.sem("run_turned")
        pen_ready, pen_out = s.sem("pen_ready"), s.sem("pen_out")
        meta_ready, meta_out = s.sem("meta_ready"), s.sem("meta_out")
        done = s.sem("dve_done")
        block = s.block()
        flat = K.dst_d
        per_edge = lambda a: a.rearrange("(p j) -> p j", p=128)

        @block.sync
        def _(sp):
            sp.dma_start(dst[:, :], per_edge(flat[0:EP])).then_inc(edges_in, 16)
            sp.dma_start(prev[1:128, :], flat[EC - 1:EP - 1].rearrange("(p j) -> p j", p=127)).then_inc(edges_in, 16)
            sp.dma_start(prev[0:1, 1:EC], flat[0:EC - 1].rearrange("(p j) -> p j", p=1)).then_inc(edges_in, 16)
            sp.dma_start(follow[:, :], per_edge(flat[1:EP + 1])).then_inc(edges_in, 16)
            sp.dma_start(src[:, :], per_edge(K.src_d)).then_inc(edges_in, 16)
            sp.dma_start(rec[:], K.rec_d.rearrange("(p j) h -> p j h", p=128)).then_inc(rec_in, 16)
            sp.wait_ge(pen_ready, 2)
            for k in range(2):
                sp.dma_start(per_edge(K.pen_d[k]), pen[:, k, :]).then_inc(pen_out, 16)
            sp.wait_ge(meta_ready, 4 + HEADS)
            sp.dma_start(K.meta_d.rearrange("(p j) r -> p j r", p=128), meta[:]).then_inc(meta_out, 16)
            sp.wait_ge(meta_out, 16)
            with nc.allow_non_contiguous_dma(reason="one number of each group, once"):
                ends = K.meta_d.rearrange("(g n) r -> g n r", n=EG)[:, EG - 1, HEADS]
                sp.dma_start(ends.rearrange("(a g) -> a g", a=1), one_row[:, :]).then_inc(meta_out, 16)
            sp.wait_ge(meta_out, 32)
            sp.wait_ge(pen_out, 32)

        @block.tensor
        def _(pe):
            pe.wait_ge(tail_ready, 2)
            for q in range(2):
                mm = nc.tensor.transpose(ps[0:HEADS, 0, q * 128:(q + 1) * 128], tail[:, q, :], K.ident[:])
            mm.then_inc(tail_turned, 1)
            pe.wait_ge(run_ready, 2)
            nc.tensor.transpose(ps[:, 1, 0:HEADS], run[:, :], K.ident[0:HEADS, 0:HEADS]).then_inc(run_turned, 1)

        @block.vector
        def _(dve):
            c = Chain(dve, done)
            v = nc.vector
            v.memset(one_row[:], 1.0).then_inc(meta_ready, 1)
            dve.wait_ge(edges_in, 80)
            c.did(v.memset(prev[0:1, 0:1], -1))
            c.settle()
            c.did(v.tensor_tensor(same[:], dst[:], prev[:], ALU.is_equal))
            c.did(v.tensor_tensor(same_next[:], dst[:], follow[:], ALU.is_equal))
            v.tensor_copy(meta[:, :, HEADS + 1], dst[:]).then_inc(meta_ready, 1)
            v.tensor_copy(meta[:, :, HEADS + 2].bitcast(I32), src[:]).then_inc(meta_ready, 1)
            c.settle()
            v.tensor_scalar(pen[:, 0, :], same[:], 1.0, -NEVER, ALU.subtract, ALU.mult).then_inc(pen_ready, 1)
            v.tensor_scalar(pen[:, 1, :], same_next[:], 1.0, -NEVER, ALU.subtract, ALU.mult).then_inc(pen_ready, 1)
            v.tensor_scalar(meta[:, :, HEADS], same_next[:], -1.0, 1.0, ALU.mult, ALU.add).then_inc(meta_ready, 1)
            c.did(v.tensor_tensor_scan(head[:], same[:], same[:], 1.0, ALU.mult, ALU.mult))
            dve.wait_ge(rec_in, 16)
            for h in range(HEADS):
                c.did(v.tensor_tensor_scan(rec[:, :, h], same[:], rec[:, :, h], 0.0, ALU.mult, ALU.add))
            c.settle()
            v.tensor_copy(tail[:, 0, :], rec[:, EC - 1, :]).then_inc(tail_ready, 1)
            v.tensor_copy(tail[:, 1, :], head[:, EC - 1:EC].to_broadcast([128, HEADS])).then_inc(tail_ready, 1)
            dve.wait_ge(tail_turned, 1)
            c.did(v.tensor_copy(rows[:, :, :], ps[0:HEADS, 0, 0:256].rearrange("p (a b) -> p a b", a=2)))
            c.settle()
            v.memset(run[:, 0:1], 0.0).then_inc(run_ready, 1)
            v.tensor_tensor_scan(run[:, 1:128], rows[:, 1, 0:127], rows[:, 0, 0:127], 0.0,
                                 ALU.mult, ALU.add).then_inc(run_ready, 1)
            dve.wait_ge(run_turned, 1)
            c.did(v.tensor_copy(carry[:, :], ps[:, 1, 0:HEADS]))
            c.settle()
            for h in range(HEADS):
                v.scalar_tensor_tensor(meta[:, :, h], head[:], carry[:, h:h + 1], rec[:, :, h],
                                       ALU.mult, ALU.add).then_inc(meta_ready, 1)


def stage_aggregate(nc, K):
    B, R = STEP_BATCH, 3
    W = ROW + HEADS + 1
    BIG = float(2.0 ** 100)
    full, rest = BATCHES // R, BATCHES % R
    assert STEPS % B == 0 and rest
    with Scope(nc, "aggregate") as s:
        meta = s.sb("meta_s", [128, R, B, 4, META])
        pen = s.sb("pen_s", [B * HEADS, R, 2, EG])
        g = s.sb("g", [128, R, B, 4, W])
        alpha = s.sb("alpha", [128, 4, B, HEADS])
        below = s.sb("below", [128, 4, B, HEADS])
        run_on = s.sb("run_on", [B * HEADS, EG])
        run_back = s.sb("run_back", [B * HEADS, EG])
        local = s.sb("local", [128, R, B, 4])
        pick = s.sb("pick", [128, R, 4, P])
        ends = s.sb("ends", [P, R, HEADS + 1])
        found = s.sb("found", [P, HEADS])
        top = s.sb("top_n", [P, HEADS])
        lower = s.sb("lower", [P, R, 2, HEADS])
        factor = s.sb("factor", [P, R, 2, HEADS])
        scaled = s.sb("scaled", [P, R, ROW])
        ps = s.ps("ps_agg", [128, B, 512])
        ps_rows = s.ps("ps_rows", [128, 512])
        ps_back = s.ps("ps_back", [128, 512])
        self_in, self_done = s.sem("self_in"), s.sem("self_done")
        meta_in = s.sems("meta_in", R)
        g_in = s.sems("g_in", R)
        alpha_sum, alpha_ready, local_ready, alpha_turned = (s.sem(n) for n in (
            "alpha_sum", "alpha_ready", "local_ready", "alpha_turned"))
        ran, max_ready, max_turned, below_ready, ends_ready, weight_ready = (s.sem(n) for n in (
            "ran", "max_ready", "max_turned", "below_ready", "ends_ready", "weight_ready"))
        pick_ready, msg_ready, agg_ready = s.sem("pick_ready"), s.sem("msg_ready"), s.sem("agg_ready")
        ends_in = s.sem("ends_in")
        node_steps, lower_ready, factor_ready, scaled_ready, merged = (s.sem(n) for n in (
            "node_steps", "lower_ready", "factor_ready", "scaled_ready", "merged"))
        block = s.block()
        groups = K.meta_d.rearrange("(g p i) r -> g p (i r)", p=128, i=4)
        pens = K.pen_d.rearrange("k (g n) -> g k n", n=EG)

        def walk(eng, batch):

            def body(it, first, n, end):
                for b in range(n):
                    last = end and b == n - 1
                    batch(it, first, b, None if last else (it, b + 1) if b + 1 < R else (it + 1, 0))

            body(0, True, R, False)
            with eng.Fori(1, full) as it:
                body(it, False, R, False)
            body(full, False, rest, True)

        @block.sync
        def _(sp):
            rows_split(sp, K.acc[:, :, :], K.h_d.rearrange("(t p) f -> p t f", p=P), self_in)

            def batch(it, first, b, ahead):
                k = it * R + b
                if not first:
                    sp.wait_ge(ends_ready, k * 2 - (2 * R - 2))
                for j in range(B):
                    t = sp.value_load(K.step_group[0:1, bass.ds(k * B + j, 1)], min_val=0, max_val=EDGE_GROUPS - 1)
                    sp.dma_start(meta[:, b, j].rearrange("p i r -> p (i r)"), one(groups, t)).then_inc(meta_in[b], 16)
                    sp.dma_start(pen[j * HEADS:(j + 1) * HEADS, b], pens[bass.ds(t, 1)].to_broadcast([HEADS, 2, EG])
                                 ).then_inc(meta_in[b], 16)

            walk(sp, batch)

        @block.gpsimd
        def _(pool):
            def batch(it, first, b, ahead):
                pool.wait_ge(meta_in[b], it * (32 * B) + 32 * B)
                pool_gate(nc, K)
                for j in range(B):
                    if not first:
                        pool.wait_ge(agg_ready, (it * R + b) * B + (j + 1 - R * B))
                        pool_gate(nc, K)
                    for i in range(4):
                        nc.gpsimd.indirect_dma_start(
                            out=g[:, b, j, i, 0:ROW], out_offset=None, in_=K.h_d,
                            in_offset=bass.IndirectOffsetOnAxis(ap=meta[:, b, j, i, META - 1:META].bitcast(I32), axis=0),
                        ).then_inc(g_in[b], 16)

            walk(pool, batch)

        @block.vector
        def _(dve):
            v = nc.vector
            dve.wait_ge(self_in, 32)
            v.memset(K.acc[:, :, OUT:ROW:OUT + 1], 1.0).then_inc(self_done, 1)
            v.tensor_tensor(K.run_max[:], K.asd[:, :, 0:HEADS], K.asd[:, :, HEADS:], ALU.add).then_inc(self_done, 1)
            dve.wait_ge(self_done, 2)
            v.scalar_tensor_tensor(K.run_max[:], K.run_max[:], NEG_SLOPE, K.run_max[:], ALU.mult, ALU.max).then_inc(self_done, 1)
            dve.wait_ge(self_done, 3)

            def sum_alpha(it, b):
                k = it * R + b
                dve.wait_ge(g_in[b], it * (64 * B) + 64 * B)
                if not (isinstance(k, int) and k == 0):
                    dve.wait_ge(below_ready, k)
                v.tensor_tensor(alpha[:].rearrange("p i j h -> p j i h"), g[:, b, :, :, OUT:ROW:OUT + 1],
                                meta[:, b, :, :, 0:HEADS], ALU.add).then_inc(alpha_sum, 1)
                v.tensor_tensor(local[:, b], meta[:, b, :, :, HEADS + 1],
                                K.step_node[:, bass.ds(k * B, B)].rearrange("p (j a) -> p j a", a=1).to_broadcast([128, B, 4]),
                                ALU.subtract).then_inc(local_ready, 1)
                dve.wait_ge(alpha_sum, k + 1)
                v.scalar_tensor_tensor(alpha[:], alpha[:], NEG_SLOPE, alpha[:], ALU.mult, ALU.max).then_inc(alpha_ready, 1)

            def run_maxima(it, b):
                k = it * R + b
                rows = ps_rows[0:B * HEADS, :]
                dve.wait_ge(alpha_turned, k + 1)
                v.tensor_tensor_scan(run_on[:], pen[:, b, 0, :], rows, NEVER, ALU.add, ALU.max).then_inc(ran, 1)
                v.tensor_tensor_scan(run_back[:, ::-1], pen[:, b, 1, ::-1], rows[:, ::-1], NEVER,
                                     ALU.add, ALU.max).then_inc(ran, 1)
                dve.wait_ge(ran, k * 2 + 2)
                v.tensor_tensor(run_on[:], run_on[:], run_back[:], ALU.max).then_inc(max_ready, 1)

            def split_alpha(it, b):
                k = it * R + b
                back = ps_back[:, 0:4 * B * HEADS].rearrange("p (i j h) -> p i j h", i=4, j=B)
                dve.wait_ge(max_turned, k + 1)
                v.tensor_tensor(below[:], alpha[:], back, ALU.subtract).then_inc(below_ready, 1)
                last = meta[:, b, :, :, HEADS:HEADS + 1]
                v.tensor_tensor(g[:, b, :, :, ROW:ROW + HEADS], back.rearrange("p i j h -> p j i h"),
                                last.to_broadcast([128, B, 4, HEADS]), ALU.mult).then_inc(ends_ready, 1)
                v.tensor_scalar(g[:, b, :, :, ROW + HEADS:W], last, BIG, None, ALU.mult).then_inc(ends_ready, 1)

            def one_hot(it, first, b, j):
                i = (it * R + b) * B + j
                q = (b * B + j) % R
                if not (first and b * B + j < R):
                    dve.wait_ge(agg_ready, i - (R - 1))
                if j == 0:
                    dve.wait_ge(local_ready, it * R + b + 1)
                v.tensor_tensor(pick[:, q], K.iota_col[:, 0:P].rearrange("p (a n) -> p a n", a=1).to_broadcast([128, 4, P]),
                                local[:, b, j, :].rearrange("p (i a) -> p i a", a=1).to_broadcast([128, 4, P]),
                                ALU.is_equal).then_inc(pick_ready, 1)

            def messages(it, b, j):
                if j == 0:
                    dve.wait_ge(weight_ready, it * R + b + 1)
                rows = g[:, b, j, :, 0:ROW].rearrange("p i (h o) -> p i h o", h=HEADS)
                v.tensor_tensor(rows[:, :, :, 0:OUT], rows[:, :, :, 0:OUT],
                                rows[:, :, :, OUT:OUT + 1].to_broadcast([128, 4, HEADS, OUT]), ALU.mult).then_inc(msg_ready, 1)

            def find(i, n):
                dve.wait_ge(ends_in, i + 1)
                if not (isinstance(i, int) and i == 0):
                    dve.wait_ge(lower_ready, i * 2)
                    dve.wait_ge(node_steps, i * 3)
                v.scalar_tensor_tensor(found[:], ends[:, n % R, HEADS:].to_broadcast([P, HEADS]), BIG, ends[:, n % R, 0:HEADS],
                                       ALU.subtract, ALU.add).then_inc(node_steps, 1)

            def raise_max(i, n, m):
                dve.wait_ge(node_steps, i * 3 + 1)
                v.tensor_tensor(top[:], found[:], m, ALU.max).then_inc(node_steps, 1)
                dve.wait_ge(node_steps, i * 3 + 2)
                v.tensor_tensor(lower[:, n % R, 0], m, top[:], ALU.subtract).then_inc(lower_ready, 1)
                v.tensor_tensor(lower[:, n % R, 1], found[:], top[:], ALU.subtract).then_inc(lower_ready, 1)

            def keep_max(i, m):
                dve.wait_ge(lower_ready, i * 2 + 2)
                v.tensor_tensor(m, top[:], found[:], ALU.max).then_inc(node_steps, 1)

            def merge(i, n, tile):
                q = n % R
                dve.wait_ge(scaled_ready, i * HEADS + HEADS)
                if not (isinstance(i, int) and i == 0):
                    dve.wait_ge(merged, i * HEADS)
                for h in range(HEADS):
                    cols = slice(h * (OUT + 1), (h + 1) * (OUT + 1))
                    a = K.acc[:, bass.ds(tile, 1), cols].rearrange("p a f -> p (a f)")
                    v.scalar_tensor_tensor(a, a, factor[:, q, 0, h:h + 1], scaled[:, q, cols],
                                           ALU.mult, ALU.add).then_inc(merged, 1)

            def step(i, n, *meanwhile):
                tile = dve.value_load(K.step_tile[0:1, bass.ds(i, 1)], min_val=0, max_val=TILES - 1)
                m = K.run_max[:, bass.ds(tile, 1), :].rearrange("p a h -> p (a h)")
                find(i, n)
                raise_max(i, n, m)
                for work in meanwhile:
                    work()
                keep_max(i, m)
                merge(i, n, tile)

            sum_alpha(0, 0)
            run_maxima(0, 0)
            split_alpha(0, 0)

            def batch(it, first, b, ahead):
                if ahead:
                    sum_alpha(*ahead)
                for j in range(B):
                    i, n = (it * R + b) * B + j, b * B + j
                    if first and n < 2:
                        one_hot(it, first, b, j)
                        messages(it, b, j)
                    else:
                        step(i - 2, n - 2, lambda: one_hot(it, first, b, j), lambda: messages(it, b, j))
                    if ahead and j == 0:
                        run_maxima(*ahead)
                    if ahead and j == 1:
                        split_alpha(*ahead)

            walk(dve, batch)
            for k in (2, 1):
                step(STEPS - k, rest * B - k)
            dve.wait_ge(merged, STEPS * HEADS)

        @block.scalar
        def _(act):
            def weights(it, b):
                k = it * R + b
                act.wait_ge(below_ready, k + 1)
                nc.scalar.activation(g[:, b, :, :, OUT:ROW:OUT + 1], below[:].rearrange("p i j h -> p j i h"),
                                     ACT.Exp).then_inc(weight_ready, 1)

            def scale(i, n, first):
                q = n % R
                act.wait_ge(lower_ready, i * 2 + 2)
                if not (first and n < R):
                    act.wait_ge(merged, i * HEADS - (R - 1) * HEADS)
                nc.scalar.activation(factor[:, q], lower[:, q], ACT.Exp).then_inc(factor_ready, 1)
                act.wait_ge(factor_ready, i + 1)
                for h in range(HEADS):
                    cols = slice(h * (OUT + 1), (h + 1) * (OUT + 1))
                    nc.scalar.activation(scaled[:, q, cols], ps[0:P, n % B, cols], ACT.Copy,
                                         scale=factor[:, q, 1, h:h + 1]).then_inc(scaled_ready, 1)

            def take_ends(i, n):
                act.wait_ge(agg_ready, i + 1)
                nc.scalar.activation(ends[:, n % R, :], ps[0:P, n % B, ROW:W], ACT.Copy).then_inc(ends_in, 1)

            weights(0, 0)
            take_ends(0, 0)

            def batch(it, first, b, ahead):
                if ahead:
                    weights(*ahead)
                for j in range(B):
                    i, n = (it * R + b) * B + j, b * B + j
                    scale(i, n, first)
                    if ahead or j < B - 1:
                        take_ends(i + 1, n + 1)

            walk(act, batch)

        @block.tensor
        def _(pe):
            rows_of = B * HEADS

            def turn_alpha(it, b, start):
                k = it * R + b
                pe.wait_ge(alpha_ready, k + 1)
                if not start:
                    pe.wait_ge(max_ready, k)
                for i in range(4):
                    mm = nc.tensor.transpose(ps_rows[0:rows_of, i:EG:4], alpha[:, i].rearrange("p j h -> p (j h)"), K.ident[:])
                mm.then_inc(alpha_turned, 1)

            def turn_maxima(it, b):
                k = it * R + b
                pe.wait_ge(max_ready, k + 1)
                for i in range(4):
                    mm = nc.tensor.matmul(ps_back[:, i * rows_of:(i + 1) * rows_of], run_on[:, i:EG:4],
                                          K.ident[0:rows_of, 0:rows_of], start=True, stop=True)
                mm.then_inc(max_turned, 1)

            turn_alpha(0, 0, True)
            turn_maxima(0, 0)

            def batch(it, first, b, ahead):
                if ahead:
                    turn_alpha(*ahead, False)
                for j in range(B):
                    i, n = (it * R + b) * B + j, b * B + j
                    q = n % R
                    pe.wait_ge(pick_ready, i + 1)
                    pe.wait_ge(msg_ready, i + 1)
                    if j == 0:
                        pe.wait_ge(ends_ready, (it * R + b) * 2 + 2)
                    if not (first and n < B):
                        pe.wait_ge(scaled_ready, i * HEADS - (B - 1) * HEADS)
                    for k in range(4):
                        mm = nc.tensor.matmul(ps[0:P, j, 0:W], pick[:, q, k, :], g[:, b, j, k, :], start=(k == 0), stop=(k == 3))
                    mm.then_inc(agg_ready, 1)
                    if ahead and j == 0:
                        turn_maxima(*ahead)

            walk(pe, batch)

def stage_tokens(nc, K, A):
    with Scope(nc, "tokens") as s:
        bias = s.sb("bias_b", [P, 2, H])
        xin = s.sb("xin", [P, 3, 2, GT, H])
        y = s.sb("y_t", [P, 2, GT, H])
        x1 = s.sb("x1", [P, 3, GT, H])
        rden = s.sb("rden", [P, GT, HEADS])
        gw = s.sb("gw", [128, HC, EXPERTS])
        gb = s.sb("gb", [P, EXPERTS])
        tokt = s.sb("tokt", [128, HC, GN])
        stats = [s.sb(f"stats{k}", [P, GT, 6]) for k in range(2)]
        mv = [s.sb(f"mv{k}", [P, GT, 3]) for k in range(2)]
        var = [s.sb(f"var{k}", [P, GT]) for k in range(2)]
        std = [s.sb(f"std{k}", [P, GT]) for k in range(2)]
        rstd = [s.sb(f"rstd{k}", [P, GT]) for k in range(2)]
        shift = [s.sb(f"shift{k}", [P, GT]) for k in range(2)]
        logit = s.sb("logit", [P, TILES, EXPERTS])
        e = s.sb("e", [P, CHUNK, EXPERTS])
        one_hot = s.sb("one_hot", [P, CHUNK, EXPERTS])
        pos = s.sb("pos", [P, CHUNK, EXPERTS])
        tot = s.sb("tot", [P, CHUNK, EXPERTS])
        run = s.sb("run", [P, CHUNK + 1, EXPERTS])
        top = s.sb("top", [P, CHUNK])
        tsum = s.sb("tsum", [P, CHUNK])
        inv = s.sb("inv", [P, CHUNK])
        best = s.sb("best", [P, CHUNK])
        slot = s.sb("slot", [P, CHUNK])
        kept = s.sb("kept", [P, CHUNK])
        rank = s.sb("rank", [P, EXPERTS])
        begin = s.sb("begin", [P, EXPERTS])
        ones = s.sb("ones", [P, P])
        ones_t = s.sb("ones_t", [P, CHUNK])
        upto = s.sb("upto", [P, P])
        ps = s.ps("ps_tok", [128, 4, 512])
        made, arg_ready, e_ready, hot_ready, counted, slot_ready, tok_out = (s.sem(n) for n in (
            "made", "arg_ready", "e_ready", "hot_ready", "counted", "slot_ready", "tok_out"))
        w_in = s.sem("w_in")
        x_in = s.sems("x_in", 3)
        var_ready, std_ready = s.sems("var_ready", 2), s.sems("std_ready", 2)
        coef_ready, y_normed = s.sems("coef_ready", 2), s.sem("y_normed")
        y_ready, x1_ready, tok_ready = s.sem("y_ready"), s.sem("x1_ready"), s.sem("tok_ready")
        x1_out = s.sems("x1_out", 3)
        tok_psum, tokt_ready, log_psum, log_ready = (s.sem(n) for n in ("tok_psum", "tokt_ready", "log_psum", "log_ready"))
        dve_done = s.sem("dve_done")
        block = s.block()
        grp = lambda a: a.rearrange("(g t p) f -> g p t f", p=P, t=GT)
        row = lambda a, n: a.rearrange("(a n) -> a n", a=1).to_broadcast([P, n])
        bcast = lambda a: a.rearrange("p (t f) -> p t f", t=1).to_broadcast([P, GT, H])

        @block.sync
        def _(sp):
            for k, a in enumerate((A.bias, A.gamma)):
                sp.dma_start(bias[:, k, :], row(a, H)).then_inc(w_in, 16)
            sp.dma_start(gb[:, :], row(A.ffn_gate_b, EXPERTS)).then_inc(w_in, 16)
            sp.dma_start(gw[:], A.ffn_gate_w.rearrange("(c p) e -> p c e", p=128)).then_inc(w_in, 16)

            def load(g):
                for k, a in enumerate((K.xn_d, K.mix_d)):
                    rows_split(sp, xin[:, g % 3, k], grp(a)[g], x_in[g % 3])

            for g in range(3):
                load(g)
            for g in range(GROUPS):
                sp.wait_ge(x1_ready, g + 1)
                rows_split(sp, grp(K.x1_d)[g], x1[:, g % 3], x1_out[g % 3])
                if g + 3 < GROUPS:
                    load(g + 3)
            for b in range(3):
                sp.wait_ge(x1_out[b], 32 * ((GROUPS + 2 - b) // 3))

        per = lambda a: a.rearrange("p (t e) -> p t e", e=1).to_broadcast([P, CHUNK, EXPERTS])
        along = lambda a: a.rearrange("p (t e) -> p t e", t=1).to_broadcast([P, CHUNK, EXPERTS])
        CG = CHUNK // GT

        @block.gpsimd
        def _(pool):
            nc.gpsimd.iota(rank[:], pattern=[[-1, EXPERTS]], base=EXPERTS, channel_multiplier=0,
                           allow_small_or_imprecise_dtypes=True).then_inc(made, 1)
            nc.gpsimd.iota(begin[:], pattern=[[CAP, EXPERTS]], base=-1, channel_multiplier=0,
                           allow_small_or_imprecise_dtypes=True).then_inc(made, 1)
            nc.gpsimd.memset(ones[:], 1.0).then_inc(made, 1)
            pool.wait_ge(made, 3)
            nc.gpsimd.affine_select(out=upto[:], in_=ones[:], compare_op=ALU.is_ge, fill=0.0, base=0,
                                    pattern=[[1, P]], channel_multiplier=-1).then_inc(made, 1)

            def scatter(g):
                pool.wait_ge(slot_ready, g // CG + 1)
                for t in range(g * GT, (g + 1) * GT):
                    nc.gpsimd.indirect_dma_start(
                        out=K.buf_d, out_offset=bass.IndirectOffsetOnAxis(ap=K.slot_i[:, t:t + 1], axis=0),
                        in_=K.acc[:, t, 0:TOKW], in_offset=None, bounds_check=SLOTS - 1, oob_is_err=False).then_inc(tok_out, 16)

            behind = CG + 3
            for g in range(GROUPS):
                pool.wait_ge(x_in[g % 3], 64 * (g // 3 + 1))
                pool.wait_ge(y_ready, g + 1)
                if g >= 3:
                    pool.wait_ge(x1_out[g % 3], 32 * (g // 3))
                    pool.wait_ge(tok_ready, GT * (g - 2))
                nc.gpsimd.tensor_tensor(x1[:, g % 3], y[:, g % 2], xin[:, g % 3, 1], ALU.add).then_inc(x1_ready, 1)
                if g >= behind:
                    scatter(g - behind)
            for g in range(GROUPS - behind, GROUPS):
                scatter(g)
            pool.wait_ge(tok_out, 16 * TILES)

        @block.vector
        def _(dve):
            c = Chain(dve, dve_done)
            dve.wait_ge(w_in, 64)

            def sums(g):
                acc, yg = K.acc[:, g * GT:(g + 1) * GT, :], y[:, g % 2]
                c.did(nc.vector.reciprocal(rden[:], acc[:, :, OUT:ROW:OUT + 1]))
                c.settle()
                if g >= 2:
                    dve.wait_ge(x1_ready, g - 1)
                c.did(nc.vector.tensor_tensor(yg.rearrange("p t (h o) -> p t h o", h=HEADS),
                                              acc.rearrange("p t (h o) -> p t h o", h=HEADS)[:, :, :, 0:OUT],
                                              rden[:].rearrange("p t (h o) -> p t h o", o=1).to_broadcast([P, GT, HEADS, OUT]),
                                              ALU.mult))
                c.settle()
                c.did(nc.vector.tensor_tensor(yg, yg, bcast(bias[:, 0, :]), ALU.add))
                c.settle()
                dve.wait_ge(x_in[g % 3], 64 * (g // 3 + 1))
                c.did(nc.vector.scalar_tensor_tensor(yg, yg, 0.0, xin[:, g % 3, 0], ALU.max, ALU.add))
                c.settle()

            def deviate(g):
                norm_stats(nc, c, y[:, g % 2], stats[0], mv[0], var[0]).then_inc(var_ready[0], 1)

            def coefs(k, g):
                dve.wait_ge(std_ready[k], g + 1)
                if k and g:
                    dve.wait_ge(tok_ready, GT * g)
                c.did(nc.vector.reciprocal(rstd[k][:], std[k][:]))
                c.settle()
                nc.vector.scalar_tensor_tensor(shift[k][:], mv[k][:, :, 0], -1.0, rstd[k][:], ALU.mult,
                                               ALU.mult).then_inc(coef_ready[k], 1)

            def scale(g):
                dve.wait_ge(y_normed, GT * (g + 1))
                nc.vector.tensor_tensor(y[:, g % 2], y[:, g % 2], bcast(bias[:, 1, :]), ALU.mult).then_inc(y_ready, 1)

            def spread(g):
                dve.wait_ge(x1_ready, g + 1)
                if g:
                    dve.wait_ge(coef_ready[1], g)
                norm_stats(nc, c, x1[:, g % 3], stats[1], mv[1], var[1]).then_inc(var_ready[1], 1)

            def logits(g):
                dve.wait_ge(log_psum, g + 1)
                nc.vector.tensor_tensor(logit[:, g * GT:(g + 1) * GT, :],
                                        ps[0:P, 2, 0:GT * EXPERTS].rearrange("p (t e) -> p t e", e=EXPERTS),
                                        gb[:].rearrange("p (a e) -> p a e", a=1).to_broadcast([P, GT, EXPERTS]),
                                        ALU.add).then_inc(log_ready, 1)

            v = nc.vector

            def step(ins):
                c.did(ins)
                c.settle()

            def exponents(q):
                dve.wait_ge(log_ready, (q + 1) * CG)
                mine = logit[:, q * CHUNK:(q + 1) * CHUNK, :]
                step(v.tensor_reduce(top[:], mine, X, ALU.max))
                v.tensor_tensor(e[:], mine, per(top[:]), ALU.subtract).then_inc(arg_ready, 1)

            def choose(q):
                dve.wait_ge(e_ready, q + 1)
                c.did(v.tensor_reduce(tsum[:], e[:], X, ALU.add))
                step(v.tensor_reduce(best[:], e[:], X, ALU.max))
                c.did(v.reciprocal(inv[:], tsum[:]))
                step(v.tensor_tensor(one_hot[:], e[:], per(best[:]), ALU.is_equal))
                step(v.tensor_tensor(one_hot[:], one_hot[:], along(rank[:]), ALU.mult))
                step(v.tensor_reduce(top[:], one_hot[:], X, ALU.max))
                c.did(v.tensor_tensor(best[:], best[:], inv[:], ALU.mult))
                v.tensor_tensor(one_hot[:], one_hot[:], per(top[:]), ALU.is_equal).then_inc(hot_ready, 1)
                c.settle()
                c.did(v.tensor_copy(K.acc[:, q * CHUNK:(q + 1) * CHUNK, H:TOKW], best[:].rearrange("p (t e) -> p t e", e=1)))

            def place(q):
                dve.wait_ge(counted, q + 1)
                n = CHUNK * EXPERTS
                flat = lambda a: a.rearrange("p t e -> p (t e)")
                c.did(v.tensor_copy(flat(pos[:]), ps[0:P, 3, 0:n]))
                step(v.tensor_copy(flat(tot[:]), ps[0:P, 3, n:2 * n]))
                for x in range(EXPERTS):
                    c.did(v.tensor_tensor_scan(run[:, 1:, x], ones_t[:], tot[:, :, x], run[:, 0, x:x + 1], ALU.mult, ALU.add))
                c.settle()
                step(v.tensor_tensor(pos[:], pos[:], run[:, 0:CHUNK, :], ALU.add))
                step(v.tensor_copy(run[:, 0, :], run[:, CHUNK, :]))
                step(v.tensor_tensor(tot[:], pos[:], one_hot[:], ALU.mult))
                step(v.tensor_reduce(kept[:], tot[:], X, ALU.add))
                step(v.tensor_scalar(kept[:], kept[:], float(C_MAX), None, ALU.is_le))
                step(v.tensor_tensor(pos[:], pos[:], along(begin[:]), ALU.add))
                step(v.tensor_tensor(pos[:], pos[:], one_hot[:], ALU.mult))
                step(v.tensor_reduce(slot[:], pos[:], X, ALU.add))
                step(v.scalar_tensor_tensor(slot[:], slot[:], float(SLOTS), kept[:], ALU.subtract, ALU.mult))
                step(v.tensor_scalar(slot[:], slot[:], float(SLOTS), None, ALU.add))
                v.tensor_copy(K.slot_i[:, q * CHUNK:(q + 1) * CHUNK], slot[:]).then_inc(slot_ready, 1)

            dve.wait_ge(made, 4)
            c.did(v.memset(ones_t[:], 1.0))
            step(v.memset(run[:, 0, :], 0.0))
            for i in range(GROUPS + 2):
                if 1 <= i <= GROUPS:
                    coefs(0, i - 1)
                if i >= 2:
                    spread(i - 2)
                if i < GROUPS:
                    sums(i)
                if 1 <= i <= GROUPS:
                    scale(i - 1)
                if i < GROUPS:
                    deviate(i)
                if i >= 2:
                    coefs(1, i - 2)
                if i >= 3:
                    logits(i - 3)
                q, part = divmod(i - 3 - (CG - 1), CG)
                if 0 <= q < TURNS - 1 and part < 3:
                    (exponents, choose, place)[part](q)
            logits(GROUPS - 1)
            for part in (exponents, choose, place):
                part(TURNS - 1)

        @block.scalar
        def _(act):
            def root(k, g):
                act.wait_ge(var_ready[k], g + 1)
                nc.scalar.activation(std[k][:, :], var[k][:, :], ACT.Sqrt).then_inc(std_ready[k], 1)

            def normalise(k, g, x, out, done):
                act.wait_ge(coef_ready[k], g + 1)
                for t in range(GT):
                    nc.scalar.activation(out[:, t, :], x[:, t, :], ACT.Identity, scale=rstd[k][:, t:t + 1],
                                         bias=shift[k][:, t:t + 1]).then_inc(done, 1)

            def columns(g):
                act.wait_ge(tok_psum, g + 1)
                if g:
                    act.wait_ge(log_psum, g)
                nc.scalar.activation(tokt[:], ps[:, 0:2, 0:GN], ACT.Copy).then_inc(tokt_ready, 1)

            def exps(q):
                act.wait_ge(arg_ready, q + 1)
                nc.scalar.activation(e[:], e[:], ACT.Exp).then_inc(e_ready, 1)

            for i in range(GROUPS + 2):
                q, part = divmod(i - 4 - (CG - 1), CG)
                if 0 <= q < TURNS - 1 and part == 0:
                    exps(q)
                if 1 <= i <= GROUPS:
                    normalise(0, i - 1, y[:, (i - 1) % 2], y[:, (i - 1) % 2], y_normed)
                if i >= 2:
                    root(1, i - 2)
                if i >= 3:
                    columns(i - 3)
                if i < GROUPS:
                    root(0, i)
                if i >= 2:
                    g = i - 2
                    normalise(1, g, x1[:, g % 3], K.acc[:, g * GT:(g + 1) * GT, 0:H], tok_ready)
            columns(GROUPS - 1)
            exps(TURNS - 1)

        @block.tensor
        def _(pe):
            def count(q):
                n = CHUNK * EXPERTS
                pe.wait_ge(hot_ready, q + 1)
                if q:
                    pe.wait_ge(slot_ready, q)
                flat = one_hot[:].rearrange("p t e -> p (t e)")
                nc.tensor.matmul(ps[0:P, 3, 0:n], upto[:], flat, start=True, stop=True)
                nc.tensor.matmul(ps[0:P, 3, n:2 * n], ones[:], flat, start=True, stop=True).then_inc(counted, 1)

            pe.wait_ge(w_in, 64)
            for g in range(GROUPS):
                pe.wait_ge(tok_ready, GT * (g + 1))
                if g:
                    pe.wait_ge(tokt_ready, g)
                for t in range(GT):
                    for k in range(HC):
                        mm = nc.tensor.transpose(ps[:, k, t * P:(t + 1) * P], K.acc[:, g * GT + t, k * 128:(k + 1) * 128],
                                                 K.ident[0:P, 0:P])
                mm.then_inc(tok_psum, 1)
                pe.wait_ge(tokt_ready, g + 1)
                if g:
                    pe.wait_ge(log_ready, g)
                for t in range(GT):
                    for k in range(HC):
                        mm = nc.tensor.matmul(ps[0:P, 2, t * EXPERTS:(t + 1) * EXPERTS], tokt[:, k, t * P:(t + 1) * P],
                                              gw[:, k, :], start=(k == 0), stop=(k == HC - 1))
                mm.then_inc(log_psum, 1)
                q, part = divmod(g - CG, CG)
                if 0 <= q < TURNS - 1 and part == 0:
                    count(q)
            count(TURNS - 1)


def stage_experts(nc, K, A):
    FC = F // 128
    per = 2 * CHUNKS
    n_turns = EXPERTS // 2
    with Scope(nc, "experts") as s:
        w1 = s.sb("w1", [128, 2, HC, F])
        w2 = s.sb("w2", [128, 2, FC, H])
        b1 = s.sb("b1", [128, 2, FC])
        b2 = s.sb("b2", [128, 2, H])
        rows = s.sb("rows_e", [128, per, 4, TOKW])
        bt = s.sb("bt", [128, 2, HC, 512])
        hm = s.sb("hm", [128, FC, 512])
        y = s.sb("y_e", [128, 2, 4, H])
        bad = s.sb("bad", [128, 4, H], I32)
        const = s.sb("const", [128, 3, 4, H])
        scrap = s.sb("scrap", [128, 2])
        ps = s.ps("ps_e", [128, 8, 512])
        w_in = s.sems("w_in4", 2)
        const_ready = s.sem("const_ready")
        rows_in = s.sems("rows_in4", per)
        bt_psum, bt_ready, h_psum, h_ready, y_psum, y_made, y_ready = (s.sem(n) for n in (
            "bt_psum", "bt_ready", "h_psum", "hm_ready", "y_psum", "y_made", "y_ready"))
        y_out = s.sems("y_out", 2)
        done = s.sem("dve_done6")
        block = s.block()
        bufc = K.buf_d.rearrange("(n t p) r -> n p t r", t=4, p=128)
        yc = K.y_d[0:SLOTS, :].rearrange("(n t p) r -> n p t r", t=4, p=128)

        @block.sync
        def _(sp):
            def weights(x, i):
                w1v = A.ffn_w1.rearrange("e (c p) f -> e p c f", p=128)
                w2v = A.ffn_w2.rearrange("e (c p) f -> e p c f", p=128)
                sp.dma_start(w1[:, i], one(w1v, x)).then_inc(w_in[i], 16)
                sp.dma_start(w2[:, i], one(w2v, x)).then_inc(w_in[i], 16)
                sp.dma_start(b2[:, i, :], A.ffn_b2[bass.ds(x, 1), :].to_broadcast([128, H])).then_inc(w_in[i], 16)
                with nc.allow_non_contiguous_dma(reason="b1 to columns"):
                    sp.dma_start(b1[:, i, :], one(A.ffn_b1.rearrange("e (f p) -> e p f", p=128), x)).then_inc(w_in[i], 16)

            weights(0, 0)
            for u in range(per):
                sp.dma_start(rows[:, u], bufc[u]).then_inc(rows_in[u], 16)
                if u == 0:
                    weights(1, 1)

            def body(it, more):
                for u in range(per):
                    j = it * per + u
                    sp.wait_ge(y_ready, j + 1)
                    sp.dma_start(one(yc, j), y[:, u % 2]).then_inc(y_out[u % 2], 16)
                    if more:
                        sp.dma_start(rows[:, u], one(bufc, j + per)).then_inc(rows_in[u], 16)
                        if u % CHUNKS == CHUNKS - 1:
                            weights(it * 2 + u // CHUNKS + 2, u // CHUNKS)

            with sp.Fori(0, n_turns - 1) as it:
                body(it, True)
            body(n_turns - 1, False)
            for b in range(2):
                sp.wait_ge(y_out[b], 16 * n_turns * CHUNKS)

        @block.tensor
        def _(pe):
            def turn_rows(it, u, first):
                pe.wait_ge(rows_in[u], it * 16 + 16)
                if not (first and u == 0):
                    pe.wait_ge(bt_ready, it * per + u)
                for t in range(4):
                    for k in range(HC):
                        mm = nc.tensor.transpose(ps[:, k, t * 128:(t + 1) * 128], rows[:, u, t, k * 128:(k + 1) * 128], K.ident[:])
                mm.then_inc(bt_psum, 1)

            def body(it, first):
                turn_rows(it, 0, first)
                for u in range(per):
                    j = it * per + u
                    x = u // CHUNKS
                    if u % CHUNKS == 0:
                        pe.wait_ge(w_in[x], it * 64 + 64)
                    pe.wait_ge(bt_ready, j + 1)
                    for f in range(FC):
                        i = j * FC + f
                        if not (first and i < 4):
                            pe.wait_ge(h_ready, i - 3)
                        for k in range(HC):
                            mm = nc.tensor.matmul(ps[:, 2 + f % 4, :], w1[:, x, k, f * 128:(f + 1) * 128], bt[:, u % 2, k, :],
                                                  start=(k == 0), stop=(k == HC - 1))
                        mm.then_inc(h_psum, 1)
                    if u < per - 1:
                        turn_rows(it, u + 1, first)
                    pe.wait_ge(h_ready, j * FC + FC)
                    if not (first and u == 0):
                        pe.wait_ge(y_made, j)
                    for t in range(4):
                        for f in range(FC):
                            mm = nc.tensor.matmul(ps[:, 6 + t // 2, (t % 2) * H:(t % 2 + 1) * H], hm[:, f, t * 128:(t + 1) * 128],
                                                  w2[:, x, f, :], start=(f == 0), stop=(f == FC - 1))
                    mm.then_inc(y_psum, 1)

            turns(pe, n_turns, body)

        @block.scalar
        def _(act):
            def body(it, first):
                for u in range(per):
                    j = it * per + u
                    for f in range(FC):
                        i = j * FC + f
                        act.wait_ge(h_psum, i + 1)
                        if f == 0 and not (first and u == 0):
                            act.wait_ge(y_psum, j)
                        if f == 0 and u % CHUNKS == 0:
                            act.wait_ge(w_in[u // CHUNKS], it * 64 + 64)
                        nc.scalar.activation(hm[:, f, :], ps[:, 2 + f % 4, :], ACT.Relu,
                                             bias=b1[:, u // CHUNKS, f:f + 1]).then_inc(h_ready, 1)

            turns(act, n_turns, body)

        @block.vector
        def _(dve):
            for k, x in enumerate((0.0, 1e4, -1e4)):
                nc.vector.memset(const[:, k], x).then_inc(const_ready, 1)
            nc.vector.memset(scrap[:], 0.0).then_inc(const_ready, 1)
            dve.wait_ge(const_ready, 4)

            def turn_copy(it, u, first):
                j = it * per + u
                dve.wait_ge(bt_psum, j + 1)
                nc.vector.tensor_copy(bt[:, u % 2], ps[:, 0:2, :]).then_inc(bt_ready, 1)

            def body(it, first):
                c = Chain(dve, done, per * 12, it)

                def carry_wait():
                    c.settle()
                    c.did(nc.vector.tensor_copy(scrap[:, 0:1], scrap[:, 1:2]))

                turn_copy(it, 0, first)
                for u in range(per):
                    j = it * per + u
                    if u < per - 1:
                        turn_copy(it, u + 1, first)
                    dve.wait_ge(y_psum, j + 1)
                    if u % CHUNKS == 0:
                        dve.wait_ge(w_in[u // CHUNKS], it * 64 + 64)
                    if not (first and u < 2):
                        dve.wait_ge(y_out[u % 2], it * (16 * CHUNKS) + u // 2 * 16)
                    yu = y[:, u % 2]
                    nc.vector.tensor_tensor(yu.rearrange("p (a b) f -> p a b f", a=2),
                                            ps[:, 6:8, :].rearrange("p a (b f) -> p a b f", b=2),
                                            b2[:, u // CHUNKS, :].rearrange("p (a b f) -> p a b f", a=1, b=1).to_broadcast([128, 2, 2, H]),
                                            ALU.add).then_inc(y_made, 1)
                    dve.wait_ge(y_made, j + 1)
                    for t in range(4):
                        c.did(nc.vector.tensor_scalar(yu[:, t, :], yu[:, t, :], rows[:, u, t, H:TOKW], None, ALU.mult))
                    c.settle()
                    c.did(nc.vector.tensor_tensor(bad[:], yu, yu, ALU.not_equal))
                    carry_wait()
                    c.did(nc.vector.copy_predicated(yu, bad[:], const[:, 0]))
                    c.settle()
                    c.did(nc.vector.tensor_scalar(bad[:], yu, FLT_MAX, None, ALU.is_gt))
                    carry_wait()
                    c.did(nc.vector.copy_predicated(yu, bad[:], const[:, 1]))
                    c.settle()
                    c.did(nc.vector.tensor_scalar(bad[:], yu, -FLT_MAX, None, ALU.is_lt))
                    carry_wait()
                    nc.vector.copy_predicated(yu, bad[:], const[:, 2]).then_inc(y_ready, 1)
                c.close()

            turns(dve, n_turns, body)


def stage_output(nc, K, A):
    U = UNROLL
    with Scope(nc, "output") as s:
        x1 = s.sb("x1_o", [P, U, GT, H])
        y = s.sb("y_o", [P, U, GT, H])
        x_in = s.sems("x_in5", U)
        y_in = s.sems("y_in5", U)
        o_ready = s.sem("o_ready")
        o_out = s.sems("o_out", U)
        block = s.block()
        grp = lambda a: a.rearrange("(g t p) f -> g p t f", p=P, t=GT)

        @block.sync
        def _(sp):
            for g in range(U):
                rows_split(sp, x1[:, g], grp(K.x1_d)[g], x_in[g])
            for g in range(GROUPS):
                sp.wait_ge(o_ready, g + 1)
                rows_split(sp, grp(A.out)[g], x1[:, g % U], o_out[g % U])
                if g + U < GROUPS:
                    sp.wait_ge(o_out[g % U], 32 * (g // U + 1))
                    rows_split(sp, x1[:, g % U], grp(K.x1_d)[g + U], x_in[g % U])
            for u in range(U):
                sp.wait_ge(o_out[u], 32 * TURNS)

        @block.gpsimd
        def _(pool):
            for g in range(GROUPS):
                if g >= U:
                    pool.wait_ge(o_ready, g - U + 1)
                for t in range(GT):
                    i = g * GT + t
                    nc.gpsimd.indirect_dma_start(
                        out=y[:, g % U, t, :], out_offset=None, in_=K.y_d,
                        in_offset=bass.IndirectOffsetOnAxis(ap=K.slot_i[:, i:i + 1], axis=0)).then_inc(y_in[g % U], 16)

        @block.vector
        def _(dve):
            for g in range(GROUPS):
                dve.wait_ge(x_in[g % U], 32 * (g // U + 1))
                dve.wait_ge(y_in[g % U], 64 * (g // U + 1))
                nc.vector.tensor_tensor(x1[:, g % U], x1[:, g % U], y[:, g % U], ALU.add).then_inc(o_ready, 1)


class Shared:
    pass


class Arguments:

    def __init__(self, aps, out):
        self.x = aps["x"]
        self.src = aps["src"]
        self.dst = aps["dst"]
        self.W = aps["L0_gnn_W"]
        self.att_src = aps["L0_gnn_att_src"]
        self.att_dst = aps["L0_gnn_att_dst"]
        self.bias = aps["L0_gnn_bias"]
        self.gamma = aps["L0_gnn_gamma"]
        self.beta = aps["L0_gnn_beta"]
        self.mix_Wqkv = aps["L0_mix_Wqkv"]
        self.mix_Wproj = aps["L0_mix_Wproj"]
        self.mix_bproj = aps["L0_mix_bproj"]
        self.mix_ln_g = aps["L0_mix_ln_g"]
        self.mix_ln_b = aps["L0_mix_ln_b"]
        self.mix_Wg1 = aps["L0_mix_Wg1"]
        self.mix_bg1 = aps["L0_mix_bg1"]
        self.mix_Wg2 = aps["L0_mix_Wg2"]
        self.mix_bg2 = aps["L0_mix_bg2"]
        self.ffn_gate_w = aps["L0_ffn_gate_w"]
        self.ffn_gate_b = aps["L0_ffn_gate_b"]
        self.ffn_w1 = aps["L0_ffn_w1"]
        self.ffn_b1 = aps["L0_ffn_b1"]
        self.ffn_w2 = aps["L0_ffn_w2"]
        self.ffn_b2 = aps["L0_ffn_b2"]
        self.out = out


def gps_layer(nc, A, kind="Internal"):
    K = Shared()
    made = {}

    def dram(name, shape, dt=F32):
        made[name] = nc.dram_tensor(name, shape, dt, kind=kind).ap()
        return made[name]

    K.xn_d = dram("xn_d", [N, H])
    K.xt_d = dram("xt_d", [GROUPS, 128, HC * GN])
    K.h_d = dram("h_d", [N, ROW])
    K.dst_d = dram("dst_d", [DST_ROWS * FAN], I32)
    K.src_d = dram("src_d", [EP], I32)
    K.top_d = dram("top_d", [PIVOTS, FAN], I32)
    K.piv_d = dram("piv_d", [PIVOTS], I32)
    K.rp_d = dram("rp_d", [N + 1])
    K.gt_d = dram("gt_d", [GROUPS, 128, HC * GN])
    K.mix_d = dram("mix_d", [N, H])
    K.rec_d = dram("rec_d", [EP, HEADS])
    K.pen_d = dram("pen_d", [2, EP])
    K.meta_d = dram("meta_d", [EP, META])
    K.x1_d = dram("x1_d", [N, H])
    K.buf_d = dram("buf_d", [SLOTS, TOKW])
    K.y_d = dram("y_d", [SLOTS + 1, H])
    with Scope(nc, "gps_layer") as s:
        K.ident = s.sb("ident", [128, 128])
        K.iota_col = s.sb("iota_col", [128, 128])
        K.gate = s.sem("gate")
        K.node_id = s.sb("node_id", [P, TILES])
        K.asd = s.sb("asd", [P, TILES, 2 * HEADS])
        K.step_node = s.sb("step_node", [128, STEPS])
        K.step_tile = s.sb("step_tile", [1, STEPS], I32)
        K.step_group = s.sb("step_group", [1, STEPS], I32)
        constants(nc, K)
        stage_embed(nc, K, A)
        stage_mix(nc, K, A)
        stage_steps(nc, K)
        stage_edges(nc, K)
        K.slot_i = s.sb("slot_i", [P, TILES], I32)
        with Scope(nc, "gps_layer") as t:
            K.acc = t.sb("acc", [P, TILES, ROW])
            K.run_max = t.sb("run_max", [P, TILES, HEADS])
            stage_aggregate(nc, K)
            stage_tokens(nc, K, A)
        stage_experts(nc, K, A)
        stage_output(nc, K, A)


_INS = ["x", "src", "dst", "L0_gnn_W", "L0_gnn_att_src", "L0_gnn_att_dst", "L0_gnn_bias", "L0_gnn_gamma",
        "L0_gnn_beta", "L0_mix_Wqkv", "L0_mix_Wproj", "L0_mix_bproj", "L0_mix_ln_g", "L0_mix_ln_b",
        "L0_mix_Wg1", "L0_mix_bg1", "L0_mix_Wg2", "L0_mix_bg2", "L0_ffn_gate_w", "L0_ffn_gate_b",
        "L0_ffn_w1", "L0_ffn_b1", "L0_ffn_w2", "L0_ffn_b2"]


def kernel(**inputs):
    import concourse.bacc as bacc
    from concourse.bass_utils import run_bass_kernel_spmd

    nc = bacc.Bacc("TRN2", target_bir_lowering=False, num_devices=1)
    arrays, aps = {}, {}
    for name in _INS:
        a = np.ascontiguousarray(inputs[name])
        arrays[f"in_{name}"] = a
        aps[name] = nc.dram_tensor(f"in_{name}", a.shape, mybir.dt.from_np(a.dtype), kind="ExternalInput").ap()
    out = nc.dram_tensor("out", [N, H], F32, kind="ExternalOutput").ap()
    A = Arguments(aps, out)
    gps_layer(nc, A)
    r = run_bass_kernel_spmd(nc, [arrays], core_ids=[0])
    return r.results[0]["out"]
```
